# Optimizing a Trainium2 kernel written in Bass

```python
import numpy as np
import jax
import jax.numpy as jnp

def _softmax(x, axis=-1):
    return jax.nn.softmax(x, axis=axis)

def _gelu(x):
    return jax.nn.gelu(x, approximate=True)

def _silu(x):
    return jax.nn.silu(x)

def _sigmoid(x):
    return jax.nn.sigmoid(x)

def _layernorm(x, axis=-1, eps=1e-05):
    m = jnp.mean(x, axis=axis, keepdims=True)
    v = jnp.var(x, axis=axis, keepdims=True)
    return (x - m) / jnp.sqrt(v + eps)

def _scatter_add(tgt, idx, src, axis=0):
    return tgt.at[idx].add(src)

def _segment_sum(src, seg, n):
    return jax.ops.segment_sum(src, seg, n)
kernel_name = 'mk_flamingo_gated_d1_seqx_r4_070a16'

def setup_inputs(seed: int=0):
    np.random.seed(seed)
    _w = jnp.asarray

    def _rec_inputs():
        import jax
        import jax.numpy as jnp
        _rk = jax.random.key(seed)
        x = -0.0002928 + 1 * jax.random.normal(jax.random.fold_in(_rk, 1), (16, 112, 256), jnp.float32)
        _lenS = 112 - jax.random.randint(jax.random.fold_in(_rk, 7), (16,), 0, max(1, 112 // 4) + 1, jnp.int32)
        _lenS2 = 375 - jax.random.randint(jax.random.fold_in(_rk, 8), (16,), 0, max(1, 375 // 4) + 1, jnp.int32)
        _ctx_1024P = jax.random.normal(jax.random.fold_in(_rk, 11), (16, 16, 256), jnp.float32)
        _ctx_1024c = jax.random.dirichlet(jax.random.fold_in(_rk, 511), 0.3 * jnp.ones((16,), jnp.float32), (16, 375))
        _ctx_1024t = jnp.einsum('bsk,bkd->bsd', _ctx_1024c, _ctx_1024P)
        _ctx_1024t = _ctx_1024t * jax.lax.rsqrt(jnp.mean(jnp.square(_ctx_1024t)) + 1e-12) * 0.953939
        ctx_1024 = -1.39393e-06 + 0.999914 * (_ctx_1024t + 0.3 * jax.random.normal(jax.random.fold_in(_rk, 611), (16, 375, 256), jnp.float32))
        _validS = jnp.arange(112)[None, :] < _lenS[:, None]
        _validS2 = jnp.arange(375)[None, :] < _lenS2[:, None]
        _causal = jnp.tril(jnp.ones((112, 112), dtype=bool))
        mask_BxS2_if0 = jnp.where(jnp.ones((16, 375), dtype=bool), 0, 1).astype(jnp.int32)
        _g = jax.random.normal(jax.random.fold_in(_rk, 9001), (2, 1), jnp.float32)
        _g = jnp.sign(_g) * jnp.maximum(jnp.abs(_g), 1.0) + (_g == 0) * 1.0
        g_xattn = _g[0]
        g_ffn = _g[1]
        return (x, ctx_1024, mask_BxS2_if0, g_xattn, g_ffn)
    x, ctx_1024, mask_BxS2_if0, g_xattn, g_ffn = _rec_inputs()

    def _L0_xattn_setup():
        import jax, jax.numpy as jnp
        import numpy as np
        DIM = 256
        HEADS = 16
        HEAD_DIM = DIM // HEADS
        B, NQ, NK = (2, 512, 512)
        key = jax.random.key(seed)
        ks = jax.random.split(key, 8)
        s = 1.0 / np.sqrt(DIM)
        return {'query': jax.random.normal(ks[0], (B, NQ, DIM), jnp.float32), 'key': jax.random.normal(ks[1], (B, NK, DIM), jnp.float32), 'value': jax.random.normal(ks[2], (B, NK, DIM), jnp.float32), 'qpos': jnp.zeros((B, NQ), jnp.int32), 'kpos': jnp.zeros((B, NK), jnp.int32), 'Wq': jax.random.normal(ks[3], (DIM, DIM), jnp.float32) * s, 'Wk': jax.random.normal(ks[4], (DIM, DIM), jnp.float32) * s, 'Wv': jax.random.normal(ks[5], (DIM, DIM), jnp.float32) * s, 'Wo': jax.random.normal(ks[6], (DIM, DIM), jnp.float32) * s, 'bo': jax.random.normal(ks[7], (DIM,), jnp.float32) * s}
    _L0_xattn_all = _L0_xattn_setup()
    _L0_xattn_in = {k: v for k, v in _L0_xattn_all.items() if k in ('Wq', 'Wk', 'Wv', 'Wo', 'bo')}
    del _L0_xattn_all

    def _L0_ffn_setup():
        import jax, jax.numpy as jnp
        import numpy as np
        H = 256
        I = 512
        E = 8
        B, S = (2, 1024)
        EPS = 1e-05
        INIT = 0.02

        def _layernorm(x, w, b):
            mu = jnp.mean(x, axis=-1, keepdims=True)
            var = jnp.mean(jnp.square(x - mu), axis=-1, keepdims=True)
            return (x - mu) * jax.lax.rsqrt(var + EPS) * w + b
        key = jax.random.key(seed)
        ks = jax.random.split(key, 9)
        return {'hidden_states': jax.random.normal(ks[0], (B, S, H), jnp.float32), 'ln_w': jnp.ones((H,), jnp.float32), 'ln_b': jnp.zeros((H,), jnp.float32), 'router_w': jax.random.normal(ks[1], (H, E), jnp.float32) * INIT, 'gate_w': jax.random.normal(ks[2], (E, H, I), jnp.float32) * INIT, 'up_w': jax.random.normal(ks[3], (E, H, I), jnp.float32) * INIT, 'down_w': jax.random.normal(ks[4], (E, I, H), jnp.float32) * INIT, 'sh_gate': jax.random.normal(ks[5], (H, I), jnp.float32) * INIT, 'sh_up': jax.random.normal(ks[6], (H, I), jnp.float32) * INIT, 'sh_down': jax.random.normal(ks[7], (I, H), jnp.float32) * INIT}
    _L0_ffn_all = _L0_ffn_setup()
    _L0_ffn_in = {k: v for k, v in _L0_ffn_all.items() if k in ('ln_w', 'ln_b', 'router_w', 'gate_w', 'up_w', 'down_w', 'sh_gate', 'sh_up', 'sh_down')}
    del _L0_ffn_all
    return {'x': x, 'ctx_1024': ctx_1024, 'mask_BxS2_if0': mask_BxS2_if0, 'g_xattn': g_xattn, 'g_ffn': g_ffn, 'L0_xattn_Wq': _L0_xattn_in['Wq'], 'L0_xattn_Wk': _L0_xattn_in['Wk'], 'L0_xattn_Wv': _L0_xattn_in['Wv'], 'L0_xattn_Wo': _L0_xattn_in['Wo'], 'L0_xattn_bo': _L0_xattn_in['bo'], 'L0_ffn_ln_w': _L0_ffn_in['ln_w'], 'L0_ffn_ln_b': _L0_ffn_in['ln_b'], 'L0_ffn_router_w': _L0_ffn_in['router_w'], 'L0_ffn_gate_w': _L0_ffn_in['gate_w'], 'L0_ffn_up_w': _L0_ffn_in['up_w'], 'L0_ffn_down_w': _L0_ffn_in['down_w'], 'L0_ffn_sh_gate': _L0_ffn_in['sh_gate'], 'L0_ffn_sh_up': _L0_ffn_in['sh_up'], 'L0_ffn_sh_down': _L0_ffn_in['sh_down']}

def reference(x, ctx_1024, mask_BxS2_if0, g_xattn, g_ffn, L0_xattn_Wq, L0_xattn_Wk, L0_xattn_Wv, L0_xattn_Wo, L0_xattn_bo, L0_ffn_ln_w, L0_ffn_ln_b, L0_ffn_router_w, L0_ffn_gate_w, L0_ffn_up_w, L0_ffn_down_w, L0_ffn_sh_gate, L0_ffn_sh_up, L0_ffn_sh_down):
    import jax
    import jax.numpy as jnp

    def _L0_xattn_ref(query, key, value, qpos, kpos, Wq, Wk, Wv, Wo, bo):
        import jax, jax.numpy as jnp
        import numpy as np
        DIM = 256
        HEADS = 16
        HEAD_DIM = DIM // HEADS
        B, NQ, NK = (2, 512, 512)
        Bq, Nq, C = query.shape
        Nk = key.shape[1]
        scale = HEAD_DIM ** (-0.5)
        q = (query @ Wq.T).reshape(Bq, Nq, HEADS, HEAD_DIM).transpose(0, 2, 1, 3)
        k = (key @ Wk.T).reshape(Bq, Nk, HEADS, HEAD_DIM).transpose(0, 2, 1, 3)
        v = (value @ Wv.T).reshape(Bq, Nk, HEADS, HEAD_DIM).transpose(0, 2, 1, 3)
        attn = jnp.einsum('bhqd,bhkd->bhqk', q, k) * scale
        attn = jax.nn.softmax(attn, axis=-1)
        x = jnp.einsum('bhqk,bhkd->bhqd', attn, v)
        x = x.transpose(0, 2, 1, 3).reshape(Bq, Nq, C)
        return x @ Wo.T + bo

    def _L0_ffn_ref(hidden_states, ln_w, ln_b, router_w, gate_w, up_w, down_w, sh_gate, sh_up, sh_down):
        import jax, jax.numpy as jnp
        import numpy as np
        H = 256
        I = 512
        E = 8
        B, S = (2, 1024)
        EPS = 1e-05
        INIT = 0.02

        def _layernorm(x, w, b):
            mu = jnp.mean(x, axis=-1, keepdims=True)
            var = jnp.mean(jnp.square(x - mu), axis=-1, keepdims=True)
            return (x - mu) * jax.lax.rsqrt(var + EPS) * w + b
        b, s, h = hidden_states.shape
        normed = _layernorm(hidden_states, ln_w, ln_b)
        xf = normed.reshape(-1, h)
        logits = xf @ router_w
        top_idx = jnp.argmax(logits, axis=-1)
        top_score = jax.nn.sigmoid(jnp.max(logits, axis=-1))

        def body(acc, ew):
            g, u, d, e = ew
            w = jnp.where(top_idx == e, top_score, 0.0)[:, None]
            xe = xf * w
            hmid = jax.nn.silu(xe @ g) * (xe @ u)
            return (acc + hmid @ d, None)
        routed, _ = jax.lax.scan(body, jnp.zeros_like(xf), (gate_w, up_w, down_w, jnp.arange(E)))
        shared = jax.nn.silu(xf @ sh_gate) * (xf @ sh_up) @ sh_down
        moe_out = (routed + shared).reshape(b, s, h)
        return hidden_states + moe_out
    x = x + jnp.tanh(g_xattn[0]) * _L0_xattn_ref(_layernorm(x, axis=-1), ctx_1024, ctx_1024, mask_BxS2_if0, mask_BxS2_if0, L0_xattn_Wq, L0_xattn_Wk, L0_xattn_Wv, L0_xattn_Wo, L0_xattn_bo)
    x = x + jnp.tanh(g_ffn[0]) * _L0_ffn_ref(_layernorm(x, axis=-1), L0_ffn_ln_w, L0_ffn_ln_b, L0_ffn_router_w, L0_ffn_gate_w, L0_ffn_up_w, L0_ffn_down_w, L0_ffn_sh_gate, L0_ffn_sh_up, L0_ffn_sh_down)
    return x

_drawn_inputs = setup_inputs


def setup_inputs(seed=0):
    import zlib

    import numpy as np

    out = dict(_drawn_inputs(seed))
    spreads = {'L0_ffn_ln_w': (1.0, 0.2), 'L0_ffn_ln_b': (0.0, 0.276)}
    factors = {}
    for name, (base, spread) in spreads.items():
        noise = np.random.default_rng([zlib.crc32(name.encode()), seed]).standard_normal(out[name].shape)
        drawn = base * np.exp(spread * noise) if base else spread * noise
        out[name] = jnp.asarray(drawn.astype(out[name].dtype))
    for name, factor in factors.items():
        out[name] = (out[name] * factor).astype(out[name].dtype)
    return out
```

```python
from contextlib import ExitStack

import concourse.bass as bass
from concourse import mybir

F32 = mybir.dt.float32
BF16 = mybir.dt.bfloat16
I32 = mybir.dt.int32
U32 = mybir.dt.uint32
ALU = mybir.AluOpType
ACT = mybir.ActivationFunctionType
AX = mybir.AxisListType

B, S, D = 16, 112, 256
NK = 375
H, HD = 16, 16
E, FF = 8, 512
EPS = 1e-5
P = 128
T = B * S
KC = D // P
FC = FF // P
KEY_CHUNKS = [(0, 128), (128, 128), (256, NK - 256)]
HH = H // 2
PARTS = 3
K_PARTS = [0, 1, 2, 0, 1, 0]
Q_PARTS = [0, 0, 0, 1, 1, 2]
NPAIR = len(K_PARTS)
ROWS = NPAIR * HD
SHIFT_ROWS = 2
STACK = ROWS + SHIFT_ROWS
VW = HD + 1
HQ = HH * S
NB = 4 * S // 32
G, GB = 4, 4
GT = GB * S
TILES = (T + E * (P - 1)) // P
XROW = D + 1
NOBODY = 1 << 20


def build(nc, x, ctx, g_xattn, g_ffn, Wq, Wk, Wv, Wo, bo, ln_w, ln_b, router_w, gate_w, up_w, down_w,
          sh_gate, sh_up, sh_down, out):
    stack = ExitStack()
    with stack:
        def sem(name):
            return stack.enter_context(nc.semaphore(name))

        def sb(name, shape, dt=F32, scope=stack):
            return scope.enter_context(nc.sbuf_tensor(name, shape, dt))

        def bank(name, n=1):
            return stack.enter_context(nc.psum_tensor(name, [P, n * 512], F32))

        def need(eng, s, count):
            if not (isinstance(count, int) and count <= 0):
                eng.wait_ge(s, count)

        k_dram = nc.dram_tensor("k_parts_dram", [B, 2, PARTS, HD, HH, NK], BF16).ap()
        q_dram = nc.dram_tensor("q_parts_dram", [B, 2, NPAIR, HD, HH, S], BF16).ap()
        v_dram = nc.dram_tensor("v_dram", [B, P, 3 * H * VW], F32).ap()
        xs_dram = nc.dram_tensor("sorted_rows_dram", [TILES * P, XROW], F32).ap()
        resid_dram = nc.dram_tensor("resid_dram", [T, D], F32).ap()

        ident = sb("ident", [P, P])
        identb = sb("identb", [P, P], BF16)
        woT = sb("woT", [P, 4, D])
        xall = sb("xall", [S, B, D])
        eg = sb("eg", [P, E, KC, FF])
        eu = sb("eu", [P, E, KC, FF])
        ed = sb("ed", [P, E, FC, D])
        sg = sb("sg", [P, KC, FF])
        su = sb("su", [P, KC, FF])
        sd = sb("sd", [P, FC, D])
        rw = sb("rw", [P, KC, E])
        lnw = sb("lnw", [S, D])
        lnb = sb("lnb", [S, D])
        bo_b = sb("bo_b", [S, D])
        gates = sb("gates", [P, 2])
        tanhs = sb("tanhs", [P, 2])
        st = sb("st", [S, B, 6])
        mean = sb("mean", [S, B])
        var = sb("var", [S, B])
        tmp = sb("tmp", [S, B])
        rstd = sb("rstd", [S, B])
        rstd2 = sb("rstd2", [S, B])
        mhalf = sb("mhalf", [S, B])
        negmax = sb("negmax", [S, H])
        mparts = sb("mparts", [S, H, SHIFT_ROWS], BF16)

        lower = sb("lower", [S, S])
        ones = sb("ones", [S, P])
        iota_e = sb("iota_e", [S, E])
        iota_t = sb("iota_t", [P, TILES])
        start_t = sb("start_t", [P, TILES])

        s0 = ExitStack()
        cin = [sb(f"cin{p}", [P, 3, D], scope=s0) for p in range(2)]
        ctxT = [sb(f"ctxT{p}", [P, KC, NK + 1], scope=s0) for p in range(2)]
        kp = [sb(f"kp{p}", [P, 2, PARTS, NK], BF16, scope=s0) for p in range(2)]
        kr = [sb(f"kr{p}", [P, 2, NK], scope=s0) for p in range(2)]
        vg = [sb(f"vg{p}", [P, 3, H, VW], scope=s0) for p in range(2)]
        wqT = sb("wqT", [P, KC, D], scope=s0)
        wkT = sb("wkT", [P, KC, D], scope=s0)
        wvT = sb("wvT", [P, KC, D], scope=s0)
        zrow = sb("zrow", [P, XROW], scope=s0)
        s0a = ExitStack()
        wraw = sb("wraw", [P, 4, KC, D], scope=s0a)
        woX = sb("woX", [P, KC, 4, 4, 2, HD], scope=s0a)
        s0a.close()
        xn = [sb(f"xn{p}", [S, D], scope=s0) for p in range(2)]
        xnT = sb("xnT", [P, KC, T], scope=s0)
        qp = [sb(f"qp{p}", [P, PARTS, GT], BF16, scope=s0) for p in range(2)]
        qr = [sb(f"qr{p}", [P, GT], scope=s0) for p in range(2)]
        s0.close()

        s1 = ExitStack()
        kst = [sb(f"kst{p}", [STACK, H * NK + 16], BF16, scope=s1) for p in range(2)]
        qst = [sb(f"qst{p}", [STACK, H * S], BF16, scope=s1) for p in range(2)]
        vst = [sb(f"vst{p}", [P, 3, H, VW], scope=s1) for p in range(2)]
        pT = [sb(f"pT{hh}", [P, 3, HQ], scope=s1) for hh in range(2)]
        turned = sb("turned", [P, NB, 32], scope=s1)
        rec = sb("rec", [P, NB], scope=s1)
        scaled = sb("scaled", [P, NB, 32], scope=s1)
        att = sb("att", [P, 4 * S], scope=s1)
        s1.close()

        s2 = ExitStack()
        xn2 = sb("xn2", [S, GB, D], scope=s2)
        xf = sb("xf", [S, GB, D], scope=s2)
        xfT = sb("xfT", [P, KC, T], scope=s2)
        xe = sb("xe", [S, B, XROW], scope=s2)
        silu = [sb(f"silu{p}", [P, GT], scope=s2) for p in range(2)]
        hT = sb("hT", [P, FC, GT], scope=s2)
        lgT = sb("lgT", [E, GT], scope=s2)
        lg = sb("lg", [S, GB, E], scope=s2)
        top = sb("top", [S, GB], scope=s2)
        score = sb("score", [S, GB], scope=s2)
        eq = sb("eq", [S, GB, E], scope=s2)
        pick = sb("pick", [S, GB], scope=s2)
        hot = sb("hot", [S, B, E], scope=s2)
        before = sb("before", [S, B + 1, E], scope=s2)
        tot = sb("tot", [P, E], scope=s2)
        tot_i = sb("tot_i", [P, E], I32, scope=s2)
        ntile = sb("ntile", [P, E], scope=s2)
        upto = sb("upto", [P, E], scope=s2)
        first_row = sb("first_row", [P, E], scope=s2)
        passed = sb("passed", [P, TILES * E], scope=s2)
        texp = sb("texp", [P, TILES], scope=s2)
        texp_i = sb("texp_i", [P, TILES], I32, scope=s2)
        rank = sb("rank", [S, B, E], scope=s2)
        pos = sb("pos", [S, B], scope=s2)
        pos_i = sb("pos_i", [S, B], U32, scope=s2)
        xs = [sb(f"xs{p}", [P, XROW], scope=s2) for p in range(2)]
        who = [sb(f"who{p}", [P, 1], U32, scope=s2) for p in range(2)]
        xsT = sb("xsT", [P, KC, P], scope=s2)
        gact = sb("gact", [P, FF], scope=s2)
        hrow = sb("hrow", [P, FF], scope=s2)
        hrT = sb("hrT", [P, FC, P], scope=s2)
        resid = [sb(f"resid{p}", [P, D], scope=s2) for p in range(2)]
        orow = [sb(f"orow{p}", [P, D], scope=s2) for p in range(2)]
        s2.close()

        pair = [bank("pairA", 2), bank("pairB", 2)]
        single = [bank(f"single{n}") for n in range(4)]
        b0, b1 = pair[0][:, 0:512], pair[0][:, 512:1024]
        b2, b3 = pair[1][:, 0:512], pair[1][:, 512:1024]
        b4, b5, b6, b7 = (s[:, :] for s in single)

        ident_z, ident_ok, identb_ok = sem("ident_z"), sem("ident_ok"), sem("identb_ok")
        fill_ok = sem("fill_ok")
        w_in = sem("w_in")
        w2_in = sem("w2_in")
        x_in, small_in, sh_in = sem("x_in"), sem("small_in"), sem("sh_in")
        exp_in = sem("exp_in")
        zero_out = sem("zero_out")
        ones_v = sem("ones_v")
        wox_ok = sem("wox_ok")
        wT_done, wT_ok = sem("wT_done"), sem("wT_ok")
        woT_done, woT_ok = sem("woT_done"), sem("woT_ok")
        cin_in = [sem(f"cin_in{p}") for p in range(2)]
        ct_done = sem("ct_done")
        ct_a, ct_v = sem("ct_a"), sem("ct_v")
        kmm, vmm = sem("kmm"), sem("vmm")
        k1_ok, kr_ok, k2_ok, k3_ok = sem("k1_ok"), sem("kr_ok"), sem("k2_ok"), sem("k3_ok")
        v_a, v_v = sem("v_a"), sem("v_v")
        k_out = [sem(f"k_out{p}") for p in range(2)]
        v_out = [sem(f"v_out{p}") for p in range(2)]
        st_ok = sem("st_ok")
        lnv = sem("lnv")
        rs_ok = sem("rs_ok")
        xn_ok, xt_done, xt_ok = sem("xn_ok"), sem("xt_done"), sem("xt_ok")
        qmm, q1_ok, qr_ok, q2_ok, q3_ok = sem("qmm"), sem("q1_ok"), sem("qr_ok"), sem("q2_ok"), sem("q3_ok")
        q_out = [sem(f"q_out{p}") for p in range(2)]
        tanh_ok, tb_ok, xb_ok = sem("tanh_ok"), sem("tb_ok"), sem("xb_ok")
        k_in = [[sem(f"k_in{p}{hh}") for hh in range(2)] for p in range(2)]
        v_in = [sem(f"v_in{p}") for p in range(2)]
        ones_k = sem("ones_k")
        smax, red = sem("smax"), sem("red")
        mp1, mp_ok = sem("mp1"), sem("mp_ok")
        mt_done, mt_ok = sem("mt_done"), sem("mt_ok")
        sc_done, exp_ok, pv_done = sem("sc_done"), sem("exp_ok"), sem("pv_done")
        turned_ok, rec_ok, scaled_ok, att_ok = sem("turned_ok"), sem("rec_ok"), sem("scaled_ok"), sem("att_ok")
        wo_done, x2_ok = sem("wo_done"), sem("x2_ok")
        const_ok, s2_init, s2_fill = sem("const_ok"), sem("s2_init"), sem("s2_fill")
        xn2_ok, xf_ok, xfb_ok = sem("xn2_ok"), sem("xf_ok"), sem("xfb_ok")
        xn2_scaled, base_ok = sem("xn2_scaled"), sem("base_ok")
        xft_done, xft_a, xft_v = sem("xft_done"), sem("xft_a"), sem("xft_v")
        lgT_done, lgT_ok, lg_done = sem("lgT_done"), sem("lgT_ok"), sem("lg_done")
        rt = sem("rt")
        tanh_top, score_ok, xe_ok = sem("tanh_top"), sem("score_ok"), sem("xe_ok")
        g_done, u_done, silu_ok, h_ok = sem("g_done"), sem("u_done"), sem("silu_ok"), sem("h_ok")
        dn_done, y_ok, resid_out = sem("dn_done"), sem("y_ok"), sem("resid_out")
        rank_done, rk = sem("rank_done"), sem("rk")
        scat = sem("scat")
        xs_in = [sem(f"xs_in{p}") for p in range(2)]
        who_ok = sem("who_ok")
        resid_in = [sem(f"resid_in{p}") for p in range(2)]
        xst_done, xst_ok = sem("xst_done"), sem("xst_ok")
        gt_done, ut_done, gact_ok, hrow_ok = sem("gt_done"), sem("ut_done"), sem("gact_ok"), sem("hrow_ok")
        ht_done, hrt_ok, dt_done, orow_ok = sem("ht_done"), sem("hrt_ok"), sem("dt_done"), sem("orow_ok")
        out_done = [sem(f"out_done{p}") for p in range(2)]
        ROUTER_STEPS = 6 + GB
        RANK_STEPS = 19

        def stats(ve, first):
            cols = slice(0, B)
            me, mo = st[:, cols, 1], st[:, cols, 4]
            ve_, vo = st[:, cols, 2], st[:, cols, 5]
            nc.vector.tensor_tensor(mean[:, cols], me, mo, ALU.add).then_inc(lnv, 1)
            nc.vector.tensor_tensor(tmp[:, cols], me, mo, ALU.subtract).then_inc(lnv, 1)
            nc.vector.tensor_tensor(var[:, cols], ve_, vo, ALU.add).then_inc(lnv, 1)
            ve.wait_ge(lnv, first + 3)
            nc.vector.tensor_scalar(mean[:, cols], mean[:, cols], 0.5, None, ALU.mult).then_inc(lnv, 1)
            nc.vector.tensor_tensor(tmp[:, cols], tmp[:, cols], tmp[:, cols], ALU.mult).then_inc(lnv, 1)
            nc.vector.tensor_scalar(var[:, cols], var[:, cols], 1.0 / D, None, ALU.mult).then_inc(lnv, 1)
            ve.wait_ge(lnv, first + 6)
            nc.vector.scalar_tensor_tensor(out=var[:, cols], in0=tmp[:, cols], scalar=0.25, in1=var[:, cols],
                                           op0=ALU.mult, op1=ALU.add).then_inc(lnv, 1)

        STATS_STEPS = 7

        block = stack.enter_context(nc.Block())

        @block.sync
        def _(sp):
            def load_ctx(b, p):
                src = ctx[bass.ds(b, 1)]
                sp.dma_start(cin[p][:, 0:2, :], src[:, 0:256, :].rearrange("a (c p) d -> p (a c) d", p=P))\
                    .then_inc(cin_in[p], 16)
                sp.dma_start(cin[p][0:NK - 256, 2, :], src[:, 256:NK, :].rearrange("a p d -> (a p) d"))\
                    .then_inc(cin_in[p], 16)

            def weight(dst, w):
                return sp.dma_start(dst, w.rearrange("(k p) d -> p k d", p=P))

            weight(wraw[:, 0], Wk).then_inc(w_in, 16)
            weight(wraw[:, 1], Wv).then_inc(w_in, 16)
            load_ctx(0, 0)
            load_ctx(1, 1)
            weight(wraw[:, 2], Wq).then_inc(w2_in, 16)
            weight(wraw[:, 3], Wo).then_inc(w2_in, 16)
            sp.dma_start(xall[:, :, :], x.rearrange("b s d -> s b d")).then_inc(x_in, 16)
            for dst, src in ((bo_b, bo), (lnw, ln_w), (lnb, ln_b)):
                sp.dma_start(dst[:, :], src.rearrange("(a d) -> a d", a=1).broadcast_to([S, D])).then_inc(small_in, 16)
            sp.dma_start(gates[:, 0:1], g_xattn.rearrange("(a d) -> a d", a=1).broadcast_to([P, 1]))\
                .then_inc(small_in, 16)
            sp.dma_start(gates[:, 1:2], g_ffn.rearrange("(a d) -> a d", a=1).broadcast_to([P, 1]))\
                .then_inc(small_in, 16)
            sp.wait_ge(fill_ok, 3)
            for t in range(TILES):
                sp.dma_start(xs_dram[t * P:(t + 1) * P, :], zrow[:, :]).then_inc(zero_out, 16)

            def store_and_load(b, p, i, load):
                sp.wait_ge(k3_ok, b + 1)
                sp.dma_start(k_dram[bass.ds(b, 1)].rearrange("a h t d e k -> (d e) (a h t) k"),
                             kp[p][:, :, :, :].rearrange("p h t k -> p (h t) k")).then_inc(k_out[p], 16)
                sp.wait_ge(v_a, b + 1)
                sp.wait_ge(v_v, b + 1)
                sp.dma_start(v_dram[bass.ds(b, 1)].rearrange("a p n -> (a p) n"),
                             vg[p][:, :, :, :].rearrange("p c h w -> p (c h w)")).then_inc(v_out[p], 16)
                if load:
                    sp.wait_ge(ct_done, 2 * b + 2)
                    load_ctx(b + 2, p)

            with sp.Fori(0, B // 2 - 1) as i:
                for p in range(2):
                    store_and_load(2 * i + p, p, i, True)
                for dst, w in ((eg, gate_w), (eu, up_w), (ed, down_w)):
                    sp.dma_start(dst[:, bass.ds(i, 1), :, :],
                                 w[bass.ds(i, 1)].rearrange("e (k p) f -> p e k f", p=P)).then_inc(exp_in, 16)
            for b in (B - 2, B - 1):
                store_and_load(b, b % 2, B // 2 - 1, False)
            for dst, w in ((eg, gate_w), (eu, up_w), (ed, down_w)):
                sp.dma_start(dst[:, E - 1], w[E - 1].rearrange("(k p) f -> p k f", p=P)).then_inc(exp_in, 16)
            for dst, w in ((sg, sh_gate), (su, sh_up), (sd, sh_down), (rw, router_w)):
                weight(dst[:, :, :], w).then_inc(sh_in, 16)

            with sp.Fori(0, G) as g:
                for o in range(2):
                    sp.wait_ge(q3_ok, 2 * g + o + 1)
                    for j, part in enumerate(Q_PARTS):
                        dst = q_dram[bass.ds(GB * g, GB), o, j].rearrange("b d e q -> (d e) b q")
                        sp.dma_start(dst, qp[o][:, part, :].rearrange("p (b q) -> p b q", q=S))\
                            .then_inc(q_out[o], 16)

            for p in range(2):
                sp.wait_ge(k_out[p], 16 * B // 2)
                sp.wait_ge(v_out[p], 16 * B // 2)
                sp.wait_ge(q_out[p], 16 * NPAIR * G)
            sp.wait_ge(zero_out, 16 * TILES)

            def load_kq(b, p, hh):
                need(sp, sc_done, 6 * b - 12 + 3 * hh + 3)
                src = k_dram[bass.ds(b, 1), hh]
                row = 0
                for n in (3, 2, 1):
                    sp.dma_start(kst[p][row:row + n * HD, hh * HH * NK:(hh + 1) * HH * NK],
                                 src[:, 0:n].rearrange("a t d e k -> (a t d) (e k)")).then_inc(k_in[p][hh], 16)
                    row += n * HD
                sp.dma_start(qst[p][0:ROWS, hh * HQ:(hh + 1) * HQ],
                             q_dram[bass.ds(b, 1), hh].rearrange("a t d e q -> (a t d) (e q)"))\
                    .then_inc(k_in[p][hh], 16)

            def load_v(b, p):
                need(sp, pv_done, 2 * b - 2)
                sp.dma_start(vst[p][:, :, :, :].rearrange("p c h w -> p (c h w)"),
                             v_dram[bass.ds(b, 1)].rearrange("a p n -> (a p) n")).then_inc(v_in[p], 16)

            def load_batch(b, p):
                load_kq(b, p, 0)
                load_kq(b, p, 1)
                load_v(b, p)

            load_batch(0, 0)
            load_batch(1, 1)
            with sp.Fori(1, B // 2) as i:
                load_batch(2 * i, 0)
                load_batch(2 * i + 1, 1)

            out_rows = resid_dram.rearrange("(b s) d -> s b d", s=S)
            with sp.Fori(0, G) as g:
                sp.wait_ge(y_ok, 2 * g + 2)
                sp.dma_start(out_rows[:, bass.ds(GB * g, GB), :], xall[:, bass.ds(GB * g, GB), :]).then_inc(resid_out, 16)

            def load_rows(t, p):
                need(sp, xst_done, t - 1)
                need(sp, who_ok, t - 1)
                sp.dma_start(xs[p][:, :], xs_dram[bass.ds(t * P, P), :]).then_inc(xs_in[p], 16)

            sp.wait_ge(scat, 16 * B)
            load_rows(0, 0)
            load_rows(1, 1)
            with sp.Fori(1, TILES // 2) as i:
                load_rows(2 * i, 0)
                load_rows(2 * i + 1, 1)
            load_rows(TILES - 1, 0)

        @block.tensor
        def _(pe):
            def tr(out_, in_, n):
                return nc.tensor.transpose(out_, in_, ident[0:n, 0:n])

            pe.wait_ge(ident_ok, 1)
            pe.wait_ge(w_in, 32)
            for n, w in enumerate((0, 1, 2)):
                if n == 2:
                    pe.wait_ge(w2_in, 32)
                for k in range(KC):
                    for o in range(KC):
                        mm = tr((b0, b1, b2)[n][:, k * D + o * P:k * D + (o + 1) * P], wraw[:, w, o, k * P:(k + 1) * P], P)
                mm.then_inc(wT_done, 1)
            pe.wait_ge(wox_ok, 1)
            for g in range(4):
                for o in range(KC):
                    mm = tr((b3, b4)[g // 2][:, (g % 2) * D + o * P:(g % 2) * D + (o + 1) * P],
                            woX[:, o, g].rearrange("p j two d -> p (j two d)"), P)
            mm.then_inc(woT_done, 1)
            pe.wait_ge(wT_ok, 3)
            pe.wait_ge(woT_ok, 2)

            def turn_ctx(b, p, i):
                pe.wait_ge(cin_in[p], 32 * i + 32)
                for k in range(KC):
                    need(pe, (ct_a, ct_v)[k], b)
                    for c, (k0, n) in enumerate(KEY_CHUNKS):
                        mm = tr((b0, b1)[k][:, k0:k0 + n], cin[p][0:n, c, k * P:(k + 1) * P], n)
                    mm.then_inc(ct_done, 1)

            def project(b, p):
                pe.wait_ge(ct_a, b + 1)
                pe.wait_ge(ct_v, b + 1)
                for o in range(2):
                    need(pe, kr_ok, 2 * b - 2 + o + 1)
                    for k in range(KC):
                        mm = nc.tensor.matmul((b2, b3)[o][:, 0:NK], wkT[:, k, o * P:(o + 1) * P], ctxT[p][:, k, 0:NK],
                                              start=(k == 0), stop=(k == KC - 1))
                    mm.then_inc(kmm, 1)
                need(pe, v_a, b)
                need(pe, v_v, b)
                for c, (k0, n) in enumerate(KEY_CHUNKS):
                    for k in range(KC):
                        mm = nc.tensor.matmul((b4, b5)[c // 2][0:n, (c % 2) * D:(c % 2 + 1) * D],
                                              ctxT[p][:, k, k0:k0 + n], wvT[:, k, :],
                                              start=(k == 0), stop=(k == KC - 1))
                    if c > 0:
                        mm.then_inc(vmm, 1)

            turn_ctx(0, 0, 0)
            turn_ctx(1, 1, 0)
            project(0, 0)
            with pe.Fori(1, B // 2) as i:
                turn_ctx(2 * i, 0, i)
                project(2 * i - 1, 1)
                turn_ctx(2 * i + 1, 1, i)
                project(2 * i, 0)
            project(B - 1, 1)

            def turn_x(i):
                for bb in range(2):
                    pe.wait_ge(xn_ok, 2 * i + bb + 1)
                    if bb == 0:
                        need(pe, xt_ok, i)
                    for k in range(KC):
                        mm = tr(b6[:, k * 2 * S + bb * S:k * 2 * S + (bb + 1) * S], xn[bb][:, k * P:(k + 1) * P], S)
                    mm.then_inc(xt_done, 1)

            turn_x(0)
            with pe.Fori(1, B // 2) as i:
                turn_x(i)

            def project_q(g, o):
                pe.wait_ge(xt_ok, 2 * g + 2)
                need(pe, qr_ok, 2 * g - 1 + o)
                for k in range(KC):
                    mm = nc.tensor.matmul((b0, b1)[o][:, 0:GT], wqT[:, k, o * P:(o + 1) * P], xnT[:, k, bass.ds(GT * g, GT)],
                                          start=(k == 0), stop=(k == KC - 1))
                mm.then_inc(qmm, 1)

            for o in range(2):
                project_q(0, o)
            with pe.Fori(1, G) as g:
                for o in range(2):
                    project_q(g, o)

            def max_scores(b, p, hh, heads):
                for h in heads:
                    n = 16 * b + hh * HH + h
                    need(pe, red, n - 1)
                    hd = hh * HH + h
                    nc.tensor.matmul((b4, b5)[h % 2][0:S, 0:NK], qst[p][0:ROWS, hd * S:(hd + 1) * S],
                                     kst[p][0:ROWS, hd * NK:(hd + 1) * NK], start=True, stop=True).then_inc(smax, 1)

            def turn_max(b, p, hh):
                pe.wait_ge(mp_ok, 2 * b + hh + 1)
                need(pe, mt_ok, 2 * b + hh)
                need(pe, x2_ok, b - 2 + hh)
                for h in range(HH):
                    hd = hh * HH + h
                    mm = nc.tensor.transpose(b7.bitcast(BF16)[ROWS:STACK, h * S:(h + 1) * S], mparts[:, hd, :],
                                             identb[0:S, 0:S])
                mm.then_inc(mt_done, 1)

            def scores(b, p, hh, c):
                n = 6 * b + 3 * hh + c
                k0 = KEY_CHUNKS[c][0]
                if c == 0:
                    pe.wait_ge(mt_ok, 2 * b + hh + 1)
                need(pe, exp_ok, n - 1)
                for h in range(HH):
                    hd = hh * HH + h
                    at = (h // 4) * 512 + (h % 4) * S
                    mm = nc.tensor.matmul(pair[(3 * hh + c) % 2][:, at:at + S], kst[p][:, hd * NK + k0:hd * NK + k0 + P],
                                          qst[p][:, hd * S:(hd + 1) * S], start=True, stop=True)
                mm.then_inc(sc_done, 1)

            def values(b, p, hh):
                pe.wait_ge(exp_ok, 6 * b + 3 * hh + 3)
                if hh == 0:
                    pe.wait_ge(v_in[p], 8 * (b - p) + 16)
                    need(pe, turned_ok, b)
                for g in range(2):
                    for c, (_, n) in enumerate(KEY_CHUNKS):
                        for j in range(4):
                            h = 4 * g + j
                            col = (2 * hh + g) * S
                            mm = nc.tensor.matmul(b6[32 * j:32 * j + VW, col:col + S], vst[p][0:n, c, hh * HH + h, :],
                                                  pT[hh][0:n, c, h * S:(h + 1) * S], start=(c == 0), stop=(c == 2))
                mm.then_inc(pv_done, 1)

            def output(b, turns):
                pe.wait_ge(att_ok, b + 1)
                pe.wait_ge(mt_ok, turns)
                for g in range(4):
                    mm = nc.tensor.matmul(b7[0:S, 0:D], att[:, g * S:(g + 1) * S], woT[:, g, :],
                                          start=(g == 0), stop=(g == 3))
                mm.then_inc(wo_done, 1)

            def loaded(b, p, hh):
                pe.wait_ge(k_in[p][hh], 32 * (b - p) + 64)

            HEADS = [(0, 1, 2), (3, 4, 5), (6, 7)]

            def batch(b, p, first=False, last=False):
                for hh in range(2):
                    for c in range(3):
                        scores(b, p, hh, c)
                        if not last:
                            if c == 0:
                                loaded(b + 1, 1 - p, hh)
                            max_scores(b + 1, 1 - p, hh, HEADS[c])
                        if c == 0 and hh == 0:
                            turn_max(b, p, 1)
                        if c == 0 and hh == 1 and not last:
                            turn_max(b + 1, 1 - p, 0)
                    if hh == 0 and not first:
                        values(b - 1, 1 - p, 1)
                    if hh == 1:
                        values(b, p, 0)
                        if not first:
                            output(b - 1, 2 * b + 2 if last else 2 * b + 3)

            pe.wait_ge(ones_k, 4)
            for hh in range(2):
                loaded(0, 0, hh)
                max_scores(0, 0, hh, range(HH))
                if hh == 0:
                    turn_max(0, 0, 0)
            batch(0, 0, first=True)
            batch(1, 1)
            with pe.Fori(1, B // 2 - 1) as i:
                batch(2 * i, 0)
                batch(2 * i + 1, 1)
            batch(B - 2, 0)
            batch(B - 1, 1, last=True)
            values(B - 1, 1, 1)
            output(B - 1, 2 * B)

            def turn_xf(g):
                pe.wait_ge(xfb_ok, g + 1)
                need(pe, y_ok, 2 * g - 2)
                for k in range(KC):
                    need(pe, (xft_a, xft_v)[k], g)
                    for i in range(GB):
                        mm = tr((b0, b1)[k][:, i * S:(i + 1) * S], xf[:, i, k * P:(k + 1) * P], S)
                    mm.then_inc(xft_done, 1)

            def router_logits(g):
                pe.wait_ge(xft_a, g + 1)
                pe.wait_ge(xft_v, g + 1)
                need(pe, rt, ROUTER_STEPS * (g - 1) + 1)
                for k in range(KC):
                    mm = nc.tensor.matmul(b2[0:E, 0:GT], rw[:, k, :], xfT[:, k, bass.ds(GT * g, GT)],
                                          start=(k == 0), stop=(k == KC - 1))
                mm.then_inc(lgT_done, 1)

            def turn_logits(g):
                for i in range(GB):
                    mm = tr(b2[0:S, GT + i * E:GT + (i + 1) * E], lgT[:, i * S:(i + 1) * S], E)
                mm.then_inc(lg_done, 1)

            def gate_up(g, f):
                n = FC * g + f
                for w, banks, free, done in ((sg, (b3, b5), silu_ok, g_done), (su, (b4, b6), h_ok, u_done)):
                    need(pe, free, n - 1)
                    if f == 0 and w is su:
                        pe.wait_ge(lgT_ok, g + 1)
                    for k in range(KC):
                        mm = nc.tensor.matmul(banks[f % 2][:, 0:GT], w[:, k, f * P:(f + 1) * P],
                                              xfT[:, k, bass.ds(GT * g, GT)], start=(k == 0), stop=(k == KC - 1))
                    mm.then_inc(done, 1)

            def down(g, last=False):
                pe.wait_ge(h_ok, FC * g + FC)
                for j in range(2):
                    need(pe, y_ok, 2 * g - 1 + j)
                    if j == 0 and last:
                        pe.wait_ge(rk, 14)
                    if j == 1 and not last:
                        pe.wait_ge(xft_a, g + 2)
                    for i in range(2):
                        for f in range(FC):
                            at = (2 * j + i) * S
                            mm = nc.tensor.matmul((b7, b0)[j][0:S, i * D:(i + 1) * D], hT[:, f, at:at + S], sd[:, f, :],
                                                  start=(f == 0), stop=(f == FC - 1))
                    mm.then_inc(dn_done, 1)

            def ranks():
                pe.wait_ge(rt, ROUTER_STEPS * G)
                pe.wait_ge(y_ok, 2 * (G - 1) - 1)
                nc.tensor.matmul(b7[0:S, 0:B * E], lower[:, :], hot[:, :, :].rearrange("p b e -> p (b e)"),
                                 start=True, stop=False)
                nc.tensor.matmul(b7[0:S, 0:B * E], ones[:, 0:S], before[:, 0:B, :].rearrange("p b e -> p (b e)"),
                                 start=False, stop=True)
                nc.tensor.matmul(b7[:, B * E:(B + 1) * E], ones[:, :], before[:, B, :], start=True, stop=True)\
                    .then_inc(rank_done, 1)

            def group(g, last=False):
                gate_up(g, 0)
                turn_logits(g)
                gate_up(g, 1)
                gate_up(g, 2)
                if last:
                    ranks()
                gate_up(g, 3)
                if not last:
                    turn_xf(g + 1)
                down(g, last)
                if not last:
                    router_logits(g + 1)

            pe.wait_ge(x2_ok, B)
            pe.wait_ge(exp_ok, 6 * B)
            pe.wait_ge(sh_in, 64)
            pe.wait_ge(const_ok, 4)
            turn_xf(0)
            router_logits(0)
            group(0)
            with pe.Fori(1, G - 1) as g:
                group(g)
            group(G - 1, last=True)

            def expert_of(t):
                return nc.tensor.value_load(texp_i[0:1, bass.ds(t, 1)], min_val=0, max_val=E - 1)

            def turn_rows(t, p, i):
                pe.wait_ge(xs_in[p], 16 * i + 16)
                need(pe, xst_ok, t)
                for k in range(KC):
                    mm = tr(b0[:, k * P:(k + 1) * P], xs[p][:, k * P:(k + 1) * P], P)
                mm.then_inc(xst_done, 1)

            def tile_product(w, e, out_bank, done):
                for k in range(KC):
                    mm = nc.tensor.matmul(out_bank, xsT[:, k, :], w[:, bass.ds(e, 1), k, :].rearrange("p a f -> p (a f)"),
                                          start=(k == 0), stop=(k == KC - 1))
                mm.then_inc(done, 1)

            def turn_hidden(t):
                pe.wait_ge(hrow_ok, t + 1)
                need(pe, hrt_ok, t)
                for f in range(FC):
                    mm = tr(b1[:, f * P:(f + 1) * P], hrow[:, f * P:(f + 1) * P], P)
                mm.then_inc(ht_done, 1)

            def tile_down(t, e):
                pe.wait_ge(hrt_ok, t + 1)
                need(pe, orow_ok, t)
                for f in range(FC):
                    mm = nc.tensor.matmul(b7[:, 0:D], hrT[:, f, :], ed[:, bass.ds(e, 1), f, :].rearrange("p a d -> p (a d)"),
                                          start=(f == 0), stop=(f == FC - 1))
                mm.then_inc(dt_done, 1)

            def tile(t, p, i, first=False, last=False):
                e = expert_of(t)
                pe.wait_ge(xst_ok, t + 1)
                need(pe, gact_ok, t)
                tile_product(eg, e, b3, gt_done)
                if not first:
                    turn_hidden(t - 1)
                need(pe, hrow_ok, t)
                tile_product(eu, e, b4, ut_done)
                if not last:
                    turn_rows(t + 1, 1 - p, i)
                if not first:
                    tile_down(t - 1, expert_of(t - 1))

            pe.wait_ge(y_ok, 2 * G)
            pe.wait_ge(rk, RANK_STEPS)
            pe.wait_ge(exp_in, 16 * 3 * E)
            turn_rows(0, 0, 0)
            tile(0, 0, 0, first=True)
            tile(1, 1, 1)
            tile(2, 0, 1)
            with pe.Fori(2, TILES // 2) as i:
                tile(2 * i - 1, 1, i)
                tile(2 * i, 0, i)
            tile(TILES - 2, 1, TILES // 2)
            tile(TILES - 1, 0, TILES // 2, last=True)
            turn_hidden(TILES - 1)
            tile_down(TILES - 1, expert_of(TILES - 1))

        @block.scalar
        def _(act):
            def copy(o, i_, scale=1.0):
                return nc.scalar.activation(o, i_, ACT.Copy, scale=scale)

            def by_dim(w, src):
                return (w[:, :, :].rearrange("p k (o d e) -> p (k o) d e", o=2, d=HD),
                        src[:, 0:KC * D].rearrange("p (ko e d) -> p ko d e", e=HH, d=HD))

            act.wait_ge(wT_done, 1)
            for ko in range(4):
                o_, i_ = by_dim(wkT, b0)
                mm = copy(o_[:, ko], i_[:, ko])
            mm.then_inc(wT_ok, 1)
            act.wait_ge(wT_done, 2)
            copy(wvT[:, :, :].rearrange("p k d -> p (k d)"), b1).then_inc(wT_ok, 1)
            act.wait_ge(wT_done, 3)
            for ko in range(4):
                o_, i_ = by_dim(wqT, b2)
                mm = copy(o_[:, ko], i_[:, ko], scale=HD ** -0.5)
            mm.then_inc(wT_ok, 1)

            def ctx_batch(b, p):
                act.wait_ge(ct_done, 2 * b + 1)
                need(act, vmm, 2 * b - 2)
                copy(ctxT[p][:, 0, 0:NK], b0[:, 0:NK]).then_inc(ct_a, 1)

            def parts_batch(b, p, i):
                need(act, k_out[p], 16 * i)
                for o in range(2):
                    act.wait_ge(kmm, 2 * b + o + 1)
                    copy(kp[p][:, o, 0, :], (b2, b3)[o][:, 0:NK]).then_inc(k1_ok, 1)
                act.wait_ge(vmm, 2 * b + 1)
                need(act, v_out[p], 16 * i)
                if isinstance(b, int) and b == 0:
                    act.wait_ge(ones_v, 2)
                copy(vg[p][:, 0:2, :, 0:HD], b4.rearrange("p (c h d) -> p c h d", c=2, h=H)).then_inc(v_a, 1)
                act.wait_ge(kr_ok, 2 * b + 2)
                copy(kp[p][:, :, 1, :], kr[p][:, :, :]).then_inc(k2_ok, 1)

            ctx_batch(0, 0)
            ctx_batch(1, 1)
            parts_batch(0, 0, 0)
            ctx_batch(2, 0)
            parts_batch(1, 1, 0)
            with act.Fori(1, B // 2 - 1) as i:
                ctx_batch(2 * i + 1, 1)
                parts_batch(2 * i, 0, i)
                ctx_batch(2 * i + 2, 0)
                parts_batch(2 * i + 1, 1, i)
            ctx_batch(B - 1, 1)
            parts_batch(B - 2, 0, B // 2 - 1)
            parts_batch(B - 1, 1, B // 2 - 1)
            act.wait_ge(small_in, 80)
            nc.scalar.activation(tanhs[:, :], gates[:, :], ACT.Tanh).then_inc(tanh_ok, 1)

            with act.Fori(0, B // 2) as i:
                act.wait_ge(xt_done, 2 * i + 2)
                copy(xnT[:, :, bass.ds(2 * S * i, 2 * S)], b6[:, 0:4 * S].rearrange("p (k n) -> p k n", k=KC))\
                    .then_inc(xt_ok, 1)

            def q_part(g, o):
                act.wait_ge(qmm, 2 * g + o + 1)
                need(act, q_out[o], 16 * NPAIR * g)
                copy(qp[o][:, 0, :], (b0, b1)[o][:, 0:GT]).then_inc(q1_ok, 1)

            def q_second(g, o):
                act.wait_ge(qr_ok, 2 * g + o + 1)
                copy(qp[o][:, 1, :], qr[o][:, :]).then_inc(q2_ok, 1)

            for step_ in (q_part, q_second):
                for o in range(2):
                    step_(0, o)
            with act.Fori(1, G) as g:
                for step_ in (q_part, q_second):
                    for o in range(2):
                        step_(g, o)

            def exps(b, hh, c):
                n = KEY_CHUNKS[c][1]
                act.wait_ge(sc_done, 6 * b + 3 * hh + c + 1)
                if c == 0:
                    need(act, pv_done, 2 * b - 1 + hh)
                nc.scalar.activation(pT[hh][0:n, c, :].rearrange("p (a n) -> p a n", a=2),
                                     pair[(3 * hh + c) % 2][0:n, :].rearrange("p (a n) -> p a n", a=2)[:, :, 0:4 * S],
                                     ACT.Exp).then_inc(exp_ok, 1)

            def put_max(b, p, hh):
                act.wait_ge(mt_done, 2 * b + hh + 1)
                need(act, sc_done, 6 * b - 12 + 3 * hh + 3)
                copy(qst[p][ROWS:STACK, hh * HQ:(hh + 1) * HQ], b7.bitcast(BF16)[ROWS:STACK, 0:HQ])\
                    .then_inc(mt_ok, 1)

            def batch(b, p, last=False):
                exps(b, 0, 0)
                put_max(b, p, 1)
                exps(b, 0, 1)
                exps(b, 0, 2)
                exps(b, 1, 0)
                if not last:
                    put_max(b + 1, 1 - p, 0)
                exps(b, 1, 1)
                exps(b, 1, 2)

            act.wait_ge(q3_ok, 2 * G)
            for p in range(2):
                act.wait_ge(q_out[p], 16 * NPAIR * G)
            put_max(0, 0, 0)
            batch(0, 0)
            batch(1, 1)
            with act.Fori(1, B // 2 - 1) as i:
                batch(2 * i, 0)
                batch(2 * i + 1, 1)
            batch(B - 2, 0)
            batch(B - 1, 1, last=True)

            def put_xf(g):
                act.wait_ge(xft_done, 2 * g + 1)
                copy(xfT[:, 0, bass.ds(GT * g, GT)], b0[:, 0:GT]).then_inc(xft_a, 1)

            def silu_chunk(g, f):
                n = FC * g + f
                act.wait_ge(g_done, n + 1)
                need(act, h_ok, n - 1)
                nc.scalar.activation(silu[f % 2][:, :], (b3, b5)[f % 2][:, 0:GT], ACT.Silu).then_inc(silu_ok, 1)

            def group(g, last=False):
                silu_chunk(g, 0)
                act.wait_ge(rt, ROUTER_STEPS * g + 2)
                nc.scalar.activation(score[:, :], top[:, :], ACT.Tanh, scale=0.5).then_inc(tanh_top, 1)
                for f in range(1, FC):
                    silu_chunk(g, f)
                if not last:
                    put_xf(g + 1)

            put_xf(0)
            group(0)
            with act.Fori(1, G - 1) as g:
                group(g)
            group(G - 1, last=True)

            def put_rows(t):
                act.wait_ge(xst_done, t + 1)
                copy(xsT[:, :, :].rearrange("p k n -> p (k n)"), b0[:, 0:D]).then_inc(xst_ok, 1)

            def tile(t, last=False):
                act.wait_ge(gt_done, t + 1)
                need(act, hrow_ok, t)
                nc.scalar.activation(gact[:, :], b3, ACT.Silu).then_inc(gact_ok, 1)
                if not last:
                    put_rows(t + 1)

            put_rows(0)
            tile(0)
            with act.Fori(1, TILES - 1) as t:
                tile(t)
            tile(TILES - 1, last=True)

        @block.vector
        def _(ve):
            ve.wait_ge(ident_ok, 1)
            nc.vector.tensor_copy(identb[:, :], ident[:, :]).then_inc(identb_ok, 1)
            for p in range(2):
                nc.vector.memset(vg[p][:, :, :, :], 1.0).then_inc(ones_v, 1)
            ve.wait_ge(w2_in, 32)
            ve.wait_ge(fill_ok, 3)
            for o in range(KC):
                last = nc.vector.tensor_copy(woX[:, o, :, :, 0, :], wraw[:, 3, o, :].rearrange("p (g j d) -> p g j d", g=4, j=4))
            last.then_inc(wox_ok, 1)
            ve.wait_ge(woT_done, 1)
            for n in range(2):
                nc.vector.tensor_copy(woT[:, 2 * n:2 * n + 2, :].rearrange("p g d -> p (g d)"), (b3, b4)[n]).then_inc(woT_ok, 1)

            def ctx_batch(b, p):
                ve.wait_ge(ct_done, 2 * b + 2)
                need(ve, vmm, 2 * b - 2)
                nc.vector.tensor_copy(ctxT[p][:, 1, 0:NK], b1[:, 0:NK]).then_inc(ct_v, 1)

            def parts_batch(b, p, i):
                for o in range(2):
                    ve.wait_ge(k1_ok, 2 * b + o + 1)
                    if o == 0:
                        need(ve, k3_ok, b - 1)
                    nc.vector.tensor_tensor(kr[p][:, o, :], (b2, b3)[o][:, 0:NK], kp[p][:, o, 0, :], ALU.subtract)\
                        .then_inc(kr_ok, 1)
                ve.wait_ge(vmm, 2 * b + 2)
                need(ve, v_out[p], 16 * i)
                n = KEY_CHUNKS[2][1]
                nc.vector.tensor_copy(vg[p][0:n, 2, :, 0:HD], b5[0:n, 0:D].rearrange("p (h d) -> p h d", h=H)).then_inc(v_v, 1)
                nc.vector.bn_stats(st[:, bass.ds(b, 1), :].rearrange("p a n -> p (a n)"),
                                   xall[:, bass.ds(b, 1), :].rearrange("p a n -> p (a n)")).then_inc(st_ok, 1)

            ctx_batch(0, 0)
            ctx_batch(1, 1)
            ve.wait_ge(x_in, 16)
            ve.wait_ge(ones_v, 2)
            parts_batch(0, 0, 0)
            ctx_batch(2, 0)
            parts_batch(1, 1, 0)
            with ve.Fori(1, B // 2 - 1) as i:
                ctx_batch(2 * i + 1, 1)
                parts_batch(2 * i, 0, i)
                ctx_batch(2 * i + 2, 0)
                parts_batch(2 * i + 1, 1, i)
            ctx_batch(B - 1, 1)
            parts_batch(B - 2, 0, B // 2 - 1)
            parts_batch(B - 1, 1, B // 2 - 1)

            ve.wait_ge(st_ok, B)
            stats(ve, 0)

            def norm_x(b, p):
                need(ve, xt_done, b - 1)
                nc.vector.tensor_scalar(xn[p][:, :], xall[:, bass.ds(b, 1), :].rearrange("p a n -> p (a n)"),
                                        mean[:, bass.ds(b, 1)], rstd[:, bass.ds(b, 1)],
                                        ALU.subtract, ALU.mult).then_inc(xn_ok, 1)

            ve.wait_ge(rs_ok, 2)
            ve.wait_ge(woT_ok, 2)
            norm_x(0, 0)
            norm_x(1, 1)
            with ve.Fori(1, B // 2) as i:
                norm_x(2 * i, 0)
                norm_x(2 * i + 1, 1)

            def q_rest(g, o):
                ve.wait_ge(q1_ok, 2 * g + o + 1)
                need(ve, q3_ok, 2 * g - 1 + o)
                nc.vector.tensor_tensor(qr[o][:, :], (b0, b1)[o][:, 0:GT], qp[o][:, 0, :], ALU.subtract).then_inc(qr_ok, 1)

            for o in range(2):
                q_rest(0, o)
            with ve.Fori(1, G) as g:
                for o in range(2):
                    q_rest(g, o)

            def maxima(b, hh, heads=range(HH)):
                for h in heads:
                    ve.wait_ge(smax, 16 * b + hh * HH + h + 1)
                    if h == 0:
                        need(ve, mp_ok, 2 * b + hh)
                    hd = hh * HH + h
                    nc.vector.tensor_reduce(negmax[:, hd:hd + 1], (b4, b5)[h % 2][0:S, 0:NK], AX.X, ALU.max,
                                            negate=True).then_inc(red, 1)

            def split_max(b, hh):
                own = slice(hh * HH, (hh + 1) * HH)
                ve.wait_ge(red, 16 * b + (hh + 1) * HH)
                need(ve, mt_done, 2 * b + hh - 1)
                nc.vector.tensor_copy(mparts[:, own, 0], negmax[:, own]).then_inc(mp1, 1)
                ve.wait_ge(mp1, 2 * b + hh + 1)
                nc.vector.tensor_tensor(mparts[:, own, 1], negmax[:, own], mparts[:, own, 0], ALU.subtract)\
                    .then_inc(mp_ok, 1)

            def turn_out(b):
                ve.wait_ge(pv_done, 2 * b + 2)
                need(ve, scaled_ok, b)
                nc.vector.transpose(turned[:, :, :].rearrange("p a n -> p (a n)"), b6[:, 0:4 * S]).then_inc(turned_ok, 1)
                ve.wait_ge(turned_ok, b + 1)
                nc.vector.reciprocal(rec[:, :], turned[:, :, HD]).then_inc(rec_ok, 1)

            def turn_back(b):
                ve.wait_ge(scaled_ok, b + 1)
                need(ve, wo_done, b)
                nc.vector.transpose(att[:, :], scaled[:, :, :].rearrange("p a n -> p (a n)")).then_inc(att_ok, 1)

            def add_attention(b):
                ve.wait_ge(wo_done, b + 1)
                xb = xall[:, bass.ds(b, 1), :].rearrange("p a n -> p (a n)")
                nc.vector.scalar_tensor_tensor(out=xb, in0=b7[0:S, 0:D], scalar=tanhs[0:S, 0:1], in1=xb,
                                               op0=ALU.mult, op1=ALU.add).then_inc(x2_ok, 1)
                ve.wait_ge(x2_ok, b + 1)
                nc.vector.bn_stats(st[:, bass.ds(b, 1), :].rearrange("p a n -> p (a n)"), xb).then_inc(st_ok, 1)

            def batch(b, first=False, last=False):
                if not last:
                    maxima(b + 1, 0)
                    split_max(b + 1, 0)
                if not first:
                    turn_out(b - 1)
                if not last:
                    maxima(b + 1, 1, range(4))
                if not first:
                    turn_back(b - 1)
                if not last:
                    maxima(b + 1, 1, range(4, HH))
                    split_max(b + 1, 1)
                if not first:
                    add_attention(b - 1)

            nc.vector.memset(b6, 0.0).then_inc(ones_v, 1)
            ve.wait_ge(ones_v, 3)
            maxima(0, 0)
            split_max(0, 0)
            maxima(0, 1)
            split_max(0, 1)
            ve.wait_ge(xb_ok, 1)
            batch(0, first=True)
            batch(1)
            with ve.Fori(1, B // 2 - 1) as i:
                batch(2 * i)
                batch(2 * i + 1)
            batch(B - 2)
            batch(B - 1, last=True)
            turn_out(B - 1)
            turn_back(B - 1)
            add_attention(B - 1)

            def normalise(g):
                need(ve, base_ok, g)
                for i in range(GB):
                    b = bass.ds(GB * g + i, 1)
                    nc.vector.tensor_scalar(xn2[:, i, :], xall[:, b, :].rearrange("p a n -> p (a n)"), mean[:, b], rstd[:, b],
                                            ALU.subtract, ALU.mult).then_inc(xn2_ok, 1)
                need(ve, xft_done, 2 * g)
                for i in range(GB):
                    ve.wait_ge(xn2_ok, GB * g + i + 1)
                    nc.vector.scalar_tensor_tensor(out=xf[:, i, :], in0=xn2[:, i, :], scalar=rstd2[:, bass.ds(GB * g + i, 1)],
                                                   in1=lnw[:, :], op0=ALU.mult, op1=ALU.mult).then_inc(xf_ok, 1)

            def put_xf(g):
                ve.wait_ge(xft_done, 2 * g + 2)
                nc.vector.tensor_copy(xfT[:, 1, bass.ds(GT * g, GT)], b1[:, 0:GT]).then_inc(xft_v, 1)

            def put_logits(g):
                ve.wait_ge(lgT_done, g + 1)
                nc.vector.tensor_copy(lgT[:, :], b2[0:E, 0:GT]).then_inc(lgT_ok, 1)

            def router(g):
                n = ROUTER_STEPS * g
                ve.wait_ge(lg_done, g + 1)
                nc.vector.tensor_copy(lg[:, :, :].rearrange("p b e -> p (b e)"), b2[0:S, GT:GT + GB * E]).then_inc(rt, 1)
                ve.wait_ge(rt, n + 1)
                nc.vector.tensor_reduce(top[:, :], lg[:, :, :], AX.X, ALU.max).then_inc(rt, 1)
                ve.wait_ge(rt, n + 2)
                nc.vector.tensor_tensor(eq[:, :, :], lg[:, :, :], top[:, :, None].broadcast_to([S, GB, E]), ALU.is_equal)\
                    .then_inc(rt, 1)
                ve.wait_ge(rt, n + 3)
                nc.vector.scalar_tensor_tensor(out=eq[:, :, :], in0=eq[:, :, :], scalar=-float(E),
                                               in1=iota_e[:, None, :].broadcast_to([S, GB, E]),
                                               op0=ALU.mult, op1=ALU.add).then_inc(rt, 1)
                ve.wait_ge(rt, n + 4)
                nc.vector.tensor_reduce(pick[:, :], eq[:, :, :], AX.X, ALU.min).then_inc(rt, 1)
                ve.wait_ge(rt, n + 5)
                nc.vector.scalar_tensor_tensor(out=hot[:, bass.ds(GB * g, GB), :],
                                               in0=iota_e[:, None, :].broadcast_to([S, GB, E]), scalar=-float(E),
                                               in1=pick[:, :, None].broadcast_to([S, GB, E]),
                                               op0=ALU.add, op1=ALU.is_equal).then_inc(rt, 1)
                for i in range(GB):
                    ve.wait_ge(rt, n + 6 + i)
                    b = GB * g + i
                    nc.vector.tensor_tensor(before[:, bass.ds(b + 1, 1), :], before[:, bass.ds(b, 1), :],
                                            hot[:, bass.ds(b, 1), :], ALU.add).then_inc(rt, 1)
                ve.wait_ge(tanh_top, g + 1)
                nc.vector.tensor_scalar(score[:, :], score[:, :], 0.5, 0.5, ALU.mult, ALU.add).then_inc(score_ok, 1)
                ve.wait_ge(score_ok, g + 1)
                ve.wait_ge(xfb_ok, g + 1)
                for i in range(GB):
                    nc.vector.tensor_scalar(xe[:, bass.ds(GB * g + i, 1), 0:D].rearrange("p a n -> p (a n)"), xf[:, i, :],
                                            score[:, i:i + 1], None, ALU.mult).then_inc(xe_ok, 1)

            def hidden(g, f):
                n = FC * g + f
                ve.wait_ge(silu_ok, n + 1)
                ve.wait_ge(u_done, n + 1)
                if f == 0:
                    need(ve, dn_done, 2 * g)
                nc.vector.tensor_tensor(hT[:, f, :], silu[f % 2][:, :], (b4, b6)[f % 2][:, 0:GT], ALU.mult).then_inc(h_ok, 1)

            def add_shared(g):
                for j in range(2):
                    ve.wait_ge(dn_done, 2 * g + j + 1)
                    if j == 0:
                        ve.wait_ge(base_ok, g + 1)
                    xb = xall[:, bass.ds(GB * g + 2 * j, 2), :]
                    nc.vector.scalar_tensor_tensor(out=xb, in0=(b7, b0)[j][0:S, :].rearrange("p (a n) -> p a n", a=2),
                                                   scalar=tanhs[0:S, 1:2], in1=xb, op0=ALU.mult, op1=ALU.add)\
                        .then_inc(y_ok, 1)

            def tiles_and_places():
                ve.wait_ge(rank_done, 1)
                nc.vector.tensor_copy(tot[:, :], b7[:, B * E:(B + 1) * E]).then_inc(rk, 1)
                ve.wait_ge(rk, 1)
                by_expert = passed[:, :].rearrange("p (e t) -> p e t", e=E)
                nc.vector.tensor_tensor(by_expert, tot[:, :, None].broadcast_to([P, E, TILES]),
                                        start_t[:, None, :].broadcast_to([P, E, TILES]), ALU.is_gt).then_inc(rk, 1)
                ve.wait_ge(rk, 2)
                nc.vector.tensor_reduce(ntile[:, :], by_expert, AX.X, ALU.add).then_inc(rk, 1)
                ve.wait_ge(rk, 3)
                nc.vector.tensor_copy(upto[:, 0:1], ntile[:, 0:1]).then_inc(rk, 1)
                for e in range(1, E):
                    ve.wait_ge(rk, 3 + e)
                    nc.vector.tensor_tensor(upto[:, e:e + 1], upto[:, e - 1:e], ntile[:, e:e + 1], ALU.add).then_inc(rk, 1)
                ve.wait_ge(rk, 11)
                nc.vector.tensor_tensor(first_row[:, :], upto[:, :], ntile[:, :], ALU.subtract).then_inc(rk, 1)
                by_tile = passed[:, :].rearrange("p (t e) -> p t e", e=E)
                nc.vector.tensor_tensor(by_tile, iota_t[:, :, None].broadcast_to([P, TILES, E]),
                                        upto[:, None, :].broadcast_to([P, TILES, E]), ALU.is_ge).then_inc(rk, 1)
                ve.wait_ge(rk, 12)
                nc.vector.scalar_tensor_tensor(out=rank[:, :, :], in0=first_row[0:S, None, :].broadcast_to([S, B, E]),
                                               scalar=float(P), in1=b7[0:S, 0:B * E].rearrange("p (b e) -> p b e", e=E),
                                               op0=ALU.mult, op1=ALU.add).then_inc(rk, 1)
                ve.wait_ge(rk, 14)
                nc.vector.tensor_tensor(rank[:, :, :], rank[:, :, :], hot[:, :, :], ALU.mult).then_inc(rk, 1)
                nc.vector.tensor_reduce(texp[:, :], by_tile, AX.X, ALU.add).then_inc(rk, 1)
                ve.wait_ge(rk, 16)
                nc.vector.tensor_reduce(pos[:, :], rank[:, :, :], AX.X, ALU.add).then_inc(rk, 1)
                nc.vector.tensor_scalar(texp_i[:, :], texp[:, :], float(E - 1), None, ALU.min).then_inc(rk, 1)
                ve.wait_ge(rk, 17)
                nc.vector.tensor_copy(pos_i[:, :], pos[:, :]).then_inc(rk, 1)

            def group(g, last=False):
                hidden(g, 0)
                router(g)
                hidden(g, 1)
                if not last:
                    normalise(g + 1)
                hidden(g, 2)
                if last:
                    tiles_and_places()
                hidden(g, 3)
                if not last:
                    put_xf(g + 1)
                add_shared(g)
                if not last:
                    put_logits(g + 1)

            nc.vector.memset(before[:, 0, :], 0.0).then_inc(s2_init, 1)
            ve.wait_ge(st_ok, 2 * B)
            stats(ve, STATS_STEPS)
            ve.wait_ge(rs_ok, 8)
            ve.wait_ge(small_in, 80)
            ve.wait_ge(const_ok, 4)
            ve.wait_ge(s2_init, 1)
            normalise(0)
            put_xf(0)
            put_logits(0)
            group(0)
            with ve.Fori(1, G - 1) as g:
                group(g)
            group(G - 1, last=True)

            def hidden_rows(t):
                ve.wait_ge(gact_ok, t + 1)
                ve.wait_ge(ut_done, t + 1)
                need(ve, ht_done, t)
                nc.vector.tensor_tensor(hrow[:, :], gact[:, :], b4, ALU.mult).then_inc(hrow_ok, 1)

            def put_hidden(t):
                ve.wait_ge(ht_done, t + 1)
                need(ve, dt_done, t)
                nc.vector.tensor_copy(hrT[:, :, :].rearrange("p f n -> p (f n)"), b1).then_inc(hrt_ok, 1)

            def finish_rows(t, p, i):
                ve.wait_ge(dt_done, t + 1)
                ve.wait_ge(resid_in[p], 16 * i + 16)
                need(ve, out_done[p], 16 * i)
                nc.vector.scalar_tensor_tensor(out=orow[p][:, :], in0=b7[:, 0:D], scalar=tanhs[:, 1:2], in1=resid[p][:, :],
                                               op0=ALU.mult, op1=ALU.add).then_inc(orow_ok, 1)

            def tile(t, p, i):
                put_hidden(t - 1)
                hidden_rows(t)
                finish_rows(t - 1, 1 - p, i)

            hidden_rows(0)
            tile(1, 1, 0)
            tile(2, 0, 0)
            with ve.Fori(1, TILES // 2) as i:
                tile(2 * i + 1, 1, i)
                tile(2 * i + 2, 0, i)
            put_hidden(TILES - 1)
            finish_rows(TILES - 1, 0, TILES // 2)

        @block.gpsimd
        def _(pool):
            nc.gpsimd.memset(ident[:, :], 0.0).then_inc(ident_z, 1)
            pool.wait_ge(ident_z, 1)
            nc.gpsimd.affine_select(out=ident[:, :], in_=ident[:, :], compare_op=ALU.not_equal, fill=1.0, base=0,
                                    pattern=[[-1, P]], channel_multiplier=1).then_inc(ident_ok, 1)
            nc.gpsimd.memset(woX[:, :, :, :, :, :], 0.0).then_inc(fill_ok, 1)
            nc.gpsimd.memset(zrow[:, 0:D], 0.0).then_inc(fill_ok, 1)
            nc.gpsimd.memset(zrow[:, D:XROW].bitcast(I32), NOBODY).then_inc(fill_ok, 1)
            nc.gpsimd.memset(mhalf[:, :], -0.5).then_inc(fill_ok, 1)
            nc.gpsimd.memset(ones[:, :], 1.0).then_inc(fill_ok, 1)
            pool.wait_ge(fill_ok, 5)
            nc.gpsimd.affine_select(out=lower[:, :], in_=ones[:, 0:S], compare_op=ALU.is_gt, fill=0.0, base=0,
                                    pattern=[[1, S]], channel_multiplier=-1).then_inc(const_ok, 1)
            for dst, first, step, n in ((iota_e, E, 1, E), (iota_t, 0, 1, TILES), (start_t, 0, P, TILES)):
                nc.gpsimd.iota(dst[:, :], pattern=[[step, n]], base=first, channel_multiplier=0,
                               allow_small_or_imprecise_dtypes=True).then_inc(const_ok, 1)

            def parts_batch(b, p, i):
                pool.wait_ge(k2_ok, b + 1)
                nc.gpsimd.tensor_tensor(kp[p][:, :, 2, :], kr[p][:, :, :], kp[p][:, :, 1, :], ALU.subtract)\
                    .then_inc(k3_ok, 1)

            parts_batch(0, 0, 0)
            parts_batch(1, 1, 0)
            with pool.Fori(1, B // 2) as i:
                parts_batch(2 * i, 0, i)
                parts_batch(2 * i + 1, 1, i)

            pool.wait_ge(lnv, STATS_STEPS)
            pool.wait_ge(fill_ok, 4)
            nc.gpsimd.tensor_scalar(tmp[:, :], var[:, :], EPS, 1.0, ALU.add, ALU.mult).then_inc(rs_ok, 1)
            pool.wait_ge(rs_ok, 1)
            nc.gpsimd.tensor_tensor(rstd[:, :], tmp[:, :], mhalf[:, :], ALU.pow).then_inc(rs_ok, 1)

            def q_parts(g, o):
                pool.wait_ge(q2_ok, 2 * g + o + 1)
                nc.gpsimd.tensor_tensor(qp[o][:, 2, :], qr[o][:, :], qp[o][:, 1, :], ALU.subtract).then_inc(q3_ok, 1)

            for o in range(2):
                q_parts(0, o)
            with pool.Fori(1, G) as g:
                for o in range(2):
                    q_parts(g, o)

            for p in range(2):
                pool.wait_ge(q_out[p], 16 * NPAIR * G)
                pool.wait_ge(k_out[p], 16 * B // 2)
                pool.wait_ge(v_out[p], 16 * B // 2)
            pool.wait_ge(zero_out, 16 * TILES)
            for p in range(2):
                nc.gpsimd.memset(kst[p][ROWS:STACK, :], 1.0).then_inc(ones_k, 1)
                nc.gpsimd.memset(kst[p][0:ROWS, H * NK:H * NK + 16], 0.0).then_inc(ones_k, 1)
            pool.wait_ge(ones_k, 4)
            pool.wait_ge(tanh_ok, 1)
            nc.gpsimd.tensor_scalar(bo_b[:, :], bo_b[:, :], tanhs[0:S, 0:1], 0.0, ALU.mult, ALU.add).then_inc(tb_ok, 1)
            pool.wait_ge(tb_ok, 1)
            pool.wait_ge(xn_ok, B)
            nc.gpsimd.tensor_tensor(xall[:, :, :], xall[:, :, :], bo_b[:, None, :].broadcast_to([S, B, D]),
                                    ALU.add).then_inc(xb_ok, 1)

            def scale_out(b):
                pool.wait_ge(rec_ok, b + 1)
                need(pool, att_ok, b)
                nc.gpsimd.tensor_tensor(scaled[:, :, :], turned[:, :, :], rec[:, :, None].broadcast_to([P, NB, 32]),
                                        ALU.mult).then_inc(scaled_ok, 1)

            scale_out(0)
            with pool.Fori(1, B) as b:
                scale_out(b)

            pool.wait_ge(x2_ok, B)
            nc.gpsimd.iota(xe[:, :, D].bitcast(I32), pattern=[[S, B]], base=0, channel_multiplier=1).then_inc(s2_fill, 1)
            for p in range(2):
                nc.gpsimd.memset(resid[p][:, :], 0.0).then_inc(s2_fill, 1)
            pool.wait_ge(lnv, 2 * STATS_STEPS)

            def step(n, out_, a, b_, op):
                pool.wait_ge(rs_ok, n)
                nc.gpsimd.tensor_tensor(out_[:, :], a[:, :], b_[:, :], op).then_inc(rs_ok, 1)

            def plus_eps(src):
                nc.gpsimd.tensor_scalar(tmp[:, :], src[:, :], EPS, 1.0, ALU.add, ALU.mult).then_inc(rs_ok, 1)

            plus_eps(var)
            step(3, rstd, tmp, mhalf, ALU.pow)
            step(4, tmp, var, rstd, ALU.mult)
            step(5, tmp, tmp, rstd, ALU.mult)
            pool.wait_ge(rs_ok, 6)
            plus_eps(tmp)
            step(7, rstd2, tmp, mhalf, ALU.pow)

            with pool.Fori(0, G) as g:
                pool.wait_ge(xf_ok, GB * g + GB)
                nc.gpsimd.tensor_tensor(xf[:, :, :], xf[:, :, :], lnb[:, None, :].broadcast_to([S, GB, D]), ALU.add)\
                    .then_inc(xfb_ok, 1)
                nc.gpsimd.tensor_scalar(xn2[:, :, :], xn2[:, :, :], tanhs[0:S, 1:2], 0.0, ALU.mult, ALU.add)\
                    .then_inc(xn2_scaled, 1)
                pool.wait_ge(xn2_scaled, g + 1)
                xg = xall[:, bass.ds(GB * g, GB), :]
                nc.gpsimd.tensor_tensor(xg, xg, xn2[:, :, :], ALU.add).then_inc(base_ok, 1)

            pool.wait_ge(rk, RANK_STEPS)
            pool.wait_ge(xe_ok, B)
            pool.wait_ge(s2_fill, 3)
            for b in range(B):
                nc.gpsimd.indirect_dma_start(out=xs_dram[:, :], out_offset=bass.IndirectOffsetOnAxis(ap=pos_i[:, b:b + 1], axis=0),
                                             in_=xe[:, b, :], in_offset=None).then_inc(scat, 16)

            def fetch(t):
                p, i = t % 2, t // 2
                pool.wait_ge(xs_in[p], 16 * i + 16)
                need(pool, out_done[p], 16 * i)
                nc.gpsimd.tensor_copy(who[p][:, :], xs[p][:, D:XROW].bitcast(U32)).then_inc(who_ok, 1)
                pool.wait_ge(who_ok, t + 1)
                need(pool, orow_ok, t - 1)
                nc.gpsimd.indirect_dma_start(out=resid[p][:, :], out_offset=None, in_=resid_dram[:, :],
                                             in_offset=bass.IndirectOffsetOnAxis(ap=who[p][:, 0:1], axis=0),
                                             bounds_check=T - 1, oob_is_err=False).then_inc(resid_in[p], 16)

            def store(t):
                p = t % 2
                pool.wait_ge(orow_ok, t + 1)
                nc.gpsimd.indirect_dma_start(out=out.rearrange("b s d -> (b s) d"),
                                             out_offset=bass.IndirectOffsetOnAxis(ap=who[p][:, 0:1], axis=0),
                                             in_=orow[p][:, :], in_offset=None,
                                             bounds_check=T - 1, oob_is_err=False).then_inc(out_done[p], 16)

            pool.wait_ge(resid_out, 16 * G)
            for t in range(TILES):
                fetch(t)
                if t > 0:
                    store(t - 1)
            store(TILES - 1)
            pool.wait_ge(out_done[0], 16 * (TILES // 2 + 1))
            pool.wait_ge(out_done[1], 16 * (TILES // 2))


_OUTS = [((B, S, D), "float32")]


def kernel(**inputs):
    import numpy as _np
    import concourse.bacc as _bacc
    from concourse.bass_utils import run_bass_kernel_spmd as _run

    nc = _bacc.Bacc("TRN2", target_bir_lowering=False, num_devices=1)
    names = ["x", "ctx_1024", "g_xattn", "g_ffn", "L0_xattn_Wq", "L0_xattn_Wk", "L0_xattn_Wv", "L0_xattn_Wo",
             "L0_xattn_bo", "L0_ffn_ln_w", "L0_ffn_ln_b", "L0_ffn_router_w", "L0_ffn_gate_w", "L0_ffn_up_w",
             "L0_ffn_down_w", "L0_ffn_sh_gate", "L0_ffn_sh_up", "L0_ffn_sh_down"]
    arrays, args = {}, []
    for name in names:
        a = _np.ascontiguousarray(inputs[name])
        arrays[f"in_{name}"] = a
        args.append(nc.dram_tensor(f"in_{name}", a.shape, mybir.dt.from_np(a.dtype), kind="ExternalInput").ap())
    shape, dtype = _OUTS[0]
    args.append(nc.dram_tensor("out_0", shape, mybir.dt.from_np(_np.dtype(dtype)), kind="ExternalOutput").ap())
    build(nc, *args)
    r = _run(nc, [arrays], core_ids=[0])
    return r.results[0]["out_0"]
```

```python
from contextlib import ExitStack

import concourse.bass as bass
from concourse import mybir

F32 = mybir.dt.float32
BF16 = mybir.dt.bfloat16
I32 = mybir.dt.int32
U32 = mybir.dt.uint32
ALU = mybir.AluOpType
ACT = mybir.ActivationFunctionType
AX = mybir.AxisListType

B, S, D = 16, 112, 256
NK = 375
H, HD = 16, 16
E, FF = 8, 512
EPS = 1e-5
P = 128
T = B * S
KC = D // P
FC = FF // P
KEY_CHUNKS = [(0, 128), (128, 128), (256, NK - 256)]
HH = H // 2
PARTS = 3
K_PARTS = [0, 1, 2, 0, 1, 0]
Q_PARTS = [0, 0, 0, 1, 1, 2]
NPAIR = len(K_PARTS)
ROWS = NPAIR * HD
SHIFT_ROWS = 2
STACK = ROWS + SHIFT_ROWS
VW = HD + 1
HQ = HH * S
NB = 4 * S // 32
G, GB = 4, 4
GT = GB * S
TILES = (T + E * (P - 1)) // P
XROW = D + 1
NOBODY = 1 << 20


def build(nc, x, ctx, g_xattn, g_ffn, Wq, Wk, Wv, Wo, bo, ln_w, ln_b, router_w, gate_w, up_w, down_w,
          sh_gate, sh_up, sh_down, out):
    stack = ExitStack()
    with stack:
        def sem(name):
            return stack.enter_context(nc.semaphore(name))

        def sb(name, shape, dt=F32, scope=stack):
            return scope.enter_context(nc.sbuf_tensor(name, shape, dt))

        def bank(name, n=1):
            return stack.enter_context(nc.psum_tensor(name, [P, n * 512], F32))

        def need(eng, s, count):
            if not (isinstance(count, int) and count <= 0):
                eng.wait_ge(s, count)

        k_dram = nc.dram_tensor("k_parts_dram", [B, 2, PARTS, HD, HH, NK], BF16).ap()
        q_dram = nc.dram_tensor("q_parts_dram", [2, NPAIR, HD, HH, T], BF16).ap()
        xs_dram = nc.dram_tensor("sorted_rows_dram", [TILES * P, XROW], F32).ap()
        resid_dram = nc.dram_tensor("resid_dram", [T, D], F32).ap()

        ident = sb("ident", [P, P])
        identb = sb("identb", [P, P], BF16)
        woT = sb("woT", [P, 4, D])
        xall = sb("xall", [S, B, D])
        eu = sb("eu", [P, E, KC, FF])
        ed = sb("ed", [P, E, FC, D])
        sg = sb("sg", [P, KC, FF])
        su = sb("su", [P, KC, FF])
        sd = sb("sd", [P, FC, D])
        rw = sb("rw", [P, KC, E])
        lnw = sb("lnw", [S, D])
        lnb = sb("lnb", [S, D])
        bo_b = sb("bo_b", [S, D])
        gates = sb("gates", [P, 2])
        tanhs = sb("tanhs", [P, 2])
        st = sb("st", [S, B, 6])
        mean = sb("mean", [S, B])
        var = sb("var", [S, B])
        tmp = sb("tmp", [S, B])
        rstd = sb("rstd", [S, B])
        rstd2 = sb("rstd2", [S, B])
        mhalf = sb("mhalf", [S, B])
        negmax = sb("negmax", [S, H])
        mparts = sb("mparts", [S, H, SHIFT_ROWS], BF16)

        lower = sb("lower", [S, S])
        ones = sb("ones", [S, P])
        iota_e = sb("iota_e", [S, E])
        iota_t = sb("iota_t", [P, TILES])
        start_t = sb("start_t", [P, TILES])

        raw = ExitStack()
        wraw = sb("wraw", [P, 4, KC, D], scope=raw)
        raw.close()
        xn2 = sb("xn2", [S, GB, D])
        xf = sb("xf", [S, GB, D])

        s1 = ExitStack()
        cin = [sb(f"cin{p}", [P, 3, D], scope=s1) for p in range(2)]
        ctxT = [sb(f"ctxT{p}", [P, KC, NK + 1], scope=s1) for p in range(2)]
        kp = sb("kp", [P, 2, PARTS, NK], BF16, scope=s1)
        kr = sb("kr", [P, 2, NK], scope=s1)
        vst = [sb(f"vst{p}", [P, 3, H, VW], scope=s1) for p in range(2)]
        wkT = sb("wkT", [P, KC, D], scope=s1)
        wvT = sb("wvT", [P, KC, D], scope=s1)
        zrow = sb("zrow", [P, XROW], scope=s1)
        kst = [sb(f"kst{p}", [STACK, H * NK + 16], BF16, scope=s1) for p in range(2)]
        qst = [sb(f"qst{p}", [STACK, H * S], BF16, scope=s1) for p in range(2)]
        s0 = ExitStack()
        wqT = sb("wqT", [P, KC, D], scope=s0)
        woX = sb("woX", [P, KC, 4, 4, 2, HD], scope=s0)
        xn = sb("xn", [S, GB, D], scope=s0)
        xnT = [sb(f"xnT{p}", [P, KC, GT], scope=s0) for p in range(2)]
        qp = [[sb(f"qp{p}{o}", [P, PARTS, GT], BF16, scope=s0) for o in range(2)] for p in range(2)]
        qr = [sb(f"qr{p}", [P, GT], scope=s0) for p in range(2)]
        s0.close()
        pT = [sb(f"pT{hh}", [P, 3, HQ], scope=s1) for hh in range(2)]
        turned = sb("turned", [P, NB, 32], scope=s1)
        rec = sb("rec", [P, NB], scope=s1)
        scaled = sb("scaled", [P, NB, 32], scope=s1)
        att = sb("att", [P, 4 * S], scope=s1)
        s1.close()

        s2 = ExitStack()
        eg = sb("eg", [P, E, KC, FF], scope=s2)
        xfT = sb("xfT", [P, KC, T], scope=s2)
        xe = sb("xe", [S, B, XROW], scope=s2)
        silu = [sb(f"silu{p}", [P, GT], scope=s2) for p in range(2)]
        hT = sb("hT", [P, FC, GT], scope=s2)
        lgT = sb("lgT", [E, GT], scope=s2)
        lg = sb("lg", [S, GB, E], scope=s2)
        top = sb("top", [S, GB], scope=s2)
        score = sb("score", [S, GB], scope=s2)
        eq = sb("eq", [S, GB, E], scope=s2)
        pick = sb("pick", [S, GB], scope=s2)
        hot = sb("hot", [S, B, E], scope=s2)
        before = sb("before", [S, B + 1, E], scope=s2)
        tot = sb("tot", [P, E], scope=s2)
        tot_i = sb("tot_i", [P, E], I32, scope=s2)
        ntile = sb("ntile", [P, E], scope=s2)
        upto = sb("upto", [P, E], scope=s2)
        first_row = sb("first_row", [P, E], scope=s2)
        passed = sb("passed", [P, TILES * E], scope=s2)
        texp = sb("texp", [P, TILES], scope=s2)
        texp_i = sb("texp_i", [P, TILES], I32, scope=s2)
        rank = sb("rank", [S, B, E], scope=s2)
        pos = sb("pos", [S, B], scope=s2)
        pos_i = sb("pos_i", [S, B], U32, scope=s2)
        xs = [sb(f"xs{p}", [P, XROW], scope=s2) for p in range(2)]
        who = [sb(f"who{p}", [P, 1], U32, scope=s2) for p in range(2)]
        xsT = sb("xsT", [P, KC, P], scope=s2)
        gact = sb("gact", [P, FF], scope=s2)
        hrow = sb("hrow", [P, FF], scope=s2)
        hrT = sb("hrT", [P, FC, P], scope=s2)
        resid = [sb(f"resid{p}", [P, D], scope=s2) for p in range(2)]
        orow = [sb(f"orow{p}", [P, D], scope=s2) for p in range(2)]
        s2.close()

        pair = bank("pair", 2)
        single = [bank(f"single{n}") for n in range(2, 8)]
        b0, b1 = pair[:, 0:512], pair[:, 512:1024]
        b2, b3, b4, b5, b6, b7 = (s[:, :] for s in single)

        ident_z, ident_ok, identb_ok = sem("ident_z"), sem("ident_ok"), sem("identb_ok")
        fill_ok = sem("fill_ok")
        wk_in, wv_in = sem("wk_in"), sem("wv_in")
        w2_in = sem("w2_in")
        x_in, small_in, sh_in = sem("x_in"), sem("small_in"), sem("sh_in")
        exp_in = sem("exp_in")
        zero_out = sem("zero_out")
        ones_v, turn_base = sem("ones_v"), sem("turn_base")
        wox_ok = sem("wox_ok")
        wT_done, wT_ok = sem("wT_done"), sem("wT_ok")
        woT_done, woT_ok = sem("woT_done"), sem("woT_ok")
        st_ok = sem("st_ok")
        lnv = sem("lnv")
        rs_ok = sem("rs_ok")
        xn_ok, xt_done = sem("xn_ok"), sem("xt_done")
        xt_a, xt_v = sem("xt_a"), sem("xt_v")
        qmm, q1_ok, qr_ok, q2_ok, q3_ok = sem("qmm"), sem("q1_ok"), sem("qr_ok"), sem("q2_ok"), sem("q3_ok")
        q_out = [[sem(f"q_out{p}{o}") for o in range(2)] for p in range(2)]
        tanh_ok, tb_ok, xb_ok = sem("tanh_ok"), sem("tb_ok"), sem("xb_ok")
        cin_in = [sem(f"cin_in{p}") for p in range(2)]
        ct_done = sem("ct_done")
        ct_a, ct_v = sem("ct_a"), sem("ct_v")
        kmm, vmm = sem("kmm"), sem("vmm")
        k1_ok, kr_ok, k2_ok, k3_ok = sem("k1_ok"), sem("kr_ok"), sem("k2_ok"), sem("k3_ok")
        v_a, v_v = sem("v_a"), sem("v_v")
        k_out = [sem(f"k_out{o}") for o in range(2)]
        k_in = [[sem(f"k_in{p}{hh}") for hh in range(2)] for p in range(2)]
        ones_k = sem("ones_k")
        smax, red = sem("smax"), sem("red")
        mp1, mp_ok = sem("mp1"), sem("mp_ok")
        mt_done, mt_ok = sem("mt_done"), sem("mt_ok")
        sc_done, exp_ok, pv_done = sem("sc_done"), sem("exp_ok"), sem("pv_done")
        turned_ok, rec_ok, scaled_ok, att_ok = sem("turned_ok"), sem("rec_ok"), sem("scaled_ok"), sem("att_ok")
        wo_done, x2_ok = sem("wo_done"), sem("x2_ok")
        const_ok, s2_init, s2_fill = sem("const_ok"), sem("s2_init"), sem("s2_fill")
        xn2_ok, xf_ok, xfb_ok = sem("xn2_ok"), sem("xf_ok"), sem("xfb_ok")
        xn2_scaled, base_ok = sem("xn2_scaled"), sem("base_ok")
        xft_done, xft_a, xft_v = sem("xft_done"), sem("xft_a"), sem("xft_v")
        lgT_done, lgT_ok, lg_done = sem("lgT_done"), sem("lgT_ok"), sem("lg_done")
        rt = sem("rt")
        tanh_top, score_ok, xe_ok = sem("tanh_top"), sem("score_ok"), sem("xe_ok")
        g_done, u_done, silu_ok, h_ok = sem("g_done"), sem("u_done"), sem("silu_ok"), sem("h_ok")
        dn_done, y_ok, resid_out = sem("dn_done"), sem("y_ok"), sem("resid_out")
        rank_done, rk = sem("rank_done"), sem("rk")
        scat = sem("scat")
        xs_in = [sem(f"xs_in{p}") for p in range(2)]
        who_ok = sem("who_ok")
        resid_in = [sem(f"resid_in{p}") for p in range(2)]
        xst_done, xst_ok = sem("xst_done"), sem("xst_ok")
        gt_done, ut_done, gact_ok, hrow_ok = sem("gt_done"), sem("ut_done"), sem("gact_ok"), sem("hrow_ok")
        ht_done, hrt_ok, dt_done, orow_ok = sem("ht_done"), sem("hrt_ok"), sem("dt_done"), sem("orow_ok")
        out_done = [sem(f"out_done{p}") for p in range(2)]
        ROUTER_STEPS = 6 + GB
        RANK_STEPS = 19

        def stats(ve, first, cols=slice(0, B)):
            me, mo = st[:, cols, 1], st[:, cols, 4]
            ve_, vo = st[:, cols, 2], st[:, cols, 5]
            nc.vector.tensor_tensor(mean[:, cols], me, mo, ALU.add).then_inc(lnv, 1)
            nc.vector.tensor_tensor(tmp[:, cols], me, mo, ALU.subtract).then_inc(lnv, 1)
            nc.vector.tensor_tensor(var[:, cols], ve_, vo, ALU.add).then_inc(lnv, 1)
            ve.wait_ge(lnv, first + 3)
            nc.vector.tensor_scalar(mean[:, cols], mean[:, cols], 0.5, None, ALU.mult).then_inc(lnv, 1)
            nc.vector.tensor_tensor(tmp[:, cols], tmp[:, cols], tmp[:, cols], ALU.mult).then_inc(lnv, 1)
            nc.vector.tensor_scalar(var[:, cols], var[:, cols], 1.0 / D, None, ALU.mult).then_inc(lnv, 1)
            ve.wait_ge(lnv, first + 6)
            nc.vector.scalar_tensor_tensor(out=var[:, cols], in0=tmp[:, cols], scalar=0.25, in1=var[:, cols],
                                           op0=ALU.mult, op1=ALU.add).then_inc(lnv, 1)

        STATS_STEPS = 7

        block = stack.enter_context(nc.Block())

        def exists(b):
            return not isinstance(b, int) or b < B

        @block.sync
        def _(sp):
            def load_ctx(b, p):
                src = ctx[bass.ds(b, 1)]
                sp.dma_start(cin[p][:, 0:2, :], src[:, 0:256, :].rearrange("a (c p) d -> p (a c) d", p=P))\
                    .then_inc(cin_in[p], 16)
                sp.dma_start(cin[p][0:NK - 256, 2, :], src[:, 256:NK, :].rearrange("a p d -> (a p) d"))\
                    .then_inc(cin_in[p], 16)

            def load_ctx_after(b, p):
                sp.wait_ge(ct_done, 2 * b - 2)
                load_ctx(b, p)

            def weight(dst, w):
                return sp.dma_start(dst, w.rearrange("(k p) d -> p k d", p=P))

            weight(wraw[:, 0], Wk).then_inc(wk_in, 16)
            load_ctx(0, 0)
            weight(wraw[:, 1], Wv).then_inc(wv_in, 16)
            sp.dma_start(xall[:, :, :], x.rearrange("b s d -> s b d")).then_inc(x_in, 16)
            load_ctx(1, 1)
            weight(wraw[:, 2], Wq).then_inc(w2_in, 16)
            weight(wraw[:, 3], Wo).then_inc(w2_in, 16)
            for dst, src in ((bo_b, bo), (lnw, ln_w), (lnb, ln_b)):
                sp.dma_start(dst[:, :], src.rearrange("(a d) -> a d", a=1).broadcast_to([S, D])).then_inc(small_in, 16)
            for n, gate in enumerate((g_xattn, g_ffn)):
                sp.dma_start(gates[:, n:n + 1], gate.rearrange("(a d) -> a d", a=1).broadcast_to([P, 1])).then_inc(small_in, 16)

            def store_keys(b, o):
                sp.wait_ge(k3_ok, 2 * b + o + 1)
                sp.dma_start(k_dram[bass.ds(b, 1), o].rearrange("a t d e k -> (d e) (a t) k"), kp[:, o, :, :])\
                    .then_inc(k_out[o], 16)

            def load_stack(b, p, hh):
                need(sp, sc_done, 6 * b - 12 + 3 * hh + 3)
                sp.wait_ge(k_out[hh], 16 * b + 16)
                src = k_dram[bass.ds(b, 1), hh]
                row = 0
                for n in (3, 2, 1):
                    sp.dma_start(kst[p][row:row + n * HD, hh * HH * NK:(hh + 1) * HH * NK],
                                 src[:, 0:n].rearrange("a t d e k -> (a t d) (e k)")).then_inc(k_in[p][hh], 16)
                    row += n * HD
                sp.dma_start(qst[p][0:ROWS, hh * HQ:(hh + 1) * HQ].rearrange("p (e q) -> p e q", q=S),
                             q_dram[hh, :, :, :, bass.ds(b * S, S)].rearrange("t d e q -> (t d) e q"))\
                    .then_inc(k_in[p][hh], 16)

            def store_queries(g):
                for o in range(2):
                    sp.wait_ge(q3_ok, 2 * g + o + 1)
                    for j, part in enumerate(Q_PARTS):
                        sp.dma_start(q_dram[o, j, :, :, g * GT:(g + 1) * GT].rearrange("d e q -> (d e) q"),
                                     qp[g % 2][o][:, part, :]).then_inc(q_out[g % 2][o], 16)

            for b in range(2):
                store_keys(b, 0)
                store_keys(b, 1)
                load_ctx_after(b + 2, b)
            store_queries(0)
            store_queries(1)
            for b in range(2):
                for o in range(2):
                    sp.wait_ge(q_out[0][o], 16 * NPAIR)
                    load_stack(b, b, o)
                store_queries(2 + b)
            for p in range(2):
                for o in range(2):
                    sp.wait_ge(q_out[p][o], 16 * NPAIR * G // 2)
            sp.wait_ge(fill_ok, 3)
            with sp.Fori(0, TILES) as t:
                sp.dma_start(xs_dram[bass.ds(t * P, P), :], zrow[:, :]).then_inc(zero_out, 16)

            def batch(b, p):
                if exists(b + 2):
                    store_keys(b + 2, 0)
                    store_keys(b + 2, 1)
                    load_stack(b + 2, p, 0)
                    load_stack(b + 2, p, 1)
                if exists(b + 4):
                    load_ctx_after(b + 4, p)

            def expert(e):
                for dst, w in ((eu, up_w), (ed, down_w)):
                    sp.dma_start(dst[:, bass.ds(e, 1), :, :],
                                 w[bass.ds(e, 1)].rearrange("e (k p) f -> p e k f", p=P)).then_inc(exp_in, 16)

            batch(0, 0)
            batch(1, 1)
            with sp.Fori(1, B // 2 - 2) as i:
                batch(2 * i, 0)
                expert(i - 1)
                batch(2 * i + 1, 1)
            for b in range(B - 4, B):
                batch(b, b % 2)
            for e in range(B // 2 - 3, E):
                expert(e)
            for dst, w in ((sg, sh_gate), (su, sh_up), (sd, sh_down), (rw, router_w)):
                weight(dst[:, :, :], w).then_inc(sh_in, 16)
            sp.wait_ge(x2_ok, B)
            sp.wait_ge(zero_out, 16 * TILES)
            with sp.Fori(0, E) as e:
                sp.dma_start(eg[:, bass.ds(e, 1), :, :],
                             gate_w[bass.ds(e, 1)].rearrange("e (k p) f -> p e k f", p=P)).then_inc(exp_in, 16)

            out_rows = resid_dram.rearrange("(b s) d -> s b d", s=S)
            for g in range(G):
                sp.wait_ge(y_ok, 2 * g + 2)
                sp.dma_start(out_rows[:, GB * g:GB * g + GB, :], xall[:, GB * g:GB * g + GB, :]).then_inc(resid_out, 16)

            def load_rows(t, p):
                need(sp, xst_done, t - 1)
                need(sp, who_ok, t - 1)
                sp.dma_start(xs[p][:, :], xs_dram[bass.ds(t * P, P), :]).then_inc(xs_in[p], 16)

            sp.wait_ge(scat, 16 * B)
            load_rows(0, 0)
            load_rows(1, 1)
            with sp.Fori(1, TILES // 2) as i:
                load_rows(2 * i, 0)
                load_rows(2 * i + 1, 1)
            load_rows(TILES - 1, 0)

        @block.tensor
        def _(pe):
            def tr(out_, in_, n):
                return nc.tensor.transpose(out_, in_, ident[0:n, 0:n])

            pe.wait_ge(ident_ok, 1)
            def turn_weight(n, out_bank):
                for k in range(KC):
                    for o in range(KC):
                        mm = tr(out_bank[:, k * D + o * P:k * D + (o + 1) * P], wraw[:, n, o, k * P:(k + 1) * P], P)
                mm.then_inc(wT_done, 1)

            pe.wait_ge(wk_in, 16)
            turn_weight(0, b0)

            def turn_ctx(b, p, i, k):
                if k == 0:
                    pe.wait_ge(cin_in[p], 32 * i + 32)
                need(pe, (v_a, v_v)[k], b - 1)
                for c, (k0, n) in enumerate(KEY_CHUNKS):
                    mm = tr((b4, b5)[k][:, k0:k0 + n], cin[p][0:n, c, k * P:(k + 1) * P], n)
                mm.then_inc(ct_done, 1)

            def project_k(b, p, o):
                pe.wait_ge(ct_a, b + 1)
                pe.wait_ge(ct_v, b + 1)
                need(pe, kr_ok, 2 * b - 2 + o + 1)
                for k in range(KC):
                    mm = nc.tensor.matmul((b4, b5)[o][:, 0:NK], wkT[:, k, o * P:(o + 1) * P], ctxT[p][:, k, 0:NK],
                                          start=(k == 0), stop=(k == KC - 1))
                mm.then_inc(kmm, 1)

            def project_v(b, p, chunks, keys):
                o = chunks[0] // 2
                need(pe, kr_ok, keys)
                for c in chunks:
                    k0, n = KEY_CHUNKS[c]
                    for k in range(KC):
                        mm = nc.tensor.matmul((b4, b5)[o][0:n, (c % 2) * D:(c % 2 + 1) * D],
                                              ctxT[p][:, k, k0:k0 + n], wvT[:, k, :],
                                              start=(k == 0), stop=(k == KC - 1))
                mm.then_inc(vmm, 1)

            for k in range(KC):
                turn_ctx(0, 0, 0, k)
            pe.wait_ge(wv_in, 16)
            turn_weight(1, b1)
            pe.wait_ge(wT_ok, 1)
            for o in range(2):
                project_k(0, 0, o)
            for k in range(KC):
                pe.wait_ge(kr_ok, 1 + k)
                turn_ctx(1, 1, 0, k)
            pe.wait_ge(w2_in, 32)
            turn_weight(2, b2)
            pe.wait_ge(wox_ok, 1)
            for g in range(4):
                for o in range(KC):
                    mm = tr((b3, b7)[g // 2][:, (g % 2) * D + o * P:(g % 2) * D + (o + 1) * P],
                            woX[:, o, g].rearrange("p j two d -> p (j two d)"), P)
            mm.then_inc(woT_done, 1)
            for o in range(2):
                project_k(1, 1, o)

            def turn_x(g):
                pe.wait_ge(xn_ok, GB * (g + 1))
                for k in range(KC):
                    need(pe, (xt_a, xt_v)[k], g)
                    for i in range(GB):
                        mm = tr((b6, b7)[k][:, i * S:(i + 1) * S], xn[:, i, k * P:(k + 1) * P], S)
                    mm.then_inc(xt_done, 1)

            def project_q(g, o):
                pe.wait_ge(xt_a, g + 1)
                pe.wait_ge(xt_v, g + 1)
                need(pe, qr_ok, 2 * g - 3 + o)
                for k in range(KC):
                    mm = nc.tensor.matmul((b0, b1, b2, b3)[2 * (g % 2) + o][:, 0:GT], wqT[:, k, o * P:(o + 1) * P],
                                          xnT[g % 2][:, k, :], start=(k == 0), stop=(k == KC - 1))
                mm.then_inc(qmm, 1)

            pe.wait_ge(wT_ok, 3)
            pe.wait_ge(woT_ok, 2)
            turn_x(0)
            for g in range(G):
                if g + 1 < G:
                    turn_x(g + 1)
                for o in range(2):
                    project_q(g, o)

            def max_scores(b, p, heads):
                for h in heads:
                    if h % HH == 0:
                        pe.wait_ge(k_in[p][h // HH], 32 * (b - p) + 64)
                    need(pe, red, 16 * b + h - 1)
                    nc.tensor.matmul((b2, b3)[h % 2][0:S, 0:NK], qst[p][0:ROWS, h * S:(h + 1) * S],
                                     kst[p][0:ROWS, h * NK:(h + 1) * NK], start=True, stop=True).then_inc(smax, 1)

            def turn_max(b, p, hh):
                pe.wait_ge(mp_ok, 2 * b + hh + 1)
                need(pe, mt_ok, 2 * b + hh)
                need(pe, x2_ok, b - 2 + hh)
                for h in range(HH):
                    hd = hh * HH + h
                    mm = nc.tensor.transpose(b7.bitcast(BF16)[ROWS:STACK, h * S:(h + 1) * S], mparts[:, hd, :],
                                             identb[0:S, 0:S])
                mm.then_inc(mt_done, 1)

            def scores(b, p, hh, c):
                n = 6 * b + 3 * hh + c
                k0 = KEY_CHUNKS[c][0]
                if c == 0:
                    pe.wait_ge(mt_ok, 2 * b + hh + 1)
                need(pe, exp_ok, n)
                for h in range(HH):
                    hd = hh * HH + h
                    at = (h // 4) * 512 + (h % 4) * S
                    mm = nc.tensor.matmul(pair[:, at:at + S], kst[p][:, hd * NK + k0:hd * NK + k0 + P],
                                          qst[p][:, hd * S:(hd + 1) * S], start=True, stop=True)
                mm.then_inc(sc_done, 1)

            def values(b, p, hh):
                pe.wait_ge(exp_ok, 6 * b + 3 * hh + 3)
                if hh == 0:
                    pe.wait_ge(v_a, b + 1)
                    pe.wait_ge(v_v, b + 1)
                    need(pe, turned_ok, b)
                for g in range(2):
                    for c, (_, n) in enumerate(KEY_CHUNKS):
                        for j in range(4):
                            h = 4 * g + j
                            col = (2 * hh + g) * S
                            mm = nc.tensor.matmul(b6[32 * j:32 * j + VW, col:col + S], vst[p][0:n, c, hh * HH + h, :],
                                                  pT[hh][0:n, c, h * S:(h + 1) * S], start=(c == 0), stop=(c == 2))
                mm.then_inc(pv_done, 1)

            def output(b, turns):
                pe.wait_ge(att_ok, b + 1)
                pe.wait_ge(mt_ok, turns)
                for g in range(4):
                    mm = nc.tensor.matmul(b7[0:S, 0:D], att[:, g * S:(g + 1) * S], woT[:, g, :],
                                          start=(g == 0), stop=(g == 3))
                mm.then_inc(wo_done, 1)

            def batch(b, p, i, first=False):
                nxt = exists(b + 1)
                keys = 2 * b + 5 if exists(b + 2) else 2 * B - 1

                def maxima(*heads):
                    if nxt:
                        max_scores(b + 1, 1 - p, heads)

                scores(b, p, 0, 0)
                maxima(0, 1)
                turn_max(b, p, 1)
                if not first:
                    values(b - 1, 1 - p, 1)
                maxima(2, 3)
                if exists(b + 2):
                    project_k(b + 2, p, 0)

                scores(b, p, 0, 1)
                maxima(4, 5)
                if exists(b + 2):
                    project_k(b + 2, p, 1)

                scores(b, p, 0, 2)
                maxima(6, 7)
                if nxt:
                    project_v(b + 1, 1 - p, (0, 1), keys)

                scores(b, p, 1, 0)
                maxima(8, 9)
                if nxt:
                    turn_max(b + 1, 1 - p, 0)
                    project_v(b + 1, 1 - p, (2,), keys + 1)

                scores(b, p, 1, 1)
                maxima(10, 11)
                if not first:
                    output(b - 1, 2 * b + 3 if nxt else 2 * B)
                maxima(12, 13)
                if exists(b + 3):
                    turn_ctx(b + 3, 1 - p, i + 1 + p, 0)

                scores(b, p, 1, 2)
                maxima(14, 15)
                if exists(b + 3):
                    turn_ctx(b + 3, 1 - p, i + 1 + p, 1)
                values(b, p, 0)

            pe.wait_ge(ones_k, 4)
            pe.wait_ge(turn_base, 1)
            pe.wait_ge(qr_ok, 2 * G)
            max_scores(0, 0, (0, 1, 2, 3))
            project_v(0, 0, (0, 1), 3)
            max_scores(0, 0, (4, 5, 6, 7))
            project_v(0, 0, (2,), 4)
            max_scores(0, 0, (8, 9, 10, 11))
            for k in range(KC):
                turn_ctx(2, 0, 1, k)
                max_scores(0, 0, (12 + 2 * k, 13 + 2 * k))
            turn_max(0, 0, 0)
            batch(0, 0, 0, first=True)
            batch(1, 1, 0)
            with pe.Fori(1, B // 2 - 2) as i:
                batch(2 * i, 0, i)
                batch(2 * i + 1, 1, i)
            for b in range(B - 4, B):
                batch(b, b % 2, b // 2)
            values(B - 1, 1, 1)

            def turn_xf(g):
                pe.wait_ge(xfb_ok, g + 1)
                need(pe, y_ok, 2 * g - 2)
                for k in range(KC):
                    need(pe, (xft_a, xft_v)[k], g)
                    for i in range(GB):
                        mm = tr((b0, b1)[k][:, i * S:(i + 1) * S], xf[:, i, k * P:(k + 1) * P], S)
                    mm.then_inc(xft_done, 1)

            def router_logits(g):
                pe.wait_ge(xft_a, g + 1)
                pe.wait_ge(xft_v, g + 1)
                need(pe, rt, ROUTER_STEPS * (g - 1) + 1)
                for k in range(KC):
                    mm = nc.tensor.matmul(b2[0:E, 0:GT], rw[:, k, :], xfT[:, k, bass.ds(GT * g, GT)],
                                          start=(k == 0), stop=(k == KC - 1))
                mm.then_inc(lgT_done, 1)

            def turn_logits(g):
                for i in range(GB):
                    mm = tr(b2[0:S, GT + i * E:GT + (i + 1) * E], lgT[:, i * S:(i + 1) * S], E)
                mm.then_inc(lg_done, 1)

            def gate_up(g, f, last=False):
                n = FC * g + f
                for w, banks, free, done in ((sg, (b3, b5), silu_ok, g_done), (su, (b4, b6), h_ok, u_done)):
                    need(pe, free, n - 1)
                    if f == FC - 1 and w is su and not last:
                        pe.wait_ge(lgT_ok, g + 2)
                    for k in range(KC):
                        mm = nc.tensor.matmul(banks[f % 2][:, 0:GT], w[:, k, f * P:(f + 1) * P],
                                              xfT[:, k, bass.ds(GT * g, GT)], start=(k == 0), stop=(k == KC - 1))
                    mm.then_inc(done, 1)

            def down(g, last=False):
                pe.wait_ge(h_ok, FC * g + FC)
                for j in range(2):
                    need(pe, y_ok, 2 * g - 1 + j)
                    if j == 0 and last:
                        pe.wait_ge(rk, 14)
                    if j == 0 and isinstance(g, int) and g == 0:
                        pe.wait_ge(x2_ok, B)
                    for i in range(2):
                        for f in range(FC):
                            at = (2 * j + i) * S
                            mm = nc.tensor.matmul((b7, b0)[j][0:S, i * D:(i + 1) * D], hT[:, f, at:at + S], sd[:, f, :],
                                                  start=(f == 0), stop=(f == FC - 1))
                    mm.then_inc(dn_done, 1)

            def ranks():
                pe.wait_ge(rt, ROUTER_STEPS * G)
                pe.wait_ge(y_ok, 2 * (G - 1) - 1)
                nc.tensor.matmul(b7[0:S, 0:B * E], lower[:, :], hot[:, :, :].rearrange("p b e -> p (b e)"),
                                 start=True, stop=False)
                nc.tensor.matmul(b7[0:S, 0:B * E], ones[:, 0:S], before[:, 0:B, :].rearrange("p b e -> p (b e)"),
                                 start=False, stop=True)
                nc.tensor.matmul(b7[:, B * E:(B + 1) * E], ones[:, :], before[:, B, :], start=True, stop=True)\
                    .then_inc(rank_done, 1)

            def group(g, last=False):
                gate_up(g, 0)
                if last:
                    ranks()
                gate_up(g, 1)
                if not last:
                    turn_xf(g + 1)
                gate_up(g, 2)
                if not last:
                    router_logits(g + 1)
                gate_up(g, 3, last)
                if not last:
                    turn_logits(g + 1)
                down(g, last)

            pe.wait_ge(exp_ok, 6 * B)
            pe.wait_ge(red, H * B)
            turn_xf(0)
            pe.wait_ge(sh_in, 64)
            router_logits(0)
            output(B - 1, 2 * B)
            pe.wait_ge(lgT_ok, 1)
            turn_logits(0)
            pe.wait_ge(turned_ok, B)
            pe.wait_ge(v_a, B)
            pe.wait_ge(v_v, B)
            pe.wait_ge(const_ok, 4)
            for g in range(G):
                group(g, last=(g == G - 1))

            def expert_of(t):
                return nc.tensor.value_load(texp_i[0:1, bass.ds(t, 1)], min_val=0, max_val=E - 1)

            def turn_rows(t, p, i):
                pe.wait_ge(xs_in[p], 16 * i + 16)
                need(pe, xst_ok, t)
                for k in range(KC):
                    mm = tr(b0[:, k * P:(k + 1) * P], xs[p][:, k * P:(k + 1) * P], P)
                mm.then_inc(xst_done, 1)

            def tile_product(w, e, out_bank, done):
                for k in range(KC):
                    mm = nc.tensor.matmul(out_bank, xsT[:, k, :], w[:, bass.ds(e, 1), k, :].rearrange("p a f -> p (a f)"),
                                          start=(k == 0), stop=(k == KC - 1))
                mm.then_inc(done, 1)

            def turn_hidden(t):
                pe.wait_ge(hrow_ok, t + 1)
                need(pe, hrt_ok, t)
                for f in range(FC):
                    mm = tr(b1[:, f * P:(f + 1) * P], hrow[:, f * P:(f + 1) * P], P)
                mm.then_inc(ht_done, 1)

            def tile_down(t, e):
                pe.wait_ge(hrt_ok, t + 1)
                need(pe, orow_ok, t)
                for f in range(FC):
                    mm = nc.tensor.matmul(b7[:, 0:D], hrT[:, f, :], ed[:, bass.ds(e, 1), f, :].rearrange("p a d -> p (a d)"),
                                          start=(f == 0), stop=(f == FC - 1))
                mm.then_inc(dt_done, 1)

            def tile(t, p, i, first=False, last=False):
                e = expert_of(t)
                pe.wait_ge(xst_ok, t + 1)
                need(pe, gact_ok, t)
                tile_product(eg, e, b3, gt_done)
                if not first:
                    turn_hidden(t - 1)
                need(pe, hrow_ok, t)
                tile_product(eu, e, b4, ut_done)
                if not last:
                    turn_rows(t + 1, 1 - p, i)
                if not first:
                    tile_down(t - 1, expert_of(t - 1))

            pe.wait_ge(y_ok, 2 * G)
            pe.wait_ge(rk, RANK_STEPS)
            pe.wait_ge(exp_in, 16 * 3 * E)
            turn_rows(0, 0, 0)
            tile(0, 0, 0, first=True)
            tile(1, 1, 1)
            tile(2, 0, 1)
            with pe.Fori(2, TILES // 2) as i:
                tile(2 * i - 1, 1, i)
                tile(2 * i, 0, i)
            tile(TILES - 2, 1, TILES // 2)
            tile(TILES - 1, 0, TILES // 2, last=True)
            turn_hidden(TILES - 1)
            tile_down(TILES - 1, expert_of(TILES - 1))

        @block.scalar
        def _(act):
            def copy(o, i_, scale=1.0):
                return nc.scalar.activation(o, i_, ACT.Copy, scale=scale)

            def by_dim(w, src):
                return (w[:, :, :].rearrange("p k (o d e) -> p (k o) d e", o=2, d=HD),
                        src[:, 0:KC * D].rearrange("p (ko e d) -> p ko d e", e=HH, d=HD))

            def put_weight(n, w, src):
                act.wait_ge(wT_done, n + 1)
                for ko in range(4):
                    o_, i_ = by_dim(w, src)
                    mm = copy(o_[:, ko], i_[:, ko], scale=HD ** -0.5 if n == 2 else 1.0)
                mm.then_inc(wT_ok, 1)

            put_weight(0, wkT, b0)

            def put_ctx(b, p):
                act.wait_ge(ct_done, 2 * b + 1)
                need(act, vmm, 2 * b - 2)
                copy(ctxT[p][:, 0, 0:NK], b4[:, 0:NK]).then_inc(ct_a, 1)

            def first_part(b, o):
                act.wait_ge(kmm, 2 * b + o + 1)
                need(act, k_out[o], 16 * b)
                copy(kp[:, o, 0, :], (b4, b5)[o][:, 0:NK]).then_inc(k1_ok, 1)

            def second_part(b, o):
                act.wait_ge(kr_ok, 2 * b + o + 1)
                copy(kp[:, o, 1, :], kr[:, o, :]).then_inc(k2_ok, 1)

            def put_values(b, p):
                act.wait_ge(vmm, 2 * b + 1)
                need(act, pv_done, 2 * b - 2)
                copy(vst[p][:, 0:2, :, 0:HD], b4.rearrange("p (c h d) -> p c h d", c=2, h=H)).then_inc(v_a, 1)

            put_ctx(0, 0)
            act.wait_ge(wT_done, 2)
            copy(wvT[:, :, :].rearrange("p k d -> p (k d)"), b1).then_inc(wT_ok, 1)
            for o in range(2):
                first_part(0, o)
            put_ctx(1, 1)
            for o in range(2):
                second_part(0, o)
            put_weight(2, wqT, b2)
            for o in range(2):
                first_part(1, o)
            for o in range(2):
                second_part(1, o)
            act.wait_ge(small_in, 80)
            nc.scalar.activation(tanhs[:, :], gates[:, :], ACT.Tanh).then_inc(tanh_ok, 1)

            def put_x(g):
                act.wait_ge(xt_done, 2 * g + 1)
                need(act, qmm, 2 * g - 2)
                copy(xnT[g % 2][:, 0, :], b6[:, 0:GT]).then_inc(xt_a, 1)

            def q_first(g, o):
                act.wait_ge(qmm, 2 * g + o + 1)
                need(act, q_out[g % 2][o], 16 * NPAIR * (g // 2))
                copy(qp[g % 2][o][:, 0, :], (b0, b1, b2, b3)[2 * (g % 2) + o][:, 0:GT]).then_inc(q1_ok, 1)

            def q_second(g, o):
                act.wait_ge(qr_ok, 2 * g + o + 1)
                copy(qp[g % 2][o][:, 1, :], qr[o][:, :]).then_inc(q2_ok, 1)

            put_x(0)
            for g in range(G):
                if g + 1 < G:
                    put_x(g + 1)
                q_first(g, 0)
                q_first(g, 1)
                q_second(g, 0)
                q_second(g, 1)

            def exps(b, hh, c):
                n = KEY_CHUNKS[c][1]
                act.wait_ge(sc_done, 6 * b + 3 * hh + c + 1)
                if c == 0:
                    need(act, pv_done, 2 * b - 1 + hh)
                nc.scalar.activation(pT[hh][0:n, c, :].rearrange("p (a n) -> p a n", a=2),
                                     pair[0:n, :].rearrange("p (a n) -> p a n", a=2)[:, :, 0:4 * S],
                                     ACT.Exp).then_inc(exp_ok, 1)

            def put_max(b, p, hh):
                act.wait_ge(mt_done, 2 * b + hh + 1)
                need(act, sc_done, 6 * b - 12 + 3 * hh + 3)
                copy(qst[p][ROWS:STACK, hh * HQ:(hh + 1) * HQ], b7.bitcast(BF16)[ROWS:STACK, 0:HQ])\
                    .then_inc(mt_ok, 1)

            def batch(b, p):
                nxt = exists(b + 1)
                exps(b, 0, 0)
                put_max(b, p, 1)
                if exists(b + 2):
                    first_part(b + 2, 0)
                exps(b, 0, 1)
                if exists(b + 2):
                    second_part(b + 2, 0)
                    first_part(b + 2, 1)
                exps(b, 0, 2)
                if exists(b + 2):
                    second_part(b + 2, 1)
                if nxt:
                    put_values(b + 1, 1 - p)
                exps(b, 1, 0)
                if nxt:
                    put_max(b + 1, 1 - p, 0)
                exps(b, 1, 1)
                if exists(b + 3):
                    put_ctx(b + 3, 1 - p)
                exps(b, 1, 2)

            put_values(0, 0)
            put_ctx(2, 0)
            put_max(0, 0, 0)
            act.wait_ge(q3_ok, 2 * G)
            for p in range(2):
                for o in range(2):
                    act.wait_ge(q_out[p][o], 16 * NPAIR * G // 2)
            batch(0, 0)
            batch(1, 1)
            with act.Fori(1, B // 2 - 2) as i:
                batch(2 * i, 0)
                batch(2 * i + 1, 1)
            for b in range(B - 4, B):
                batch(b, b % 2)

            def put_xf(g):
                act.wait_ge(xft_done, 2 * g + 1)
                copy(xfT[:, 0, bass.ds(GT * g, GT)], b0[:, 0:GT]).then_inc(xft_a, 1)

            def silu_chunk(g, f):
                n = FC * g + f
                act.wait_ge(g_done, n + 1)
                need(act, h_ok, n - 1)
                nc.scalar.activation(silu[f % 2][:, :], (b3, b5)[f % 2][:, 0:GT], ACT.Silu).then_inc(silu_ok, 1)

            def top_score(g):
                act.wait_ge(rt, ROUTER_STEPS * g + 2)
                need(act, xe_ok, GB * g)
                nc.scalar.activation(score[:, :], top[:, :], ACT.Tanh, scale=0.5).then_inc(tanh_top, 1)

            def group(g, last=False):
                silu_chunk(g, 0)
                silu_chunk(g, 1)
                if not last:
                    put_xf(g + 1)
                silu_chunk(g, 2)
                silu_chunk(g, 3)
                if not last:
                    top_score(g + 1)

            put_xf(0)
            top_score(0)
            for g in range(G):
                group(g, last=(g == G - 1))

            def put_rows(t):
                act.wait_ge(xst_done, t + 1)
                copy(xsT[:, :, :].rearrange("p k n -> p (k n)"), b0[:, 0:D]).then_inc(xst_ok, 1)

            def tile(t, last=False):
                act.wait_ge(gt_done, t + 1)
                need(act, hrow_ok, t)
                nc.scalar.activation(gact[:, :], b3, ACT.Silu).then_inc(gact_ok, 1)
                if not last:
                    put_rows(t + 1)

            put_rows(0)
            tile(0)
            with act.Fori(1, TILES - 1) as t:
                tile(t)
            tile(TILES - 1, last=True)

        @block.vector
        def _(ve):
            ve.wait_ge(ident_ok, 1)
            nc.vector.tensor_copy(identb[:, :], ident[:, :]).then_inc(identb_ok, 1)
            for p in range(2):
                nc.vector.memset(vst[p][:, :, :, :], 1.0).then_inc(ones_v, 1)
            def put_wo():
                ve.wait_ge(woT_done, 1)
                for n in range(2):
                    nc.vector.tensor_copy(woT[:, 2 * n:2 * n + 2, :].rearrange("p g d -> p (g d)"), (b3, b7)[n])\
                        .then_inc(woT_ok, 1)

            def spread_wo():
                ve.wait_ge(w2_in, 32)
                ve.wait_ge(fill_ok, 1)
                for o in range(KC):
                    last = nc.vector.tensor_copy(woX[:, o, :, :, 0, :],
                                                 wraw[:, 3, o, :].rearrange("p (g j d) -> p g j d", g=4, j=4))
                last.then_inc(wox_ok, 1)

            def put_ctx(b, p):
                ve.wait_ge(ct_done, 2 * b + 2)
                need(ve, vmm, 2 * b - 2)
                nc.vector.tensor_copy(ctxT[p][:, 1, 0:NK], b5[:, 0:NK]).then_inc(ct_v, 1)

            def rest(b, o):
                ve.wait_ge(k1_ok, 2 * b + o + 1)
                need(ve, k3_ok, 2 * b - 1 + o)
                nc.vector.tensor_tensor(kr[:, o, :], (b4, b5)[o][:, 0:NK], kp[:, o, 0, :], ALU.subtract).then_inc(kr_ok, 1)

            def put_values(b, p):
                ve.wait_ge(vmm, 2 * b + 2)
                need(ve, pv_done, 2 * b - 2)
                n = KEY_CHUNKS[2][1]
                nc.vector.tensor_copy(vst[p][0:n, 2, :, 0:HD], b5[0:n, 0:D].rearrange("p (h d) -> p h d", h=H)).then_inc(v_v, 1)

            def statistics(b):
                nc.vector.bn_stats(st[:, bass.ds(b, 1), :].rearrange("p a n -> p (a n)"),
                                   xall[:, bass.ds(b, 1), :].rearrange("p a n -> p (a n)")).then_inc(st_ok, 1)

            put_ctx(0, 0)
            ve.wait_ge(x_in, 16)
            for b in range(4):
                statistics(b)
            for o in range(2):
                rest(0, o)
            for b in range(4, 8):
                statistics(b)
            put_ctx(1, 1)
            for b in range(8, B):
                statistics(b)
            ve.wait_ge(st_ok, B)
            stats(ve, 0)
            spread_wo()
            for o in range(2):
                rest(1, o)
            put_wo()

            def norm_x(g):
                need(ve, xt_done, 2 * g)
                for i in range(GB):
                    b = GB * g + i
                    nc.vector.tensor_scalar(xn[:, i, :], xall[:, b, :], mean[:, b:b + 1], rstd[:, b:b + 1],
                                            ALU.subtract, ALU.mult).then_inc(xn_ok, 1)

            def put_x(g):
                ve.wait_ge(xt_done, 2 * g + 2)
                need(ve, qmm, 2 * g - 2)
                nc.vector.tensor_copy(xnT[g % 2][:, 1, :], b7[:, 0:GT]).then_inc(xt_v, 1)

            def q_rest(g, o):
                ve.wait_ge(q1_ok, 2 * g + o + 1)
                need(ve, q3_ok, 2 * g - 1 + o)
                nc.vector.tensor_tensor(qr[o][:, :], (b0, b1, b2, b3)[2 * (g % 2) + o][:, 0:GT], qp[g % 2][o][:, 0, :],
                                        ALU.subtract).then_inc(qr_ok, 1)

            ve.wait_ge(rs_ok, 2)
            norm_x(0)
            put_x(0)
            for g in range(G):
                if g + 1 < G:
                    norm_x(g + 1)
                    put_x(g + 1)
                for o in range(2):
                    q_rest(g, o)

            def maxima(b, heads):
                for h in heads:
                    ve.wait_ge(smax, 16 * b + h + 1)
                    if h % HH == 0:
                        need(ve, mp_ok, 2 * b - 1 + h // HH)
                    nc.vector.tensor_reduce(negmax[:, h:h + 1], (b2, b3)[h % 2][0:S, 0:NK], AX.X, ALU.max,
                                            negate=True).then_inc(red, 1)

            def split_max(b, hh):
                own = slice(hh * HH, (hh + 1) * HH)
                ve.wait_ge(red, 16 * b + (hh + 1) * HH)
                need(ve, mt_done, 2 * b + hh - 1)
                nc.vector.tensor_copy(mparts[:, own, 0], negmax[:, own]).then_inc(mp1, 1)
                ve.wait_ge(mp1, 2 * b + hh + 1)
                nc.vector.tensor_tensor(mparts[:, own, 1], negmax[:, own], mparts[:, own, 0], ALU.subtract)\
                    .then_inc(mp_ok, 1)

            def turn_out(b):
                ve.wait_ge(pv_done, 2 * b + 2)
                need(ve, scaled_ok, b)
                nc.vector.transpose(turned[:, :, :].rearrange("p a n -> p (a n)"), b6[:, 0:4 * S]).then_inc(turned_ok, 1)
                ve.wait_ge(turned_ok, b + 1)
                nc.vector.reciprocal(rec[:, :], turned[:, :, HD]).then_inc(rec_ok, 1)

            def turn_back(b):
                ve.wait_ge(scaled_ok, b + 1)
                need(ve, wo_done, b)
                nc.vector.transpose(att[:, :], scaled[:, :, :].rearrange("p a n -> p (a n)")).then_inc(att_ok, 1)

            def add_attention(b):
                ve.wait_ge(wo_done, b + 1)
                xb = xall[:, bass.ds(b, 1), :].rearrange("p a n -> p (a n)")
                nc.vector.scalar_tensor_tensor(out=xb, in0=b7[0:S, 0:D], scalar=tanhs[0:S, 0:1], in1=xb,
                                               op0=ALU.mult, op1=ALU.add).then_inc(x2_ok, 1)
                ve.wait_ge(x2_ok, b + 1)
                nc.vector.bn_stats(st[:, bass.ds(b, 1), :].rearrange("p a n -> p (a n)"), xb).then_inc(st_ok, 1)

            def batch(b, p, first=False):
                nxt = exists(b + 1)
                if nxt:
                    maxima(b + 1, (0, 1))
                if not first:
                    turn_out(b - 1)
                if nxt:
                    maxima(b + 1, (2, 3))
                if exists(b + 2):
                    rest(b + 2, 0)
                if nxt:
                    maxima(b + 1, (4, 5))
                if not first:
                    turn_back(b - 1)
                if exists(b + 2):
                    rest(b + 2, 1)
                if nxt:
                    maxima(b + 1, (6, 7))
                    split_max(b + 1, 0)
                    maxima(b + 1, (8, 9))
                    put_values(b + 1, 1 - p)
                    maxima(b + 1, (10, 11, 12, 13, 14, 15))
                    split_max(b + 1, 1)
                if exists(b + 3):
                    put_ctx(b + 3, 1 - p)
                if not first:
                    add_attention(b - 1)

            nc.vector.memset(b6, 0.0).then_inc(turn_base, 1)
            ve.wait_ge(ones_v, 2)
            maxima(0, (0, 1, 2, 3))
            maxima(0, (4, 5, 6, 7))
            split_max(0, 0)
            put_values(0, 0)
            maxima(0, range(8, 14))
            put_ctx(2, 0)
            maxima(0, (14, 15))
            split_max(0, 1)
            ve.wait_ge(xb_ok, 1)
            batch(0, 0, first=True)
            batch(1, 1)
            with ve.Fori(1, B // 2 - 2) as i:
                batch(2 * i, 0)
                batch(2 * i + 1, 1)
            def normalise(g):
                need(ve, base_ok, g)
                for i in range(GB):
                    b = GB * g + i
                    nc.vector.tensor_scalar(xn2[:, i, :], xall[:, b, :], mean[:, b:b + 1], rstd[:, b:b + 1],
                                            ALU.subtract, ALU.mult).then_inc(xn2_ok, 1)
                need(ve, xft_done, 2 * g)
                for i in range(GB):
                    ve.wait_ge(xn2_ok, GB * g + i + 1)
                    nc.vector.scalar_tensor_tensor(out=xf[:, i, :], in0=xn2[:, i, :], scalar=rstd2[:, GB * g + i:GB * g + i + 1],
                                                   in1=lnw[:, :], op0=ALU.mult, op1=ALU.mult).then_inc(xf_ok, 1)

            for b in range(B - 4, B):
                batch(b, b % 2)
                if b == B - GB + 1:
                    ve.wait_ge(st_ok, 2 * B - GB)
                    stats(ve, STATS_STEPS, slice(0, B - GB))
                if b == B - 2:
                    ve.wait_ge(rs_ok, 8)
                    ve.wait_ge(small_in, 80)
                    normalise(0)
            turn_out(B - 1)

            def put_xf(g):
                ve.wait_ge(xft_done, 2 * g + 2)
                nc.vector.tensor_copy(xfT[:, 1, bass.ds(GT * g, GT)], b1[:, 0:GT]).then_inc(xft_v, 1)

            def put_logits(g):
                ve.wait_ge(lgT_done, g + 1)
                nc.vector.tensor_copy(lgT[:, :], b2[0:E, 0:GT]).then_inc(lgT_ok, 1)

            def router(g):
                n = ROUTER_STEPS * g
                ve.wait_ge(lg_done, g + 1)
                nc.vector.tensor_copy(lg[:, :, :].rearrange("p b e -> p (b e)"), b2[0:S, GT:GT + GB * E]).then_inc(rt, 1)
                ve.wait_ge(rt, n + 1)
                nc.vector.tensor_reduce(top[:, :], lg[:, :, :], AX.X, ALU.max).then_inc(rt, 1)
                ve.wait_ge(rt, n + 2)
                nc.vector.tensor_tensor(eq[:, :, :], lg[:, :, :], top[:, :, None].broadcast_to([S, GB, E]), ALU.is_equal)\
                    .then_inc(rt, 1)
                ve.wait_ge(rt, n + 3)
                nc.vector.scalar_tensor_tensor(out=eq[:, :, :], in0=eq[:, :, :], scalar=-float(E),
                                               in1=iota_e[:, None, :].broadcast_to([S, GB, E]),
                                               op0=ALU.mult, op1=ALU.add).then_inc(rt, 1)
                ve.wait_ge(rt, n + 4)
                nc.vector.tensor_reduce(pick[:, :], eq[:, :, :], AX.X, ALU.min).then_inc(rt, 1)
                ve.wait_ge(rt, n + 5)
                nc.vector.scalar_tensor_tensor(out=hot[:, bass.ds(GB * g, GB), :],
                                               in0=iota_e[:, None, :].broadcast_to([S, GB, E]), scalar=-float(E),
                                               in1=pick[:, :, None].broadcast_to([S, GB, E]),
                                               op0=ALU.add, op1=ALU.is_equal).then_inc(rt, 1)
                for i in range(GB):
                    ve.wait_ge(rt, n + 6 + i)
                    b = GB * g + i
                    nc.vector.tensor_tensor(before[:, bass.ds(b + 1, 1), :], before[:, bass.ds(b, 1), :],
                                            hot[:, bass.ds(b, 1), :], ALU.add).then_inc(rt, 1)
                ve.wait_ge(tanh_top, g + 1)
                nc.vector.tensor_scalar(score[:, :], score[:, :], 0.5, 0.5, ALU.mult, ALU.add).then_inc(score_ok, 1)
                ve.wait_ge(score_ok, g + 1)
                ve.wait_ge(xfb_ok, g + 1)
                for i in range(GB):
                    nc.vector.tensor_scalar(xe[:, bass.ds(GB * g + i, 1), 0:D].rearrange("p a n -> p (a n)"), xf[:, i, :],
                                            score[:, i:i + 1], None, ALU.mult).then_inc(xe_ok, 1)

            def hidden(g, f):
                n = FC * g + f
                ve.wait_ge(silu_ok, n + 1)
                ve.wait_ge(u_done, n + 1)
                if f == 0:
                    need(ve, dn_done, 2 * g)
                nc.vector.tensor_tensor(hT[:, f, :], silu[f % 2][:, :], (b4, b6)[f % 2][:, 0:GT], ALU.mult).then_inc(h_ok, 1)

            def add_shared(g, j):
                ve.wait_ge(dn_done, 2 * g + j + 1)
                if j == 0:
                    ve.wait_ge(base_ok, g + 1)
                xb = xall[:, GB * g + 2 * j:GB * g + 2 * j + 2, :]
                nc.vector.scalar_tensor_tensor(out=xb, in0=(b7, b0)[j][0:S, :].rearrange("p (a n) -> p a n", a=2),
                                               scalar=tanhs[0:S, 1:2], in1=xb, op0=ALU.mult, op1=ALU.add).then_inc(y_ok, 1)

            def tiles_and_places():
                ve.wait_ge(rank_done, 1)
                nc.vector.tensor_copy(tot[:, :], b7[:, B * E:(B + 1) * E]).then_inc(rk, 1)
                ve.wait_ge(rk, 1)
                by_expert = passed[:, :].rearrange("p (e t) -> p e t", e=E)
                nc.vector.tensor_tensor(by_expert, tot[:, :, None].broadcast_to([P, E, TILES]),
                                        start_t[:, None, :].broadcast_to([P, E, TILES]), ALU.is_gt).then_inc(rk, 1)
                ve.wait_ge(rk, 2)
                nc.vector.tensor_reduce(ntile[:, :], by_expert, AX.X, ALU.add).then_inc(rk, 1)
                ve.wait_ge(rk, 3)
                nc.vector.tensor_copy(upto[:, 0:1], ntile[:, 0:1]).then_inc(rk, 1)
                for e in range(1, E):
                    ve.wait_ge(rk, 3 + e)
                    nc.vector.tensor_tensor(upto[:, e:e + 1], upto[:, e - 1:e], ntile[:, e:e + 1], ALU.add).then_inc(rk, 1)
                ve.wait_ge(rk, 11)
                nc.vector.tensor_tensor(first_row[:, :], upto[:, :], ntile[:, :], ALU.subtract).then_inc(rk, 1)
                by_tile = passed[:, :].rearrange("p (t e) -> p t e", e=E)
                nc.vector.tensor_tensor(by_tile, iota_t[:, :, None].broadcast_to([P, TILES, E]),
                                        upto[:, None, :].broadcast_to([P, TILES, E]), ALU.is_ge).then_inc(rk, 1)
                ve.wait_ge(rk, 12)
                nc.vector.scalar_tensor_tensor(out=rank[:, :, :], in0=first_row[0:S, None, :].broadcast_to([S, B, E]),
                                               scalar=float(P), in1=b7[0:S, 0:B * E].rearrange("p (b e) -> p b e", e=E),
                                               op0=ALU.mult, op1=ALU.add).then_inc(rk, 1)
                ve.wait_ge(rk, 14)
                nc.vector.tensor_tensor(rank[:, :, :], rank[:, :, :], hot[:, :, :], ALU.mult).then_inc(rk, 1)
                nc.vector.tensor_reduce(texp[:, :], by_tile, AX.X, ALU.add).then_inc(rk, 1)
                ve.wait_ge(rk, 16)
                nc.vector.tensor_reduce(pos[:, :], rank[:, :, :], AX.X, ALU.add).then_inc(rk, 1)
                nc.vector.tensor_scalar(texp_i[:, :], texp[:, :], float(E - 1), None, ALU.min).then_inc(rk, 1)
                ve.wait_ge(rk, 17)
                nc.vector.tensor_copy(pos_i[:, :], pos[:, :]).then_inc(rk, 1)

            put_xf(0)
            turn_back(B - 1)
            put_logits(0)
            add_attention(B - 1)
            nc.vector.memset(before[:, 0, :], 0.0).then_inc(s2_init, 1)
            ve.wait_ge(st_ok, 2 * B)
            stats(ve, 2 * STATS_STEPS, slice(B - GB, B))
            ve.wait_ge(const_ok, 4)
            ve.wait_ge(s2_init, 1)
            router(0)
            normalise(1)
            for g in range(G):
                hidden(g, 0)
                if g == G - 1:
                    tiles_and_places()
                hidden(g, 1)
                if g + 1 < G:
                    put_xf(g + 1)
                hidden(g, 2)
                if g + 1 < G:
                    put_logits(g + 1)
                hidden(g, 3)
                if g + 1 < G:
                    router(g + 1)
                add_shared(g, 0)
                if g + 2 == G - 1:
                    ve.wait_ge(rs_ok, 14)
                if g + 2 < G:
                    normalise(g + 2)
                add_shared(g, 1)

            def hidden_rows(t):
                ve.wait_ge(gact_ok, t + 1)
                ve.wait_ge(ut_done, t + 1)
                need(ve, ht_done, t)
                nc.vector.tensor_tensor(hrow[:, :], gact[:, :], b4, ALU.mult).then_inc(hrow_ok, 1)

            def put_hidden(t):
                ve.wait_ge(ht_done, t + 1)
                need(ve, dt_done, t)
                nc.vector.tensor_copy(hrT[:, :, :].rearrange("p f n -> p (f n)"), b1).then_inc(hrt_ok, 1)

            def finish_rows(t, p, i):
                ve.wait_ge(dt_done, t + 1)
                ve.wait_ge(resid_in[p], 16 * i + 16)
                need(ve, out_done[p], 16 * i)
                nc.vector.scalar_tensor_tensor(out=orow[p][:, :], in0=b7[:, 0:D], scalar=tanhs[:, 1:2], in1=resid[p][:, :],
                                               op0=ALU.mult, op1=ALU.add).then_inc(orow_ok, 1)

            def tile(t, p, i):
                put_hidden(t - 1)
                hidden_rows(t)
                finish_rows(t - 1, 1 - p, i)

            hidden_rows(0)
            tile(1, 1, 0)
            tile(2, 0, 0)
            with ve.Fori(1, TILES // 2) as i:
                tile(2 * i + 1, 1, i)
                tile(2 * i + 2, 0, i)
            put_hidden(TILES - 1)
            finish_rows(TILES - 1, 0, TILES // 2)

        @block.gpsimd
        def _(pool):
            nc.gpsimd.memset(ident[:, :], 0.0).then_inc(ident_z, 1)
            pool.wait_ge(ident_z, 1)
            nc.gpsimd.affine_select(out=ident[:, :], in_=ident[:, :], compare_op=ALU.not_equal, fill=1.0, base=0,
                                    pattern=[[-1, P]], channel_multiplier=1).then_inc(ident_ok, 1)
            nc.gpsimd.memset(woX[:, :, :, :, :, :], 0.0).then_inc(fill_ok, 1)
            nc.gpsimd.memset(zrow[:, 0:D], 0.0).then_inc(fill_ok, 1)
            nc.gpsimd.memset(zrow[:, D:XROW].bitcast(I32), NOBODY).then_inc(fill_ok, 1)
            nc.gpsimd.memset(mhalf[:, :], -0.5).then_inc(fill_ok, 1)
            nc.gpsimd.memset(ones[:, :], 1.0).then_inc(fill_ok, 1)
            pool.wait_ge(fill_ok, 5)
            nc.gpsimd.affine_select(out=lower[:, :], in_=ones[:, 0:S], compare_op=ALU.is_gt, fill=0.0, base=0,
                                    pattern=[[1, S]], channel_multiplier=-1).then_inc(const_ok, 1)
            for dst, first, step, n in ((iota_e, E, 1, E), (iota_t, 0, 1, TILES), (start_t, 0, P, TILES)):
                nc.gpsimd.iota(dst[:, :], pattern=[[step, n]], base=first, channel_multiplier=0,
                               allow_small_or_imprecise_dtypes=True).then_inc(const_ok, 1)

            pool.wait_ge(const_ok, 4)
            for p in range(2):
                need(pool, ones_k, 2 * p)
                nc.gpsimd.memset(kst[p][ROWS:STACK, :], 1.0).then_inc(ones_k, 1)
                nc.gpsimd.memset(kst[p][0:ROWS, H * NK:H * NK + 16], 0.0).then_inc(ones_k, 1)
            pool.wait_ge(ones_k, 4)

            def third_part(b, o):
                pool.wait_ge(k2_ok, 2 * b + o + 1)
                nc.gpsimd.tensor_tensor(kp[:, o, 2, :], kr[:, o, :], kp[:, o, 1, :], ALU.subtract).then_inc(k3_ok, 1)

            for b in range(2):
                for o in range(2):
                    third_part(b, o)

            pool.wait_ge(lnv, STATS_STEPS)
            pool.wait_ge(fill_ok, 4)
            nc.gpsimd.tensor_scalar(tmp[:, :], var[:, :], EPS, 1.0, ALU.add, ALU.mult).then_inc(rs_ok, 1)
            pool.wait_ge(rs_ok, 1)
            nc.gpsimd.tensor_tensor(rstd[:, :], tmp[:, :], mhalf[:, :], ALU.pow).then_inc(rs_ok, 1)

            for g in range(G):
                for o in range(2):
                    pool.wait_ge(q2_ok, 2 * g + o + 1)
                    nc.gpsimd.tensor_tensor(qp[g % 2][o][:, 2, :], qr[o][:, :], qp[g % 2][o][:, 1, :], ALU.subtract)\
                        .then_inc(q3_ok, 1)

            pool.wait_ge(ones_k, 4)
            pool.wait_ge(tanh_ok, 1)
            nc.gpsimd.tensor_scalar(bo_b[:, :], bo_b[:, :], tanhs[0:S, 0:1], 0.0, ALU.mult, ALU.add).then_inc(tb_ok, 1)
            pool.wait_ge(tb_ok, 1)
            pool.wait_ge(xn_ok, B)
            nc.gpsimd.tensor_tensor(xall[:, :, :], xall[:, :, :], bo_b[:, None, :].broadcast_to([S, B, D]),
                                    ALU.add).then_inc(xb_ok, 1)

            def rsqrt(first, cols):
                def step(n, out_, a, b_, op):
                    pool.wait_ge(rs_ok, n)
                    nc.gpsimd.tensor_tensor(out_[:, cols], a[:, cols], b_[:, cols], op).then_inc(rs_ok, 1)

                def plus_eps(src):
                    nc.gpsimd.tensor_scalar(tmp[:, cols], src[:, cols], EPS, 1.0, ALU.add, ALU.mult).then_inc(rs_ok, 1)

                pool.wait_ge(lnv, STATS_STEPS * (2 + (first - 2) // 6))
                plus_eps(var)
                step(first + 1, rstd, tmp, mhalf, ALU.pow)
                step(first + 2, tmp, var, rstd, ALU.mult)
                step(first + 3, tmp, tmp, rstd, ALU.mult)
                pool.wait_ge(rs_ok, first + 4)
                plus_eps(tmp)
                step(first + 5, rstd2, tmp, mhalf, ALU.pow)

            def shift(g):
                pool.wait_ge(xf_ok, GB * g + GB)
                nc.gpsimd.tensor_tensor(xf[:, :, :], xf[:, :, :], lnb[:, None, :].broadcast_to([S, GB, D]), ALU.add)\
                    .then_inc(xfb_ok, 1)

            def base(g):
                nc.gpsimd.tensor_scalar(xn2[:, :, :], xn2[:, :, :], tanhs[0:S, 1:2], 0.0, ALU.mult, ALU.add)\
                    .then_inc(xn2_scaled, 1)
                pool.wait_ge(xn2_scaled, g + 1)
                xg = xall[:, GB * g:GB * g + GB, :]
                nc.gpsimd.tensor_tensor(xg, xg, xn2[:, :, :], ALU.add).then_inc(base_ok, 1)

            def scale_out(b):
                pool.wait_ge(rec_ok, b + 1)
                need(pool, att_ok, b)
                nc.gpsimd.tensor_tensor(scaled[:, :, :], turned[:, :, :], rec[:, :, None].broadcast_to([P, NB, 32]),
                                        ALU.mult).then_inc(scaled_ok, 1)

            def batch(b):
                if exists(b + 2):
                    third_part(b + 2, 0)
                scale_out(b - 1)
                if exists(b + 2):
                    third_part(b + 2, 1)

            for o in range(2):
                third_part(2, o)
            batch(1)
            with pool.Fori(2, B - 2) as b:
                batch(b)
            batch(B - 2)
            rsqrt(2, slice(0, B - GB))
            shift(0)
            batch(B - 1)
            base(0)
            scale_out(B - 1)

            rsqrt(8, slice(B - GB, B))
            pool.wait_ge(x2_ok, B)
            nc.gpsimd.iota(xe[:, :, D].bitcast(I32), pattern=[[S, B]], base=0, channel_multiplier=1).then_inc(s2_fill, 1)
            for p in range(2):
                nc.gpsimd.memset(resid[p][:, :], 0.0).then_inc(s2_fill, 1)
            for g in range(1, G):
                shift(g)
                base(g)

            pool.wait_ge(rk, RANK_STEPS)
            pool.wait_ge(xe_ok, B)
            pool.wait_ge(s2_fill, 3)
            for b in range(B):
                nc.gpsimd.indirect_dma_start(out=xs_dram[:, :], out_offset=bass.IndirectOffsetOnAxis(ap=pos_i[:, b:b + 1], axis=0),
                                             in_=xe[:, b, :], in_offset=None).then_inc(scat, 16)

            def fetch(t):
                p, i = t % 2, t // 2
                pool.wait_ge(xs_in[p], 16 * i + 16)
                need(pool, out_done[p], 16 * i)
                nc.gpsimd.tensor_copy(who[p][:, :], xs[p][:, D:XROW].bitcast(U32)).then_inc(who_ok, 1)
                pool.wait_ge(who_ok, t + 1)
                need(pool, orow_ok, t - 1)
                nc.gpsimd.indirect_dma_start(out=resid[p][:, :], out_offset=None, in_=resid_dram[:, :],
                                             in_offset=bass.IndirectOffsetOnAxis(ap=who[p][:, 0:1], axis=0),
                                             bounds_check=T - 1, oob_is_err=False).then_inc(resid_in[p], 16)

            def store(t):
                p = t % 2
                pool.wait_ge(orow_ok, t + 1)
                nc.gpsimd.indirect_dma_start(out=out.rearrange("b s d -> (b s) d"),
                                             out_offset=bass.IndirectOffsetOnAxis(ap=who[p][:, 0:1], axis=0),
                                             in_=orow[p][:, :], in_offset=None,
                                             bounds_check=T - 1, oob_is_err=False).then_inc(out_done[p], 16)

            pool.wait_ge(resid_out, 16 * G)
            for t in range(TILES):
                fetch(t)
                if t > 0:
                    store(t - 1)
            store(TILES - 1)
            pool.wait_ge(out_done[0], 16 * (TILES // 2 + 1))
            pool.wait_ge(out_done[1], 16 * (TILES // 2))


_OUTS = [((B, S, D), "float32")]


def kernel(**inputs):
    import numpy as _np
    import concourse.bacc as _bacc
    from concourse.bass_utils import run_bass_kernel_spmd as _run

    nc = _bacc.Bacc("TRN2", target_bir_lowering=False, num_devices=1)
    names = ["x", "ctx_1024", "g_xattn", "g_ffn", "L0_xattn_Wq", "L0_xattn_Wk", "L0_xattn_Wv", "L0_xattn_Wo",
             "L0_xattn_bo", "L0_ffn_ln_w", "L0_ffn_ln_b", "L0_ffn_router_w", "L0_ffn_gate_w", "L0_ffn_up_w",
             "L0_ffn_down_w", "L0_ffn_sh_gate", "L0_ffn_sh_up", "L0_ffn_sh_down"]
    arrays, args = {}, []
    for name in names:
        a = _np.ascontiguousarray(inputs[name])
        arrays[f"in_{name}"] = a
        args.append(nc.dram_tensor(f"in_{name}", a.shape, mybir.dt.from_np(a.dtype), kind="ExternalInput").ap())
    shape, dtype = _OUTS[0]
    args.append(nc.dram_tensor("out_0", shape, mybir.dt.from_np(_np.dtype(dtype)), kind="ExternalOutput").ap())
    build(nc, *args)
    r = _run(nc, [arrays], core_ids=[0])
    return r.results[0]["out_0"]
```

```python
from contextlib import ExitStack

import concourse.bass as bass
from concourse import mybir

F32 = mybir.dt.float32
F32R = mybir.dt.float32r
BF16 = mybir.dt.bfloat16
I32 = mybir.dt.int32
U32 = mybir.dt.uint32
ALU = mybir.AluOpType
ACT = mybir.ActivationFunctionType
AX = mybir.AxisListType

B, S, D = 16, 112, 256
NK = 375
H, HD = 16, 16
E, FF = 8, 512
EPS = 1e-5
P = 128
T = B * S
KC = D // P
FC = FF // P
KEY_CHUNKS = [(0, 128), (128, 128), (256, NK - 256)]
HH = H // 2
PARTS = 3
ROUNDED_PAIRS = [(0, 0), (0, 1), (1, 0)]
K_PARTS = [0, 1, 2, 0, 1, 0]
Q_PARTS = [0, 0, 0, 1, 1, 2]
NPAIR = len(K_PARTS)
ROWS = NPAIR * HD
SHIFT_ROWS = 2
STACK = ROWS + SHIFT_ROWS
VW = HD + 1
HQ = HH * S
NB = 4 * S // 32
G, GB = 4, 4
GT = GB * S
TILES = (T + E * (P - 1)) // P
SLOTS = 3
assert TILES % SLOTS == 0
XROW = D + 1
NOBODY = 1 << 20


def build(nc, x, ctx, g_xattn, g_ffn, Wq, Wk, Wv, Wo, bo, ln_w, ln_b, router_w, gate_w, up_w, down_w,
          sh_gate, sh_up, sh_down, out):
    stack = ExitStack()
    with stack:
        def sem(name):
            return stack.enter_context(nc.semaphore(name))

        def sb(name, shape, dt=F32, scope=stack):
            return scope.enter_context(nc.sbuf_tensor(name, shape, dt))

        def bank(name, n=1):
            return stack.enter_context(nc.psum_tensor(name, [P, n * 512], F32))

        def need(eng, s, count):
            if not (isinstance(count, int) and count <= 0):
                eng.wait_ge(s, count)

        k_dram = nc.dram_tensor("k_parts_dram", [B, 2, PARTS, HD, HH, NK], BF16).ap()
        q_dram = nc.dram_tensor("q_parts_dram", [2, NPAIR, HD, HH, T], BF16).ap()
        xs_dram = nc.dram_tensor("sorted_rows_dram", [TILES * P, XROW], F32).ap()
        resid_dram = nc.dram_tensor("resid_dram", [T, D], F32).ap()

        ident = sb("ident", [P, P])
        identb = sb("identb", [P, P], BF16)
        woT = sb("woT", [P, 4, D])
        xall = sb("xall", [S, B, D])
        eu = sb("eu", [P, E, KC, FF])
        ed = sb("ed", [P, E, FC, D])
        sd = sb("sd", [P, FC, D])
        lnw = sb("lnw", [S, D])
        lnb = sb("lnb", [S, D])
        bo_b = sb("bo_b", [S, D])
        gates = sb("gates", [P, 2])
        tanhs = sb("tanhs", [P, 2])
        st = sb("st", [S, B, 6])
        mean = sb("mean", [S, B])
        var = sb("var", [S, B])
        tmp = sb("tmp", [S, B])
        rstd = sb("rstd", [S, B])
        rstd2 = sb("rstd2", [S, B])
        mhalf = sb("mhalf", [S, B])
        negmax = sb("negmax", [S, H])
        mparts = sb("mparts", [S, H, SHIFT_ROWS], BF16)

        lower = sb("lower", [S, S])
        ones = sb("ones", [S, P])
        iota_e = sb("iota_e", [S, E])
        iota_t = sb("iota_t", [P, TILES])
        start_t = sb("start_t", [P, TILES])

        raw = ExitStack()
        wraw = sb("wraw", [P, 4, KC, D], scope=raw)
        woX = sb("woX", [P, KC, 4, 4, 2, HD], scope=raw)
        qr = [sb(f"qr{p}", [P, GT], scope=raw) for p in range(2)]
        raw.close()
        raw2 = ExitStack()
        sg_raw = sb("sg_raw", [P, KC, FF], scope=raw2)
        su_raw = sb("su_raw", [P, KC, FF], scope=raw2)
        rw_raw = sb("rw_raw", [P, KC, E], scope=raw2)
        raw2.close()
        sg_lo = sb("sg_lo", [P, KC, FF], F32R)
        su_lo = sb("su_lo", [P, KC, FF], F32R)
        rw_lo = sb("rw_lo", [P, KC, E], F32R)
        xn2 = sb("xn2", [S, GB, D])
        xf0 = sb("xf0", [S, GB, D])

        s1 = ExitStack()
        cin = [sb(f"cin{p}", [P, 3, D], scope=s1) for p in range(2)]
        ctxT = [sb(f"ctxT{p}", [P, 2, KC, NK + 1], F32R, scope=s1) for p in range(2)]
        kp = sb("kp", [P, 2, PARTS, NK], BF16, scope=s1)
        kr = sb("kr", [P, 2, NK], scope=s1)
        vst = [sb(f"vst{p}", [P, 3, H, VW], scope=s1) for p in range(2)]
        wkT = sb("wkT", [P, 2, KC, D], F32R, scope=s1)
        wvT = sb("wvT", [P, 2, KC, D], F32R, scope=s1)
        zrow = sb("zrow", [P, XROW], scope=s1)
        kst = [sb(f"kst{p}", [STACK, H * NK + 16], BF16, scope=s1) for p in range(2)]
        qst = [sb(f"qst{p}", [STACK, H * S], BF16, scope=s1) for p in range(2)]
        s0 = ExitStack()
        wqT = sb("wqT", [P, KC, D], scope=s0)
        xn = sb("xn", [S, GB, D], scope=s0)
        xnT = [sb(f"xnT{p}", [P, KC, GT], scope=s0) for p in range(2)]
        qp = [[sb(f"qp{p}{o}", [P, PARTS, GT], BF16, scope=s0) for o in range(2)] for p in range(2)]
        s0.close()
        pT = [sb(f"pT{hh}", [P, 3, HQ], scope=s1) for hh in range(2)]
        turned = sb("turned", [P, NB, 32], scope=s1)
        rec = sb("rec", [P, NB], scope=s1)
        scaled = sb("scaled", [P, NB, 32], scope=s1)
        att = sb("att", [P, 4 * S], scope=s1)
        s1.close()

        s2 = ExitStack()
        eg = sb("eg", [P, E, KC, FF], scope=s2)
        xe = sb("xe", [S, B, XROW], scope=s2)
        s3 = ExitStack()
        xf = [xf0, sb("xf1", [S, GB, D], scope=s3)]
        passed = sb("passed", [P, TILES * E], scope=s3)
        before = sb("before", [S, B + 1, E], scope=s3)
        rank = sb("rank", [S, B, E], scope=s3)
        sg_hi = sb("sg_hi", [P, KC, FF], F32R, scope=s3)
        su_hi = sb("su_hi", [P, KC, FF], F32R, scope=s3)
        rw_hi = sb("rw_hi", [P, KC, E], F32R, scope=s3)
        sg, su, rw = (sg_hi, sg_lo), (su_hi, su_lo), (rw_hi, rw_lo)
        xfT = [sb(f"xfT{p}", [P, 2, KC, GT], F32R, scope=s3) for p in range(2)]
        silu = [sb(f"silu{p}", [P, GT], scope=s3) for p in range(2)]
        hT = sb("hT", [P, FC, GT], scope=s3)
        lgT = sb("lgT", [E, GT], scope=s3)
        s3.close()
        tg_round = [sb(f"tg_round{p}", [P, KC * FF], F32R, scope=s2) for p in range(SLOTS)]
        tg_rest = sb("tg_rest", [P, KC * FF], F32R, scope=s2)
        tu = sb("tu", [P, 2, KC * FF], F32R, scope=s2)
        td = sb("td", [P, 2, FC * D], F32R, scope=s2)
        td_last = tg_round[0:2]
        assert (TILES - 1) % SLOTS == 2 and KC * FF == FC * D
        gact = sb("gact", [P, FF], scope=s2)
        hrow = sb("hrow", [P, FF], scope=s2)
        xsT = sb("xsT", [P, 2, KC * P], F32R, scope=s2)
        hrT = sb("hrT", [P, 2, FC * P], F32R, scope=s2)
        lg = sb("lg", [S, GB, E], scope=s2)
        top = sb("top", [S, GB], scope=s2)
        score = sb("score", [S, GB], scope=s2)
        eq = sb("eq", [S, GB, E], scope=s2)
        pick = sb("pick", [S, GB], scope=s2)
        hot = sb("hot", [S, B, E], scope=s2)
        tot = sb("tot", [P, E], scope=s2)
        ntile = sb("ntile", [P, E], scope=s2)
        upto = sb("upto", [P, E], scope=s2)
        first_row = sb("first_row", [P, E], scope=s2)
        texp = sb("texp", [P, TILES], scope=s2)
        texp_i = sb("texp_i", [P, TILES], I32, scope=s2)
        pos = sb("pos", [S, B], scope=s2)
        pos_i = sb("pos_i", [S, B], U32, scope=s2)
        xs = [sb(f"xs{p}", [P, XROW], scope=s2) for p in range(SLOTS)]
        who = [sb(f"who{p}", [P, 1], U32, scope=s2) for p in range(SLOTS)]
        resid = [sb(f"resid{p}", [P, D], scope=s2) for p in range(SLOTS)]
        s2.close()

        pair = bank("pair", 2)
        single = [bank(f"single{n}") for n in range(2, 8)]
        b0, b1 = pair[:, 0:512], pair[:, 512:1024]
        b2, b3, b4, b5, b6, b7 = (s[:, :] for s in single)

        ident_z, ident_ok, identb_ok = sem("ident_z"), sem("ident_ok"), sem("identb_ok")
        fill_ok = sem("fill_ok")
        wk_in, wv_in = sem("wk_in"), sem("wv_in")
        w2_in = sem("w2_in")
        x_in, small_in, sh_in = sem("x_in"), sem("small_in"), sem("sh_in")
        exp_in = sem("exp_in")
        zero_out = sem("zero_out")
        ones_v, pad_ok, turn_base = sem("ones_v"), sem("pad_ok"), sem("turn_base")
        wox_ok = sem("wox_ok")
        wT_done, wT_ok, wlo_ok = sem("wT_done"), sem("wT_ok"), sem("wlo_ok")
        woT_done, woT_ok = sem("woT_done"), sem("woT_ok")
        st_ok = sem("st_ok")
        lnv = sem("lnv")
        rs_ok = sem("rs_ok")
        xn_ok, xt_done = sem("xn_ok"), sem("xt_done")
        xt_a, xt_v = sem("xt_a"), sem("xt_v")
        qmm, q1_ok, qr_ok, q2_ok, q3_ok = sem("qmm"), sem("q1_ok"), sem("qr_ok"), sem("q2_ok"), sem("q3_ok")
        q_out = [[sem(f"q_out{p}{o}") for o in range(2)] for p in range(2)]
        tanh_ok, tb_ok, xb_ok = sem("tanh_ok"), sem("tb_ok"), sem("xb_ok")
        cin_in = [sem(f"cin_in{p}") for p in range(2)]
        ct_done = sem("ct_done")
        ct_hi, ct_lo = sem("ct_hi"), sem("ct_lo")
        kmm, vmm = sem("kmm"), sem("vmm")
        k1_ok, kr_ok, k2_ok, k3_ok = sem("k1_ok"), sem("kr_ok"), sem("k2_ok"), sem("k3_ok")
        v_a, v_v = sem("v_a"), sem("v_v")
        k_out = [sem(f"k_out{o}") for o in range(2)]
        k_in = [[sem(f"k_in{p}{hh}") for hh in range(2)] for p in range(2)]
        ones_k = sem("ones_k")
        smax, red = sem("smax"), sem("red")
        mp1, mp_ok = sem("mp1"), sem("mp_ok")
        mt_done, mt_ok = sem("mt_done"), sem("mt_ok")
        sc_done, exp_ok, pv_done = sem("sc_done"), sem("exp_ok"), sem("pv_done")
        turned_ok, rec_ok, scaled_ok, att_ok = sem("turned_ok"), sem("rec_ok"), sem("scaled_ok"), sem("att_ok")
        wo_done, x2_ok = sem("wo_done"), sem("x2_ok")
        const_ok, s2_init, s2_fill = sem("const_ok"), sem("s2_init"), sem("s2_fill")
        xn2_ok, xf_ok, xfb_ok = sem("xn2_ok"), sem("xf_ok"), sem("xfb_ok")
        xn2_scaled, base_ok = sem("xn2_scaled"), sem("base_ok")
        sw_hi, sw_lo = sem("sw_hi"), sem("sw_lo")
        xft_done, xft_hi, xft_lo = sem("xft_done"), sem("xft_hi"), sem("xft_lo")
        lgT_done, lgT_ok, lg_done = sem("lgT_done"), sem("lgT_ok"), sem("lg_done")
        rt = sem("rt")
        tanh_top, score_ok, xe_ok = sem("tanh_top"), sem("score_ok"), sem("xe_ok")
        g_done, u_done, silu_ok, h_ok = sem("g_done"), sem("u_done"), sem("silu_ok"), sem("h_ok")
        dn_done, y_ok, resid_out = sem("dn_done"), sem("y_ok"), sem("resid_out")
        rank_done, rk = sem("rank_done"), sem("rk")
        scat = sem("scat")
        xs_in = [sem(f"xs_in{p}") for p in range(SLOTS)]
        who_ok = sem("who_ok")
        resid_in = [sem(f"resid_in{p}") for p in range(SLOTS)]
        xst_done, xst_hi, xst_lo = sem("xst_done"), sem("xst_hi"), sem("xst_lo")
        tg_hi, tg_lo, tu_hi, tu_lo = sem("tg_hi"), sem("tg_lo"), sem("tu_hi"), sem("tu_lo")
        td_hi, td_lo, td_lo_last = sem("td_hi"), sem("td_lo"), sem("td_lo_last")
        gt_done, ut_done, gact_ok, hrow_ok = sem("gt_done"), sem("ut_done"), sem("gact_ok"), sem("hrow_ok")
        ht_done, hrt_hi, hrt_lo = sem("ht_done"), sem("hrt_hi"), sem("hrt_lo")
        dt_done, orow_ok = sem("dt_done"), sem("orow_ok")
        out_done = [sem(f"out_done{p}") for p in range(SLOTS)]
        ROUTER_STEPS = 6 + GB
        RANK_STEPS = 19

        def stats(ve, first, cols=slice(0, B)):
            me, mo = st[:, cols, 1], st[:, cols, 4]
            ve_, vo = st[:, cols, 2], st[:, cols, 5]
            nc.vector.tensor_tensor(mean[:, cols], me, mo, ALU.add).then_inc(lnv, 1)
            nc.vector.tensor_tensor(tmp[:, cols], me, mo, ALU.subtract).then_inc(lnv, 1)
            nc.vector.tensor_tensor(var[:, cols], ve_, vo, ALU.add).then_inc(lnv, 1)
            ve.wait_ge(lnv, first + 3)
            nc.vector.tensor_scalar(mean[:, cols], mean[:, cols], 0.5, None, ALU.mult).then_inc(lnv, 1)
            nc.vector.tensor_tensor(tmp[:, cols], tmp[:, cols], tmp[:, cols], ALU.mult).then_inc(lnv, 1)
            nc.vector.tensor_scalar(var[:, cols], var[:, cols], 1.0 / D, None, ALU.mult).then_inc(lnv, 1)
            ve.wait_ge(lnv, first + 6)
            nc.vector.scalar_tensor_tensor(out=var[:, cols], in0=tmp[:, cols], scalar=0.25, in1=var[:, cols],
                                           op0=ALU.mult, op1=ALU.add).then_inc(lnv, 1)

        STATS_STEPS = 7

        block = stack.enter_context(nc.Block())

        def g_lead(g):
            return 0 if g + 2 == G else 1

        def exists(b):
            return not isinstance(b, int) or b < B

        @block.sync
        def _(sp):
            def load_ctx(b, p):
                src = ctx[bass.ds(b, 1)]
                sp.dma_start(cin[p][:, 0:2, :], src[:, 0:256, :].rearrange("a (c p) d -> p (a c) d", p=P))\
                    .then_inc(cin_in[p], 16)
                sp.dma_start(cin[p][0:NK - 256, 2, :], src[:, 256:NK, :].rearrange("a p d -> (a p) d"))\
                    .then_inc(cin_in[p], 16)

            def load_ctx_after(b, p):
                sp.wait_ge(ct_done, 2 * b - 2)
                load_ctx(b, p)

            def weight(dst, w):
                return sp.dma_start(dst, w.rearrange("(k p) d -> p k d", p=P))

            weight(wraw[:, 0], Wk).then_inc(wk_in, 16)
            load_ctx(0, 0)
            weight(wraw[:, 1], Wv).then_inc(wv_in, 16)
            sp.dma_start(xall[:, :, :], x.rearrange("b s d -> s b d")).then_inc(x_in, 16)
            load_ctx(1, 1)
            weight(wraw[:, 2], Wq).then_inc(w2_in, 16)
            weight(wraw[:, 3], Wo).then_inc(w2_in, 16)
            for dst, src in ((bo_b, bo), (lnw, ln_w), (lnb, ln_b)):
                sp.dma_start(dst[:, :], src.rearrange("(a d) -> a d", a=1).broadcast_to([S, D])).then_inc(small_in, 16)
            for n, gate in enumerate((g_xattn, g_ffn)):
                sp.dma_start(gates[:, n:n + 1], gate.rearrange("(a d) -> a d", a=1).broadcast_to([P, 1])).then_inc(small_in, 16)

            def store_keys(b, o):
                sp.wait_ge(k3_ok, 2 * b + o + 1)
                sp.dma_start(k_dram[bass.ds(b, 1), o].rearrange("a t d e k -> (d e) (a t) k"), kp[:, o, :, :])\
                    .then_inc(k_out[o], 16)

            def load_stack(b, p, hh):
                need(sp, sc_done, 6 * b - 12 + 3 * hh + 3)
                sp.wait_ge(k_out[hh], 16 * b + 16)
                src = k_dram[bass.ds(b, 1), hh]
                row = 0
                for n in (3, 2, 1):
                    sp.dma_start(kst[p][row:row + n * HD, hh * HH * NK:(hh + 1) * HH * NK],
                                 src[:, 0:n].rearrange("a t d e k -> (a t d) (e k)")).then_inc(k_in[p][hh], 16)
                    row += n * HD
                sp.dma_start(qst[p][0:ROWS, hh * HQ:(hh + 1) * HQ].rearrange("p (e q) -> p e q", q=S),
                             q_dram[hh, :, :, :, bass.ds(b * S, S)].rearrange("t d e q -> (t d) e q"))\
                    .then_inc(k_in[p][hh], 16)

            def store_queries(g):
                for o in range(2):
                    sp.wait_ge(q3_ok, 2 * g + o + 1)
                    row = 0
                    for part, n in enumerate((3, 2, 1)):
                        sp.dma_start(q_dram[o, row:row + n, :, :, g * GT:(g + 1) * GT].rearrange("t d e q -> (d e) t q"),
                                     qp[g % 2][o][:, part:part + 1, :].broadcast_to([P, n, GT])).then_inc(q_out[g % 2][o], 16)
                        row += n

            for b in range(2):
                store_keys(b, 0)
                store_keys(b, 1)
                load_ctx_after(b + 2, b)
            store_queries(0)
            store_queries(1)
            for b in range(2):
                for o in range(2):
                    sp.wait_ge(q_out[0][o], 16 * PARTS)
                    load_stack(b, b, o)
                store_queries(2 + b)
            for p in range(2):
                for o in range(2):
                    sp.wait_ge(q_out[p][o], 16 * PARTS * G // 2)
            sp.wait_ge(fill_ok, 3)
            sp.dma_start(xs_dram.rearrange("(t p) c -> p t c", p=P), zrow[:, None, :].broadcast_to([P, TILES, XROW]))\
                .then_inc(zero_out, 16)

            def batch(b, p):
                if exists(b + 2):
                    store_keys(b + 2, 0)
                    store_keys(b + 2, 1)
                    load_stack(b + 2, p, 0)
                    load_stack(b + 2, p, 1)
                if exists(b + 4):
                    load_ctx_after(b + 4, p)

            def expert(e):
                for dst, w in ((eu, up_w), (ed, down_w)):
                    sp.dma_start(dst[:, bass.ds(e, 1), :, :],
                                 w[bass.ds(e, 1)].rearrange("e (k p) f -> p e k f", p=P)).then_inc(exp_in, 16)

            batch(0, 0)
            batch(1, 1)
            with sp.Fori(1, B // 2 - 2) as i:
                batch(2 * i, 0)
                expert(i - 1)
                batch(2 * i + 1, 1)
            for dst, w in ((sg_raw, sh_gate), (su_raw, sh_up), (sd, sh_down), (rw_raw, router_w)):
                weight(dst[:, :, :], w).then_inc(sh_in, 16)
            for b in range(B - 4, B):
                batch(b, b % 2)
            for e in range(B // 2 - 3, E):
                expert(e)
            sp.wait_ge(x2_ok, B)
            sp.wait_ge(zero_out, 16)
            with sp.Fori(0, E) as e:
                sp.dma_start(eg[:, bass.ds(e, 1), :, :],
                             gate_w[bass.ds(e, 1)].rearrange("e (k p) f -> p e k f", p=P)).then_inc(exp_in, 16)

            out_rows = resid_dram.rearrange("(b s) d -> s b d", s=S)
            for g in range(G):
                sp.wait_ge(y_ok, 2 * g + 2)
                sp.dma_start(out_rows[:, GB * g:GB * g + GB, :], xall[:, GB * g:GB * g + GB, :]).then_inc(resid_out, 16)

            def load_rows(t, p):
                need(sp, xst_done, t - 2)
                need(sp, who_ok, t - 2)
                sp.dma_start(xs[p][:, :], xs_dram[bass.ds(t * P, P), :]).then_inc(xs_in[p], 16)

            sp.wait_ge(scat, 16 * B)
            for p in range(SLOTS):
                load_rows(p, p)
            with sp.Fori(1, TILES // SLOTS) as i:
                for p in range(SLOTS):
                    load_rows(SLOTS * i + p, p)

        @block.tensor
        def _(pe):
            def tr(out_, in_, n):
                return nc.tensor.transpose(out_, in_, ident[0:n, 0:n])

            pe.wait_ge(ident_ok, 1)
            def turn_weight(n, out_bank):
                for k in range(KC):
                    for o in range(KC):
                        mm = tr(out_bank[:, k * D + o * P:k * D + (o + 1) * P], wraw[:, n, o, k * P:(k + 1) * P], P)
                mm.then_inc(wT_done, 1)

            pe.wait_ge(wk_in, 16)
            turn_weight(0, b0)

            def turn_ctx(b, p, i, k):
                if k == 0:
                    pe.wait_ge(cin_in[p], 32 * i + 32)
                need(pe, (v_a, v_v)[k], b - 1)
                for c, (k0, n) in enumerate(KEY_CHUNKS):
                    mm = tr((b4, b5)[k][:, k0:k0 + n], cin[p][0:n, c, k * P:(k + 1) * P], n)
                mm.then_inc(ct_done, 1)

            def project_k(b, p, o):
                pe.wait_ge(ct_hi, 2 * b + 2)
                pe.wait_ge(ct_lo, 2 * b + 2)
                need(pe, kr_ok, 2 * b - 2 + o + 1)
                for n, (w, c) in enumerate(ROUNDED_PAIRS):
                    for k in range(KC):
                        mm = nc.tensor.matmul((b4, b5)[o][:, 0:NK + 1], wkT[:, w, k, o * P:(o + 1) * P], ctxT[p][:, c, k, :],
                                              start=(n + k == 0), stop=(n + k == 3))
                mm.then_inc(kmm, 1)

            def project_v(b, p, chunks, keys):
                o = chunks[0] // 2
                need(pe, kr_ok, keys)
                for c in chunks:
                    k0, n = KEY_CHUNKS[c]
                    for j, (a, w) in enumerate(ROUNDED_PAIRS):
                        for k in range(KC):
                            mm = nc.tensor.matmul((b4, b5)[o][0:n, (c % 2) * D:(c % 2 + 1) * D],
                                                  ctxT[p][:, a, k, k0:k0 + n], wvT[:, w, k, :],
                                                  start=(j + k == 0), stop=(j + k == 3))
                mm.then_inc(vmm, 1)

            for k in range(KC):
                turn_ctx(0, 0, 0, k)
            pe.wait_ge(wv_in, 16)
            turn_weight(1, b1)
            pe.wait_ge(wlo_ok, 1)
            pe.wait_ge(pad_ok, 2)
            for o in range(2):
                project_k(0, 0, o)
            for k in range(KC):
                pe.wait_ge(kr_ok, 1 + k)
                turn_ctx(1, 1, 0, k)
            pe.wait_ge(w2_in, 32)
            turn_weight(2, b2)
            for o in range(2):
                project_k(1, 1, o)
            pe.wait_ge(wox_ok, 1)
            for g in range(4):
                for o in range(KC):
                    mm = tr((b3, b7)[g // 2][:, (g % 2) * D + o * P:(g % 2) * D + (o + 1) * P],
                            woX[:, o, g].rearrange("p j two d -> p (j two d)"), P)
            mm.then_inc(woT_done, 1)
            def turn_x(g):
                pe.wait_ge(xn_ok, GB * (g + 1))
                for k in range(KC):
                    need(pe, (xt_a, xt_v)[k], g)
                    for i in range(GB):
                        mm = tr((b6, b7)[k][:, i * S:(i + 1) * S], xn[:, i, k * P:(k + 1) * P], S)
                    mm.then_inc(xt_done, 1)

            def project_q(g, o):
                pe.wait_ge(xt_a, g + 1)
                pe.wait_ge(xt_v, g + 1)
                need(pe, qr_ok, 2 * g - 3 + o)
                for k in range(KC):
                    mm = nc.tensor.matmul((b0, b1, b2, b3)[2 * (g % 2) + o][:, 0:GT], wqT[:, k, o * P:(o + 1) * P],
                                          xnT[g % 2][:, k, :], start=(k == 0), stop=(k == KC - 1))
                mm.then_inc(qmm, 1)

            pe.wait_ge(wT_ok, 3)
            pe.wait_ge(wlo_ok, 2)
            pe.wait_ge(woT_ok, 2)
            turn_x(0)
            for g in range(G):
                if g + 1 < G:
                    turn_x(g + 1)
                for o in range(2):
                    project_q(g, o)

            def max_scores(b, p, heads):
                for h in heads:
                    if h % HH == 0:
                        pe.wait_ge(k_in[p][h // HH], 32 * (b - p) + 64)
                    need(pe, red, 16 * b + h - 1)
                    nc.tensor.matmul((b2, b3)[h % 2][0:S, 0:NK], qst[p][0:ROWS, h * S:(h + 1) * S],
                                     kst[p][0:ROWS, h * NK:(h + 1) * NK], start=True, stop=True).then_inc(smax, 1)

            def turn_max(b, p, hh):
                pe.wait_ge(mp_ok, 2 * b + hh + 1)
                need(pe, mt_ok, 2 * b + hh)
                need(pe, x2_ok, b - 2 + hh)
                for h in range(HH):
                    hd = hh * HH + h
                    mm = nc.tensor.transpose(b7.bitcast(BF16)[ROWS:STACK, h * S:(h + 1) * S], mparts[:, hd, :],
                                             identb[0:S, 0:S])
                mm.then_inc(mt_done, 1)

            def scores(b, p, hh, c):
                n = 6 * b + 3 * hh + c
                k0 = KEY_CHUNKS[c][0]
                if c == 0:
                    pe.wait_ge(mt_ok, 2 * b + hh + 1)
                need(pe, exp_ok, n)
                for h in range(HH):
                    hd = hh * HH + h
                    at = (h // 4) * 512 + (h % 4) * S
                    mm = nc.tensor.matmul(pair[:, at:at + S], kst[p][:, hd * NK + k0:hd * NK + k0 + P],
                                          qst[p][:, hd * S:(hd + 1) * S], start=True, stop=True)
                mm.then_inc(sc_done, 1)

            def values(b, p, hh):
                pe.wait_ge(exp_ok, 6 * b + 3 * hh + 3)
                if isinstance(b, int) and b == 0:
                    pe.wait_ge(turn_base, 1)
                if hh == 0:
                    pe.wait_ge(v_a, b + 1)
                    pe.wait_ge(v_v, b + 1)
                    need(pe, turned_ok, b)
                for g in range(2):
                    for c, (_, n) in enumerate(KEY_CHUNKS):
                        for j in range(4):
                            h = 4 * g + j
                            col = (2 * hh + g) * S
                            mm = nc.tensor.matmul(b6[32 * j:32 * j + VW, col:col + S], vst[p][0:n, c, hh * HH + h, :],
                                                  pT[hh][0:n, c, h * S:(h + 1) * S], start=(c == 0), stop=(c == 2))
                mm.then_inc(pv_done, 1)

            def output(b, turns):
                pe.wait_ge(att_ok, b + 1)
                pe.wait_ge(mt_ok, turns)
                for g in range(4):
                    mm = nc.tensor.matmul(b7[0:S, 0:D], att[:, g * S:(g + 1) * S], woT[:, g, :],
                                          start=(g == 0), stop=(g == 3))
                mm.then_inc(wo_done, 1)

            def batch(b, p, i, first=False):
                nxt = exists(b + 1)
                keys = 2 * b + 5 if exists(b + 2) else 2 * B - 1

                def maxima(*heads):
                    if nxt:
                        max_scores(b + 1, 1 - p, heads)

                scores(b, p, 0, 0)
                maxima(0, 1)
                turn_max(b, p, 1)
                if not first:
                    values(b - 1, 1 - p, 1)
                maxima(2, 3)
                if exists(b + 2):
                    project_k(b + 2, p, 0)

                scores(b, p, 0, 1)
                maxima(4, 5)
                if exists(b + 2):
                    project_k(b + 2, p, 1)

                scores(b, p, 0, 2)
                maxima(6, 7)
                if nxt:
                    project_v(b + 1, 1 - p, (0, 1), keys)

                scores(b, p, 1, 0)
                maxima(8, 9)
                if nxt:
                    turn_max(b + 1, 1 - p, 0)
                    project_v(b + 1, 1 - p, (2,), keys + 1)

                scores(b, p, 1, 1)
                maxima(10, 11)
                if not first:
                    output(b - 1, 2 * b + 3 if nxt else 2 * B)
                maxima(12, 13)
                if exists(b + 3):
                    turn_ctx(b + 3, 1 - p, i + 1 + p, 0)

                scores(b, p, 1, 2)
                maxima(14, 15)
                if exists(b + 3):
                    turn_ctx(b + 3, 1 - p, i + 1 + p, 1)
                values(b, p, 0)

            pe.wait_ge(ones_k, 4)
            project_v(0, 0, (0, 1), 3)
            pe.wait_ge(qr_ok, 2 * G)
            max_scores(0, 0, (0, 1, 2, 3))
            max_scores(0, 0, (4, 5, 6, 7))
            project_v(0, 0, (2,), 4)
            max_scores(0, 0, (8, 9, 10, 11))
            for k in range(KC):
                turn_ctx(2, 0, 1, k)
                max_scores(0, 0, (12 + 2 * k, 13 + 2 * k))
            turn_max(0, 0, 0)
            batch(0, 0, 0, first=True)
            batch(1, 1, 0)
            with pe.Fori(1, B // 2 - 2) as i:
                batch(2 * i, 0, i)
                batch(2 * i + 1, 1, i)
            for b in range(B - 4, B):
                batch(b, b % 2, b // 2)
            values(B - 1, 1, 1)

            def turn_xf(g):
                pe.wait_ge(xfb_ok, g + 1)
                need(pe, y_ok, 2 * g - 2)
                for k in range(KC):
                    need(pe, xft_lo, 2 * g - 1 + k)
                    for i in range(GB):
                        mm = tr((b0, b1)[k][:, i * S:(i + 1) * S], xf[g % 2][:, i, k * P:(k + 1) * P], S)
                    mm.then_inc(xft_done, 1)

            def router_logits(g):
                pe.wait_ge(xft_lo, 2 * g + 2)
                need(pe, rt, ROUTER_STEPS * (g - 1) + 1)
                for n, (w, c) in enumerate(ROUNDED_PAIRS):
                    for k in range(KC):
                        mm = nc.tensor.matmul(b2[0:E, 0:GT], rw[w][:, k, :], xfT[g % 2][:, c, k, :],
                                              start=(n + k == 0), stop=(n + k == 3))
                mm.then_inc(lgT_done, 1)

            def turn_logits(g):
                pe.wait_ge(lgT_ok, g + 1)
                for i in range(GB):
                    mm = tr(b2[0:S, GT + i * E:GT + (i + 1) * E], lgT[:, i * S:(i + 1) * S], E)
                mm.then_inc(lg_done, 1)

            def gate_up(g, f):
                n = FC * g + f
                for w, banks, free, done in ((sg, (b3, b5), silu_ok, g_done), (su, (b4, b6), h_ok, u_done)):
                    need(pe, free, n - 1)
                    for j, (a, c) in enumerate(ROUNDED_PAIRS):
                        for k in range(KC):
                            mm = nc.tensor.matmul(banks[f % 2][:, 0:GT], w[a][:, k, f * P:(f + 1) * P],
                                                  xfT[g % 2][:, c, k, :], start=(j + k == 0), stop=(j + k == 3))
                    mm.then_inc(done, 1)

            def down(g, j):
                need(pe, y_ok, 2 * g - 1 + j)
                if g == 0 and j == 0:
                    pe.wait_ge(x2_ok, B)
                for i in range(2):
                    for f in range(FC):
                        if j == 0 and i == 0:
                            pe.wait_ge(h_ok, FC * g + f + 1)
                        at = (2 * j + i) * S
                        mm = nc.tensor.matmul((b7, b0)[j][0:S, i * D:(i + 1) * D], hT[:, f, at:at + S], sd[:, f, :],
                                              start=(f == 0), stop=(f == FC - 1))
                mm.then_inc(dn_done, 1)

            def ranks():
                pe.wait_ge(rt, ROUTER_STEPS * G)
                nc.tensor.matmul(b2[0:S, 0:B * E], lower[:, :], hot[:, :, :].rearrange("p b e -> p (b e)"),
                                 start=True, stop=False)
                nc.tensor.matmul(b2[0:S, 0:B * E], ones[:, 0:S], before[:, 0:B, :].rearrange("p b e -> p (b e)"),
                                 start=False, stop=True)
                nc.tensor.matmul(b2[:, B * E:(B + 1) * E], ones[:, :], before[:, B, :], start=True, stop=True)\
                    .then_inc(rank_done, 1)

            def group(g, last=False):
                router_steps = {} if last else {g_lead(g) + n: step for n, step in
                                                enumerate((turn_xf, router_logits, turn_logits))}
                for f in range(FC):
                    gate_up(g, f)
                    if f in router_steps:
                        router_steps[f](g + 1)
                if g == G - 2:
                    ranks()
                down(g, 0)
                down(g, 1)

            pe.wait_ge(exp_ok, 6 * B)
            pe.wait_ge(red, H * B)
            turn_xf(0)
            pe.wait_ge(sh_in, 64)
            pe.wait_ge(sw_lo, 3)
            router_logits(0)
            output(B - 1, 2 * B)
            turn_logits(0)
            pe.wait_ge(turned_ok, B)
            pe.wait_ge(v_a, B)
            pe.wait_ge(v_v, B)
            pe.wait_ge(const_ok, 4)
            for g in range(G):
                group(g, last=(g == G - 1))

            TERMS = [(0, 0), (1, 0), (0, 1)]

            def turn_rows(t, p, i):
                pe.wait_ge(xs_in[p], 16 * i + 16)
                need(pe, xst_lo, t)
                for k in range(KC):
                    mm = tr(b0[:, k * P:(k + 1) * P], xs[p][:, k * P:(k + 1) * P], P)
                mm.then_inc(xst_done, 1)

            def gate(t, p):
                tg = (tg_round[p], tg_rest)
                pe.wait_ge(xst_hi, t + 1)
                pe.wait_ge(tg_hi, t + 1)
                need(pe, gact_ok, t)
                for n, (w, a) in enumerate(TERMS):
                    if n == 1:
                        pe.wait_ge(tg_lo, t + 1)
                    if n == 2:
                        pe.wait_ge(xst_lo, t + 1)
                    for k in range(KC):
                        mm = nc.tensor.matmul(b3, xsT[:, a, k * P:(k + 1) * P], tg[w][:, k * FF:(k + 1) * FF],
                                              start=(n + k == 0), stop=(n + k == 3))
                mm.then_inc(gt_done, 1)

            def up(t):
                pe.wait_ge(tu_hi, t + 1)
                need(pe, hrow_ok, t)
                for n, (a, w) in enumerate(TERMS):
                    if n == 2:
                        pe.wait_ge(tu_lo, t + 1)
                    for k in range(KC):
                        mm = nc.tensor.matmul(b4, xsT[:, a, k * P:(k + 1) * P], tu[:, w, k * FF:(k + 1) * FF],
                                              start=(n + k == 0), stop=(n + k == 3))
                mm.then_inc(ut_done, 1)

            def turn_hidden(t):
                pe.wait_ge(hrow_ok, t + 1)
                need(pe, hrt_lo, t)
                for f in range(FC):
                    mm = tr(b1[:, f * P:(f + 1) * P], hrow[:, f * P:(f + 1) * P], P)
                mm.then_inc(ht_done, 1)

            def tile_down(t):
                pe.wait_ge(hrt_hi, t + 1)
                pe.wait_ge(td_hi, t + 1)
                need(pe, orow_ok, t)
                last = isinstance(t, int) and t + 1 == TILES
                weights = td_last if last else (td[:, 0, :], td[:, 1, :])
                for n, (a, w) in enumerate(TERMS):
                    if n == 1:
                        pe.wait_ge(hrt_lo, t + 1)
                    if n == 2 and not last:
                        pe.wait_ge(td_lo, t + 1)
                    if n == 2 and last:
                        pe.wait_ge(td_lo_last, 1)
                    for f in range(FC):
                        mm = nc.tensor.matmul(b7[:, 0:D], hrT[:, a, f * P:(f + 1) * P], weights[w][:, f * D:(f + 1) * D],
                                              start=(n + f == 0), stop=(n + f == 2 + FC - 1))
                mm.then_inc(dt_done, 1)

            def tile(t, p, i):
                gate(t, p)
                turn_hidden(t - 1)
                up(t)
                if not (isinstance(t, int) and t + 1 == TILES):
                    turn_rows(t + 1, (p + 1) % SLOTS, i + (p + 1) // SLOTS)
                tile_down(t - 1)

            pe.wait_ge(y_ok, 2 * G)
            turn_rows(0, 0, 0)
            gate(0, 0)
            up(0)
            turn_rows(1, 1, 0)
            tile(1, 1, 0)
            tile(2, 2, 0)
            with pe.Fori(1, TILES // SLOTS - 1) as i:
                for p in range(SLOTS):
                    tile(SLOTS * i + p, p, i)
            for p in range(SLOTS):
                tile(TILES - SLOTS + p, p, TILES // SLOTS - 1)
            turn_hidden(TILES - 1)
            tile_down(TILES - 1)

        @block.scalar
        def _(act):
            def copy(o, i_, scale=1.0):
                return nc.scalar.activation(o, i_, ACT.Copy, scale=scale)

            def by_dim(w, src):
                return (w.rearrange("p k (o d e) -> p (k o) d e", o=2, d=HD),
                        src[:, 0:KC * D].rearrange("p (ko e d) -> p ko d e", e=HH, d=HD))

            def put_weight(n, w, src):
                act.wait_ge(wT_done, n + 1)
                for ko in range(4):
                    o_, i_ = by_dim(w, src)
                    mm = copy(o_[:, ko], i_[:, ko], scale=HD ** -0.5 if n == 2 else 1.0)
                mm.then_inc(wT_ok, 1)

            put_weight(0, wkT[:, 0], b0)

            def round_ctx(b, p, k):
                act.wait_ge(ct_done, 2 * b + k + 1)
                need(act, vmm, 2 * b - 2)
                copy(ctxT[p][:, 0, k, 0:NK], (b4, b5)[k][:, 0:NK]).then_inc(ct_hi, 1)

            def first_part(b, o):
                act.wait_ge(kmm, 2 * b + o + 1)
                need(act, k_out[o], 16 * b)
                copy(kp[:, o, 0, :], (b4, b5)[o][:, 0:NK]).then_inc(k1_ok, 1)

            def second_part(b, o):
                act.wait_ge(kr_ok, 2 * b + o + 1)
                copy(kp[:, o, 1, :], kr[:, o, :]).then_inc(k2_ok, 1)

            def put_values(b, p):
                act.wait_ge(vmm, 2 * b + 1)
                need(act, pv_done, 2 * b - 2)
                copy(vst[p][:, 0:2, :, 0:HD], b4.rearrange("p (c h d) -> p c h d", c=2, h=H)).then_inc(v_a, 1)

            for k in range(KC):
                round_ctx(0, 0, k)
            act.wait_ge(wT_done, 2)
            copy(wvT[:, 0].rearrange("p k d -> p (k d)"), b1).then_inc(wT_ok, 1)
            for o in range(2):
                first_part(0, o)
            for k in range(KC):
                round_ctx(1, 1, k)
            for o in range(2):
                second_part(0, o)
            put_weight(2, wqT[:, :, :], b2)
            for o in range(2):
                first_part(1, o)
            for o in range(2):
                second_part(1, o)
            act.wait_ge(small_in, 80)
            nc.scalar.activation(tanhs[:, :], gates[:, :], ACT.Tanh).then_inc(tanh_ok, 1)

            def put_x(g):
                act.wait_ge(xt_done, 2 * g + 1)
                need(act, qmm, 2 * g - 2)
                copy(xnT[g % 2][:, 0, :], b6[:, 0:GT]).then_inc(xt_a, 1)

            def q_first(g, o):
                act.wait_ge(qmm, 2 * g + o + 1)
                need(act, q_out[g % 2][o], 16 * PARTS * (g // 2))
                copy(qp[g % 2][o][:, 0, :], (b0, b1, b2, b3)[2 * (g % 2) + o][:, 0:GT]).then_inc(q1_ok, 1)

            def q_second(g, o):
                act.wait_ge(qr_ok, 2 * g + o + 1)
                copy(qp[g % 2][o][:, 1, :], qr[o][:, :]).then_inc(q2_ok, 1)

            put_x(0)
            put_x(1)
            for g in range(G):
                if 0 < g < G - 1:
                    put_x(g + 1)
                q_first(g, 0)
                q_first(g, 1)
                q_second(g, 0)
                q_second(g, 1)

            def exps(b, hh, c):
                n = KEY_CHUNKS[c][1]
                act.wait_ge(sc_done, 6 * b + 3 * hh + c + 1)
                if c == 0:
                    need(act, pv_done, 2 * b - 1 + hh)
                nc.scalar.activation(pT[hh][0:n, c, :].rearrange("p (a n) -> p a n", a=2),
                                     pair[0:n, :].rearrange("p (a n) -> p a n", a=2)[:, :, 0:4 * S],
                                     ACT.Exp).then_inc(exp_ok, 1)

            def put_max(b, p, hh):
                act.wait_ge(mt_done, 2 * b + hh + 1)
                need(act, sc_done, 6 * b - 12 + 3 * hh + 3)
                copy(qst[p][ROWS:STACK, hh * HQ:(hh + 1) * HQ], b7.bitcast(BF16)[ROWS:STACK, 0:HQ])\
                    .then_inc(mt_ok, 1)

            def batch(b, p):
                nxt = exists(b + 1)
                exps(b, 0, 0)
                put_max(b, p, 1)
                if exists(b + 2):
                    first_part(b + 2, 0)
                exps(b, 0, 1)
                if exists(b + 2):
                    second_part(b + 2, 0)
                    first_part(b + 2, 1)
                exps(b, 0, 2)
                if exists(b + 2):
                    second_part(b + 2, 1)
                if nxt:
                    put_values(b + 1, 1 - p)
                exps(b, 1, 0)
                if nxt:
                    put_max(b + 1, 1 - p, 0)
                exps(b, 1, 1)
                if exists(b + 3):
                    round_ctx(b + 3, 1 - p, 0)
                exps(b, 1, 2)
                if exists(b + 3):
                    round_ctx(b + 3, 1 - p, 1)

            put_values(0, 0)
            for k in range(KC):
                round_ctx(2, 0, k)
            put_max(0, 0, 0)
            act.wait_ge(q3_ok, 2 * G)
            for p in range(2):
                for o in range(2):
                    act.wait_ge(q_out[p][o], 16 * PARTS * G // 2)
            batch(0, 0)
            batch(1, 1)
            with act.Fori(1, B // 2 - 2) as i:
                batch(2 * i, 0)
                batch(2 * i + 1, 1)
            for b in range(B - 4, B):
                batch(b, b % 2)

            def round_xf(g):
                for k in range(KC):
                    act.wait_ge(xft_done, 2 * g + k + 1)
                    copy(xfT[g % 2][:, 0, k, :], (b0, b1)[k][:, 0:GT]).then_inc(xft_hi, 1)

            act.wait_ge(sh_in, 64)
            for hi, raw_ in ((sg_hi, sg_raw), (su_hi, su_raw), (rw_hi, rw_raw)):
                copy(hi[:, :, :], raw_[:, :, :]).then_inc(sw_hi, 1)

            def silu_chunk(g, f):
                n = FC * g + f
                act.wait_ge(g_done, n + 1)
                need(act, h_ok, n - 1)
                nc.scalar.activation(silu[f % 2][:, :], (b3, b5)[f % 2][:, 0:GT], ACT.Silu).then_inc(silu_ok, 1)

            def top_score(g):
                act.wait_ge(rt, ROUTER_STEPS * g + 2)
                need(act, xe_ok, GB * g)
                nc.scalar.activation(score[:, :], top[:, :], ACT.Tanh, scale=0.5).then_inc(tanh_top, 1)

            def group(g, last=False):
                for f in range(FC):
                    silu_chunk(g, f)
                    if f == g_lead(g) and not last:
                        round_xf(g + 1)
                if not last:
                    top_score(g + 1)

            round_xf(0)
            top_score(0)
            for g in range(G):
                group(g, last=(g == G - 1))

            def expert_of(t):
                return nc.scalar.value_load(texp_i[0:1, bass.ds(t, 1)], min_val=0, max_val=E - 1)

            def round_expert(e, whole, part, done):
                copy(part, whole[:, bass.ds(e, 1), :, :].rearrange("p a k f -> p (a k f)")).then_inc(done, 1)

            def round_gate(t, p, e):
                need(act, gt_done, t - 2)
                round_expert(e, eg, tg_round[p][:, :], tg_hi)

            def round_up(t, e):
                need(act, ut_done, t)
                round_expert(e, eu, tu[:, 0, :], tu_hi)

            def round_down(t, e):
                if isinstance(t, int) and t + 1 == TILES:
                    act.wait_ge(gt_done, TILES - 1)
                    round_expert(e, ed, td_last[0][:, :], td_hi)
                    return
                need(act, dt_done, t)
                round_expert(e, ed, td[:, 0, :], td_hi)

            def round_rows(t):
                act.wait_ge(xst_done, t + 1)
                copy(xsT[:, 0, :], b0[:, 0:D]).then_inc(xst_hi, 1)

            def gate_silu(t):
                act.wait_ge(gt_done, t + 1)
                need(act, hrow_ok, t)
                nc.scalar.activation(gact[:, :], b3, ACT.Silu).then_inc(gact_ok, 1)

            def round_hidden(t):
                act.wait_ge(ht_done, t + 1)
                copy(hrT[:, 0, :], b1).then_inc(hrt_hi, 1)

            act.wait_ge(rk, RANK_STEPS)
            act.wait_ge(exp_in, 16 * 3 * E)
            act.wait_ge(h_ok, FC * G)
            def tile(t, p):
                last = isinstance(t, int) and t + 1 == TILES
                further = isinstance(t, int) and t + 2 >= TILES
                first = isinstance(t, int) and t == 0
                if not first:
                    this = expert_of(t)
                if not last:
                    following = expert_of(t + 1)
                if not further:
                    second = expert_of(t + 2)
                if not first:
                    round_hidden(t - 1)
                gate_silu(t)
                if not last:
                    round_rows(t + 1)
                    round_up(t + 1, following)
                if not first:
                    round_down(t, this)
                if not further:
                    round_gate(t + 2, (p + 2) % SLOTS, second)

            e = expert_of(0)
            round_gate(0, 0, e)
            round_up(0, e)
            round_down(0, e)
            round_gate(1, 1, expert_of(1))
            round_rows(0)
            for p in range(SLOTS):
                tile(p, p)
            with act.Fori(1, TILES // SLOTS - 1) as i:
                for p in range(SLOTS):
                    tile(SLOTS * i + p, p)
            for p in range(SLOTS):
                tile(TILES - SLOTS + p, p)
            round_hidden(TILES - 1)

        @block.vector
        def _(ve):
            ve.wait_ge(ident_ok, 1)
            nc.vector.tensor_copy(identb[:, :], ident[:, :]).then_inc(identb_ok, 1)
            for p in range(2):
                nc.vector.memset(vst[p][:, :, :, :], 1.0).then_inc(ones_v, 1)
                nc.vector.memset(ctxT[p][:, :, :, NK:NK + 1].bitcast(F32), 0.0).then_inc(pad_ok, 1)
            def put_wo():
                ve.wait_ge(woT_done, 1)
                for n in range(2):
                    nc.vector.tensor_copy(woT[:, 2 * n:2 * n + 2, :].rearrange("p g d -> p (g d)"), (b3, b7)[n])\
                        .then_inc(woT_ok, 1)

            def spread_wo():
                ve.wait_ge(w2_in, 32)
                ve.wait_ge(fill_ok, 1)
                for o in range(KC):
                    last = nc.vector.tensor_copy(woX[:, o, :, :, 0, :],
                                                 wraw[:, 3, o, :].rearrange("p (g j d) -> p g j d", g=4, j=4))
                last.then_inc(wox_ok, 1)

            def rest_ctx(b, p):
                for k in range(KC):
                    ve.wait_ge(ct_hi, 2 * b + k + 1)
                    if k == 0:
                        need(ve, vmm, 2 * b - 2)
                    nc.vector.tensor_tensor(ctxT[p][:, 1, k, 0:NK], (b4, b5)[k][:, 0:NK], ctxT[p][:, 0, k, 0:NK],
                                            ALU.subtract).then_inc(ct_lo, 1)

            def by_dim(w, src):
                return (w.rearrange("p k (o d e) -> p (k o) d e", o=2, d=HD),
                        src[:, 0:KC * D].rearrange("p (ko e d) -> p ko d e", e=HH, d=HD))

            def rest_wk():
                ve.wait_ge(wT_ok, 1)
                hi, src = by_dim(wkT[:, 0], b0)
                lo, _ = by_dim(wkT[:, 1], b0)
                for ko in range(4):
                    last = nc.vector.tensor_tensor(lo[:, ko], src[:, ko], hi[:, ko], ALU.subtract)
                last.then_inc(wlo_ok, 1)

            def rest_wv():
                ve.wait_ge(wT_ok, 2)
                nc.vector.tensor_tensor(wvT[:, 1].rearrange("p k d -> p (k d)"), b1,
                                        wvT[:, 0].rearrange("p k d -> p (k d)"), ALU.subtract).then_inc(wlo_ok, 1)

            def rest(b, o):
                ve.wait_ge(k1_ok, 2 * b + o + 1)
                need(ve, k3_ok, 2 * b - 1 + o)
                nc.vector.tensor_tensor(kr[:, o, :], (b4, b5)[o][:, 0:NK], kp[:, o, 0, :], ALU.subtract).then_inc(kr_ok, 1)

            def put_values(b, p):
                ve.wait_ge(vmm, 2 * b + 2)
                need(ve, pv_done, 2 * b - 2)
                n = KEY_CHUNKS[2][1]
                nc.vector.tensor_copy(vst[p][0:n, 2, :, 0:HD], b5[0:n, 0:D].rearrange("p (h d) -> p h d", h=H)).then_inc(v_v, 1)

            def statistics(b):
                nc.vector.bn_stats(st[:, bass.ds(b, 1), :].rearrange("p a n -> p (a n)"),
                                   xall[:, bass.ds(b, 1), :].rearrange("p a n -> p (a n)")).then_inc(st_ok, 1)

            rest_wk()
            rest_ctx(0, 0)
            rest_wv()
            ve.wait_ge(x_in, 16)
            for b in range(4):
                statistics(b)
            for o in range(2):
                rest(0, o)
            for b in range(4, 8):
                statistics(b)
            rest_ctx(1, 1)
            for b in range(8, B):
                statistics(b)
            ve.wait_ge(st_ok, B)
            stats(ve, 0)
            spread_wo()

            def norm_x(g):
                need(ve, xt_done, 2 * g)
                for i in range(GB):
                    b = GB * g + i
                    nc.vector.tensor_scalar(xn[:, i, :], xall[:, b, :], mean[:, b:b + 1], rstd[:, b:b + 1],
                                            ALU.subtract, ALU.mult).then_inc(xn_ok, 1)

            def put_x(g):
                ve.wait_ge(xt_done, 2 * g + 2)
                need(ve, qmm, 2 * g - 2)
                nc.vector.tensor_copy(xnT[g % 2][:, 1, :], b7[:, 0:GT]).then_inc(xt_v, 1)

            def q_rest(g, o):
                ve.wait_ge(q1_ok, 2 * g + o + 1)
                need(ve, q3_ok, 2 * g - 1 + o)
                nc.vector.tensor_tensor(qr[o][:, :], (b0, b1, b2, b3)[2 * (g % 2) + o][:, 0:GT], qp[g % 2][o][:, 0, :],
                                        ALU.subtract).then_inc(qr_ok, 1)

            for o in range(2):
                rest(1, o)
            ve.wait_ge(rs_ok, 2)
            norm_x(0)
            put_wo()
            put_x(0)
            norm_x(1)
            for g in range(G):
                if g + 1 < G:
                    put_x(g + 1)
                if g + 2 < G:
                    norm_x(g + 2)
                for o in range(2):
                    q_rest(g, o)

            def maxima(b, heads):
                for h in heads:
                    ve.wait_ge(smax, 16 * b + h + 1)
                    if h % HH == 0:
                        need(ve, mp_ok, 2 * b - 1 + h // HH)
                    nc.vector.tensor_reduce(negmax[:, h:h + 1], (b2, b3)[h % 2][0:S, 0:NK], AX.X, ALU.max,
                                            negate=True).then_inc(red, 1)

            def split_max(b, hh):
                own = slice(hh * HH, (hh + 1) * HH)
                ve.wait_ge(red, 16 * b + (hh + 1) * HH)
                need(ve, mt_done, 2 * b + hh - 1)
                nc.vector.tensor_copy(mparts[:, own, 0], negmax[:, own]).then_inc(mp1, 1)
                ve.wait_ge(mp1, 2 * b + hh + 1)
                nc.vector.tensor_tensor(mparts[:, own, 1], negmax[:, own], mparts[:, own, 0], ALU.subtract)\
                    .then_inc(mp_ok, 1)

            def turn_out(b):
                ve.wait_ge(pv_done, 2 * b + 2)
                need(ve, scaled_ok, b)
                nc.vector.transpose(turned[:, :, :].rearrange("p a n -> p (a n)"), b6[:, 0:4 * S]).then_inc(turned_ok, 1)
                ve.wait_ge(turned_ok, b + 1)
                nc.vector.reciprocal(rec[:, :], turned[:, :, HD]).then_inc(rec_ok, 1)

            def turn_back(b):
                ve.wait_ge(scaled_ok, b + 1)
                need(ve, wo_done, b)
                nc.vector.transpose(att[:, :], scaled[:, :, :].rearrange("p a n -> p (a n)")).then_inc(att_ok, 1)

            def add_attention(b):
                ve.wait_ge(wo_done, b + 1)
                xb = xall[:, bass.ds(b, 1), :].rearrange("p a n -> p (a n)")
                nc.vector.scalar_tensor_tensor(out=xb, in0=b7[0:S, 0:D], scalar=tanhs[0:S, 0:1], in1=xb,
                                               op0=ALU.mult, op1=ALU.add).then_inc(x2_ok, 1)

            def statistics_of_output(b):
                ve.wait_ge(x2_ok, b + 1)
                statistics(b)

            def batch(b, p, first=False):
                nxt = exists(b + 1)
                if nxt:
                    maxima(b + 1, (0, 1))
                if not first:
                    turn_out(b - 1)
                if nxt:
                    maxima(b + 1, (2, 3))
                if exists(b + 2):
                    rest(b + 2, 0)
                if nxt:
                    maxima(b + 1, (4, 5))
                if not first:
                    turn_back(b - 1)
                if exists(b + 2):
                    rest(b + 2, 1)
                if nxt:
                    maxima(b + 1, (6, 7))
                    split_max(b + 1, 0)
                    maxima(b + 1, (8, 9))
                    put_values(b + 1, 1 - p)
                    maxima(b + 1, (10, 11))
                if not first:
                    add_attention(b - 1)
                if nxt:
                    maxima(b + 1, (12, 13, 14, 15))
                    split_max(b + 1, 1)
                if exists(b + 3):
                    rest_ctx(b + 3, 1 - p)
                if not first:
                    statistics_of_output(b - 1)

            nc.vector.memset(b6, 0.0).then_inc(turn_base, 1)
            ve.wait_ge(ones_v, 2)
            maxima(0, (0, 1, 2, 3))
            maxima(0, (4, 5, 6, 7))
            split_max(0, 0)
            put_values(0, 0)
            maxima(0, range(8, 14))
            rest_ctx(2, 0)
            maxima(0, (14, 15))
            split_max(0, 1)
            ve.wait_ge(xb_ok, 1)
            batch(0, 0, first=True)
            batch(1, 1)
            with ve.Fori(1, B // 2 - 2) as i:
                batch(2 * i, 0)
                batch(2 * i + 1, 1)
            def normalise(g):
                need(ve, base_ok, g)
                for i in range(GB):
                    b = GB * g + i
                    nc.vector.tensor_scalar(xn2[:, i, :], xall[:, b, :], mean[:, b:b + 1], rstd[:, b:b + 1],
                                            ALU.subtract, ALU.mult).then_inc(xn2_ok, 1)

            def normalise_again(g):
                need(ve, xft_done, 2 * g - 2)
                for i in range(GB):
                    ve.wait_ge(xn2_ok, GB * g + i + 1)
                    nc.vector.scalar_tensor_tensor(out=xf[g % 2][:, i, :], in0=xn2[:, i, :],
                                                   scalar=rstd2[:, GB * g + i:GB * g + i + 1],
                                                   in1=lnw[:, :], op0=ALU.mult, op1=ALU.mult).then_inc(xf_ok, 1)

            for b in range(B - 4, B):
                batch(b, b % 2)
                if b == B - GB + 1:
                    ve.wait_ge(st_ok, 2 * B - GB)
                    stats(ve, STATS_STEPS, slice(0, B - GB))
                if b == B - 2:
                    ve.wait_ge(rs_ok, 8)
                    ve.wait_ge(small_in, 80)
                    normalise(0)
                    normalise_again(0)
            for n, (lo, raw_, hi) in enumerate(((sg_lo, sg_raw, sg_hi), (su_lo, su_raw, su_hi), (rw_lo, rw_raw, rw_hi))):
                ve.wait_ge(sw_hi, n + 1)
                nc.vector.tensor_tensor(lo[:, :, :], raw_[:, :, :], hi[:, :, :], ALU.subtract).then_inc(sw_lo, 1)
            turn_out(B - 1)

            def rest_xf(g):
                for k in range(KC):
                    ve.wait_ge(xft_hi, 2 * g + k + 1)
                    nc.vector.tensor_tensor(xfT[g % 2][:, 1, k, :], (b0, b1)[k][:, 0:GT], xfT[g % 2][:, 0, k, :],
                                            ALU.subtract).then_inc(xft_lo, 1)

            def put_logits(g):
                ve.wait_ge(lgT_done, g + 1)
                nc.vector.tensor_copy(lgT[:, :], b2[0:E, 0:GT]).then_inc(lgT_ok, 1)

            def router(g):
                n = ROUTER_STEPS * g
                ve.wait_ge(lg_done, g + 1)
                nc.vector.tensor_copy(lg[:, :, :].rearrange("p b e -> p (b e)"), b2[0:S, GT:GT + GB * E]).then_inc(rt, 1)
                ve.wait_ge(rt, n + 1)
                nc.vector.tensor_reduce(top[:, :], lg[:, :, :], AX.X, ALU.max).then_inc(rt, 1)
                ve.wait_ge(rt, n + 2)
                nc.vector.tensor_tensor(eq[:, :, :], lg[:, :, :], top[:, :, None].broadcast_to([S, GB, E]), ALU.is_equal)\
                    .then_inc(rt, 1)
                ve.wait_ge(rt, n + 3)
                nc.vector.scalar_tensor_tensor(out=eq[:, :, :], in0=eq[:, :, :], scalar=-float(E),
                                               in1=iota_e[:, None, :].broadcast_to([S, GB, E]),
                                               op0=ALU.mult, op1=ALU.add).then_inc(rt, 1)
                ve.wait_ge(rt, n + 4)
                nc.vector.tensor_reduce(pick[:, :], eq[:, :, :], AX.X, ALU.min).then_inc(rt, 1)
                ve.wait_ge(rt, n + 5)
                nc.vector.scalar_tensor_tensor(out=hot[:, bass.ds(GB * g, GB), :],
                                               in0=iota_e[:, None, :].broadcast_to([S, GB, E]), scalar=-float(E),
                                               in1=pick[:, :, None].broadcast_to([S, GB, E]),
                                               op0=ALU.add, op1=ALU.is_equal).then_inc(rt, 1)
                for i in range(GB):
                    ve.wait_ge(rt, n + 6 + i)
                    b = GB * g + i
                    nc.vector.tensor_tensor(before[:, bass.ds(b + 1, 1), :], before[:, bass.ds(b, 1), :],
                                            hot[:, bass.ds(b, 1), :], ALU.add).then_inc(rt, 1)

            def rows_to_route(g):
                ve.wait_ge(tanh_top, g + 1)
                nc.vector.tensor_scalar(score[:, :], score[:, :], 0.5, 0.5, ALU.mult, ALU.add).then_inc(score_ok, 1)
                ve.wait_ge(score_ok, g + 1)
                ve.wait_ge(xfb_ok, g + 1)
                for i in range(GB):
                    nc.vector.tensor_scalar(xe[:, bass.ds(GB * g + i, 1), 0:D].rearrange("p a n -> p (a n)"), xf[g % 2][:, i, :],
                                            score[:, i:i + 1], None, ALU.mult).then_inc(xe_ok, 1)

            def hidden(g, f):
                n = FC * g + f
                ve.wait_ge(silu_ok, n + 1)
                ve.wait_ge(u_done, n + 1)
                if f == 0:
                    need(ve, dn_done, 2 * g)
                nc.vector.tensor_tensor(hT[:, f, :], silu[f % 2][:, :], (b4, b6)[f % 2][:, 0:GT], ALU.mult).then_inc(h_ok, 1)

            def add_shared(g, j):
                ve.wait_ge(dn_done, 2 * g + j + 1)
                if j == 0:
                    ve.wait_ge(base_ok, g + 1)
                xb = xall[:, GB * g + 2 * j:GB * g + 2 * j + 2, :]
                nc.vector.scalar_tensor_tensor(out=xb, in0=(b7, b0)[j][0:S, :].rearrange("p (a n) -> p a n", a=2),
                                               scalar=tanhs[0:S, 1:2], in1=xb, op0=ALU.mult, op1=ALU.add).then_inc(y_ok, 1)

            def tiles_and_places():
                ve.wait_ge(rank_done, 1)
                nc.vector.tensor_copy(tot[:, :], b2[:, B * E:(B + 1) * E]).then_inc(rk, 1)
                ve.wait_ge(rk, 1)
                by_expert = passed[:, :].rearrange("p (e t) -> p e t", e=E)
                nc.vector.tensor_tensor(by_expert, tot[:, :, None].broadcast_to([P, E, TILES]),
                                        start_t[:, None, :].broadcast_to([P, E, TILES]), ALU.is_gt).then_inc(rk, 1)
                ve.wait_ge(rk, 2)
                nc.vector.tensor_reduce(ntile[:, :], by_expert, AX.X, ALU.add).then_inc(rk, 1)
                ve.wait_ge(rk, 3)
                nc.vector.tensor_copy(upto[:, 0:1], ntile[:, 0:1]).then_inc(rk, 1)
                for e in range(1, E):
                    ve.wait_ge(rk, 3 + e)
                    nc.vector.tensor_tensor(upto[:, e:e + 1], upto[:, e - 1:e], ntile[:, e:e + 1], ALU.add).then_inc(rk, 1)
                ve.wait_ge(rk, 11)
                nc.vector.tensor_tensor(first_row[:, :], upto[:, :], ntile[:, :], ALU.subtract).then_inc(rk, 1)
                by_tile = passed[:, :].rearrange("p (t e) -> p t e", e=E)
                nc.vector.tensor_tensor(by_tile, iota_t[:, :, None].broadcast_to([P, TILES, E]),
                                        upto[:, None, :].broadcast_to([P, TILES, E]), ALU.is_ge).then_inc(rk, 1)
                ve.wait_ge(rk, 12)
                nc.vector.scalar_tensor_tensor(out=rank[:, :, :], in0=first_row[0:S, None, :].broadcast_to([S, B, E]),
                                               scalar=float(P), in1=b2[0:S, 0:B * E].rearrange("p (b e) -> p b e", e=E),
                                               op0=ALU.mult, op1=ALU.add).then_inc(rk, 1)
                ve.wait_ge(rk, 14)
                nc.vector.tensor_tensor(rank[:, :, :], rank[:, :, :], hot[:, :, :], ALU.mult).then_inc(rk, 1)
                nc.vector.tensor_reduce(texp[:, :], by_tile, AX.X, ALU.add).then_inc(rk, 1)
                ve.wait_ge(rk, 16)
                nc.vector.tensor_reduce(pos[:, :], rank[:, :, :], AX.X, ALU.add).then_inc(rk, 1)
                nc.vector.tensor_scalar(texp_i[:, :], texp[:, :], float(E - 1), None, ALU.min).then_inc(rk, 1)
                ve.wait_ge(rk, 17)
                nc.vector.tensor_copy(pos_i[:, :], pos[:, :]).then_inc(rk, 1)

            rest_xf(0)
            turn_back(B - 1)
            normalise(1)
            put_logits(0)
            normalise_again(1)
            add_attention(B - 1)
            statistics_of_output(B - 1)
            nc.vector.memset(before[:, 0, :], 0.0).then_inc(s2_init, 1)
            ve.wait_ge(const_ok, 4)
            ve.wait_ge(s2_init, 1)
            router(0)
            rows_to_route(0)
            for g in range(G):
                for f in range(FC):
                    if g + 2 == G and f == FC - 1:
                        router(g + 1)
                    hidden(g, f)
                    if g + 1 < G and f == g_lead(g):
                        rest_xf(g + 1)
                    if g + 1 < G and f == g_lead(g) + 1:
                        put_logits(g + 1)
                        if g == G - 3:
                            ve.wait_ge(rs_ok, 14)
                            normalise(g + 2)
                if g + 2 < G:
                    router(g + 1)
                    rows_to_route(g + 1)
                if g == 0:
                    ve.wait_ge(st_ok, 2 * B)
                    stats(ve, 2 * STATS_STEPS, slice(B - GB, B))
                if g + 2 == G:
                    tiles_and_places()
                    rows_to_route(g + 1)
                add_shared(g, 0)
                if g + 3 < G:
                    normalise(g + 2)
                if g + 2 < G:
                    normalise_again(g + 2)
                add_shared(g, 1)

            def expert_of(t):
                return nc.vector.value_load(texp_i[0:1, bass.ds(t, 1)], min_val=0, max_val=E - 1)

            def rest_expert(e, whole, rounded, rest, done):
                nc.vector.tensor_tensor(rest, whole[:, bass.ds(e, 1), :, :].rearrange("p a k f -> p (a k f)"),
                                        rounded, ALU.subtract).then_inc(done, 1)

            def rest_gate(t, p, e):
                ve.wait_ge(tg_hi, t + 1)
                need(ve, gt_done, t)
                rest_expert(e, eg, tg_round[p][:, :], tg_rest[:, :], tg_lo)

            def rest_up(t, e):
                ve.wait_ge(tu_hi, t + 1)
                rest_expert(e, eu, tu[:, 0, :], tu[:, 1, :], tu_lo)

            def rest_rows(t):
                ve.wait_ge(xst_hi, t + 1)
                nc.vector.tensor_tensor(xsT[:, 1, :], b0[:, 0:D], xsT[:, 0, :], ALU.subtract).then_inc(xst_lo, 1)

            def hidden_rows(t):
                ve.wait_ge(gact_ok, t + 1)
                ve.wait_ge(ut_done, t + 1)
                need(ve, ht_done, t)
                nc.vector.tensor_tensor(hrow[:, :], gact[:, :], b4, ALU.mult).then_inc(hrow_ok, 1)

            def take_who(t, p, i):
                ve.wait_ge(xs_in[p], 16 * i + 16)
                need(ve, out_done[p], 16 * i)
                nc.vector.tensor_copy(who[p][:, :], xs[p][:, D:XROW].bitcast(U32)).then_inc(who_ok, 1)

            def rest_hidden(t):
                ve.wait_ge(hrt_hi, t + 1)
                nc.vector.tensor_tensor(hrT[:, 1, :], b1, hrT[:, 0, :], ALU.subtract).then_inc(hrt_lo, 1)

            def finish_rows(t, p, i):
                ve.wait_ge(dt_done, t + 1)
                ve.wait_ge(resid_in[p], 16 * i + 16)
                nc.vector.scalar_tensor_tensor(out=resid[p][:, :], in0=b7[:, 0:D], scalar=tanhs[:, 1:2], in1=resid[p][:, :],
                                               op0=ALU.mult, op1=ALU.add).then_inc(orow_ok, 1)

            def tile(t, p, i):
                following = None
                if not (isinstance(t, int) and t + 1 == TILES):
                    following = expert_of(t + 1)
                rest_hidden(t - 1)
                take_who(t, (p + 1) % SLOTS, i + (p + 1) // SLOTS)
                if following is not None:
                    rest_gate(t + 1, (p + 2) % SLOTS, following)
                    rest_rows(t + 1)
                hidden_rows(t)
                if following is not None:
                    rest_up(t + 1, following)
                else:
                    ve.wait_ge(td_hi, TILES)
                    rest_expert(e, ed, td_last[0][:, :], td_last[1][:, :], td_lo_last)
                finish_rows(t - 1, p, i)

            e = expert_of(0)
            rest_gate(0, 0, e)
            rest_up(0, e)
            take_who(0, 0, 0)
            rest_rows(0)
            e = expert_of(1)
            rest_gate(1, 1, e)
            hidden_rows(0)
            rest_rows(1)
            rest_up(1, e)
            for p in range(SLOTS):
                tile(1 + p, p, 0)
            with ve.Fori(1, TILES // SLOTS - 1) as i:
                for p in range(SLOTS):
                    tile(SLOTS * i + p + 1, p, i)
            e = expert_of(TILES - 1)
            for p in range(SLOTS - 1):
                tile(TILES - SLOTS + p + 1, p, TILES // SLOTS - 1)
            rest_hidden(TILES - 1)
            finish_rows(TILES - 1, SLOTS - 1, TILES // SLOTS - 1)

        @block.gpsimd
        def _(pool):
            nc.gpsimd.memset(ident[:, :], 0.0).then_inc(ident_z, 1)
            pool.wait_ge(ident_z, 1)
            nc.gpsimd.affine_select(out=ident[:, :], in_=ident[:, :], compare_op=ALU.not_equal, fill=1.0, base=0,
                                    pattern=[[-1, P]], channel_multiplier=1).then_inc(ident_ok, 1)
            nc.gpsimd.memset(woX[:, :, :, :, :, :], 0.0).then_inc(fill_ok, 1)
            nc.gpsimd.memset(zrow[:, 0:D], 0.0).then_inc(fill_ok, 1)
            nc.gpsimd.memset(zrow[:, D:XROW].bitcast(I32), NOBODY).then_inc(fill_ok, 1)
            nc.gpsimd.memset(mhalf[:, :], -0.5).then_inc(fill_ok, 1)
            nc.gpsimd.memset(ones[:, :], 1.0).then_inc(fill_ok, 1)
            pool.wait_ge(fill_ok, 5)
            nc.gpsimd.affine_select(out=lower[:, :], in_=ones[:, 0:S], compare_op=ALU.is_gt, fill=0.0, base=0,
                                    pattern=[[1, S]], channel_multiplier=-1).then_inc(const_ok, 1)
            for dst, first, step, n in ((iota_e, E, 1, E), (iota_t, 0, 1, TILES), (start_t, 0, P, TILES)):
                nc.gpsimd.iota(dst[:, :], pattern=[[step, n]], base=first, channel_multiplier=0,
                               allow_small_or_imprecise_dtypes=True).then_inc(const_ok, 1)

            pool.wait_ge(const_ok, 4)
            for p in range(2):
                need(pool, ones_k, 2 * p)
                nc.gpsimd.memset(kst[p][ROWS:STACK, :], 1.0).then_inc(ones_k, 1)
                nc.gpsimd.memset(kst[p][0:ROWS, H * NK:H * NK + 16], 0.0).then_inc(ones_k, 1)
            pool.wait_ge(ones_k, 4)

            def third_part(b, o):
                pool.wait_ge(k2_ok, 2 * b + o + 1)
                nc.gpsimd.tensor_tensor(kp[:, o, 2, :], kr[:, o, :], kp[:, o, 1, :], ALU.subtract).then_inc(k3_ok, 1)

            for o in range(2):
                third_part(0, o)
            pool.wait_ge(lnv, STATS_STEPS)
            pool.wait_ge(fill_ok, 4)
            nc.gpsimd.tensor_scalar(tmp[:, :], var[:, :], EPS, 1.0, ALU.add, ALU.mult).then_inc(rs_ok, 1)
            pool.wait_ge(rs_ok, 1)
            nc.gpsimd.tensor_tensor(rstd[:, :], tmp[:, :], mhalf[:, :], ALU.pow).then_inc(rs_ok, 1)
            for o in range(2):
                third_part(1, o)

            for g in range(G):
                for o in range(2):
                    pool.wait_ge(q2_ok, 2 * g + o + 1)
                    nc.gpsimd.tensor_tensor(qp[g % 2][o][:, 2, :], qr[o][:, :], qp[g % 2][o][:, 1, :], ALU.subtract)\
                        .then_inc(q3_ok, 1)

            pool.wait_ge(ones_k, 4)
            pool.wait_ge(tanh_ok, 1)
            nc.gpsimd.tensor_scalar(bo_b[:, :], bo_b[:, :], tanhs[0:S, 0:1], 0.0, ALU.mult, ALU.add).then_inc(tb_ok, 1)
            pool.wait_ge(tb_ok, 1)
            pool.wait_ge(xn_ok, B)
            nc.gpsimd.tensor_tensor(xall[:, :, :], xall[:, :, :], bo_b[:, None, :].broadcast_to([S, B, D]),
                                    ALU.add).then_inc(xb_ok, 1)

            def rsqrt(first, cols):
                def step(n, out_, a, b_, op):
                    pool.wait_ge(rs_ok, n)
                    nc.gpsimd.tensor_tensor(out_[:, cols], a[:, cols], b_[:, cols], op).then_inc(rs_ok, 1)

                def plus_eps(src):
                    nc.gpsimd.tensor_scalar(tmp[:, cols], src[:, cols], EPS, 1.0, ALU.add, ALU.mult).then_inc(rs_ok, 1)

                pool.wait_ge(lnv, STATS_STEPS * (2 + (first - 2) // 6))
                plus_eps(var)
                step(first + 1, rstd, tmp, mhalf, ALU.pow)
                step(first + 2, tmp, var, rstd, ALU.mult)
                step(first + 3, tmp, tmp, rstd, ALU.mult)
                pool.wait_ge(rs_ok, first + 4)
                plus_eps(tmp)
                step(first + 5, rstd2, tmp, mhalf, ALU.pow)

            def shift(g):
                pool.wait_ge(xf_ok, GB * g + GB)
                nc.gpsimd.tensor_tensor(xf[g % 2][:, :, :], xf[g % 2][:, :, :], lnb[:, None, :].broadcast_to([S, GB, D]), ALU.add)\
                    .then_inc(xfb_ok, 1)

            def base(g):
                nc.gpsimd.tensor_scalar(xn2[:, :, :], xn2[:, :, :], tanhs[0:S, 1:2], 0.0, ALU.mult, ALU.add)\
                    .then_inc(xn2_scaled, 1)
                pool.wait_ge(xn2_scaled, g + 1)
                xg = xall[:, GB * g:GB * g + GB, :]
                nc.gpsimd.tensor_tensor(xg, xg, xn2[:, :, :], ALU.add).then_inc(base_ok, 1)

            def scale_out(b):
                pool.wait_ge(rec_ok, b + 1)
                need(pool, att_ok, b)
                nc.gpsimd.tensor_tensor(scaled[:, :, :], turned[:, :, :], rec[:, :, None].broadcast_to([P, NB, 32]),
                                        ALU.mult).then_inc(scaled_ok, 1)

            def batch(b):
                scale_out(b - 1)
                if exists(b + 2):
                    third_part(b + 2, 0)
                    third_part(b + 2, 1)

            for o in range(2):
                third_part(2, o)
            batch(1)
            with pool.Fori(2, B - 2) as b:
                batch(b)
            batch(B - 2)
            rsqrt(2, slice(0, B - GB))
            shift(0)
            batch(B - 1)
            base(0)
            scale_out(B - 1)
            shift(1)

            base(1)
            rsqrt(8, slice(B - GB, B))
            nc.gpsimd.iota(xe[:, :, D].bitcast(I32), pattern=[[S, B]], base=0, channel_multiplier=1).then_inc(s2_fill, 1)
            for p in range(SLOTS):
                nc.gpsimd.memset(resid[p][:, :], 0.0).then_inc(s2_fill, 1)
            for g in range(2, G):
                shift(g)
                base(g)

            pool.wait_ge(rk, RANK_STEPS)
            pool.wait_ge(s2_fill, 1 + SLOTS)
            for b in range(B):
                pool.wait_ge(xe_ok, b + 1)
                nc.gpsimd.indirect_dma_start(out=xs_dram[:, :], out_offset=bass.IndirectOffsetOnAxis(ap=pos_i[:, b:b + 1], axis=0),
                                             in_=xe[:, b, :], in_offset=None).then_inc(scat, 16)

            def fetch(t):
                p = t % SLOTS
                pool.wait_ge(who_ok, t + 1)
                nc.gpsimd.indirect_dma_start(out=resid[p][:, :], out_offset=None, in_=resid_dram[:, :],
                                             in_offset=bass.IndirectOffsetOnAxis(ap=who[p][:, 0:1], axis=0),
                                             bounds_check=T - 1, oob_is_err=False).then_inc(resid_in[p], 16)

            def expert_of(t):
                return nc.gpsimd.value_load(texp_i[0:1, t:t + 1], min_val=0, max_val=E - 1)

            def rest_down(t, e):
                pool.wait_ge(td_hi, t + 1)
                nc.gpsimd.tensor_tensor(td[:, 1, :], ed[:, bass.ds(e, 1), :, :].rearrange("p a k f -> p (a k f)"),
                                        td[:, 0, :], ALU.subtract).then_inc(td_lo, 1)

            def store(t):
                p = t % SLOTS
                pool.wait_ge(orow_ok, t + 1)
                nc.gpsimd.indirect_dma_start(out=out.rearrange("b s d -> (b s) d"),
                                             out_offset=bass.IndirectOffsetOnAxis(ap=who[p][:, 0:1], axis=0),
                                             in_=resid[p][:, :], in_offset=None,
                                             bounds_check=T - 1, oob_is_err=False).then_inc(out_done[p], 16)

            pool.wait_ge(dn_done, 2 * G)
            rest_down(0, expert_of(0))
            pool.wait_ge(resid_out, 16 * G)
            fetch(0)
            for t in range(TILES):
                if 0 < t < TILES - 1:
                    rest_down(t, e)
                if t + 2 < TILES:
                    e = expert_of(t + 1)
                if t + 1 < TILES:
                    fetch(t + 1)
                if t > 0:
                    store(t - 1)
            store(TILES - 1)
            for p in range(SLOTS):
                pool.wait_ge(out_done[p], 16 * TILES // SLOTS)



_OUTS = [((B, S, D), "float32")]


def kernel(**inputs):
    import numpy as _np
    import concourse.bacc as _bacc
    from concourse.bass_utils import run_bass_kernel_spmd as _run

    nc = _bacc.Bacc("TRN2", target_bir_lowering=False, num_devices=1)
    names = ["x", "ctx_1024", "g_xattn", "g_ffn", "L0_xattn_Wq", "L0_xattn_Wk", "L0_xattn_Wv", "L0_xattn_Wo",
             "L0_xattn_bo", "L0_ffn_ln_w", "L0_ffn_ln_b", "L0_ffn_router_w", "L0_ffn_gate_w", "L0_ffn_up_w",
             "L0_ffn_down_w", "L0_ffn_sh_gate", "L0_ffn_sh_up", "L0_ffn_sh_down"]
    arrays, args = {}, []
    for name in names:
        a = _np.ascontiguousarray(inputs[name])
        arrays[f"in_{name}"] = a
        args.append(nc.dram_tensor(f"in_{name}", a.shape, mybir.dt.from_np(a.dtype), kind="ExternalInput").ap())
    shape, dtype = _OUTS[0]
    args.append(nc.dram_tensor("out_0", shape, mybir.dt.from_np(_np.dtype(dtype)), kind="ExternalOutput").ap())
    build(nc, *args)
    r = _run(nc, [arrays], core_ids=[0])
    return r.results[0]["out_0"]
```
